# Optimizing a Trainium2 kernel written in Bass

```python
import numpy as np
import jax
import jax.numpy as jnp

def _softmax(x, axis=-1):
    return jax.nn.softmax(x, axis=axis)

def _gelu(x):
    return jax.nn.gelu(x, approximate=True)

def _silu(x):
    return jax.nn.silu(x)

def _sigmoid(x):
    return jax.nn.sigmoid(x)

def _layernorm(x, axis=-1, eps=1e-05):
    m = jnp.mean(x, axis=axis, keepdims=True)
    v = jnp.var(x, axis=axis, keepdims=True)
    return (x - m) / jnp.sqrt(v + eps)

def _scatter_add(tgt, idx, src, axis=0):
    return tgt.at[idx].add(src)

def _segment_sum(src, seg, n):
    return jax.ops.segment_sum(src, seg, n)
kernel_name = 'mk_xattn_ffn_d2_seqx_r8_d925c9'

def setup_inputs(seed: int=0):
    np.random.seed(seed)
    _w = jnp.asarray

    def _rec_inputs():
        import jax
        import jax.numpy as jnp
        _rk = jax.random.key(seed)
        x = -0.0001033 + 0.9999 * jax.random.normal(jax.random.fold_in(_rk, 1), (4, 512, 128), jnp.float32)
        _lenS = 512 - jax.random.randint(jax.random.fold_in(_rk, 7), (4,), 0, max(1, 512 // 4) + 1, jnp.int32)
        _lenS2 = 77 - jax.random.randint(jax.random.fold_in(_rk, 8), (4,), 0, max(1, 77 // 4) + 1, jnp.int32)
        _ctx_1024P = jax.random.normal(jax.random.fold_in(_rk, 11), (4, 16, 128), jnp.float32)
        _ctx_1024c = jax.random.dirichlet(jax.random.fold_in(_rk, 511), 0.3 * jnp.ones((16,), jnp.float32), (4, 77))
        _ctx_1024t = jnp.einsum('bsk,bkd->bsd', _ctx_1024c, _ctx_1024P)
        _ctx_1024t = _ctx_1024t * jax.lax.rsqrt(jnp.mean(jnp.square(_ctx_1024t)) + 1e-12) * 0.953939
        ctx_1024 = -0.000292821 + 1.00034 * (_ctx_1024t + 0.3 * jax.random.normal(jax.random.fold_in(_rk, 611), (4, 77, 128), jnp.float32))
        return (x, ctx_1024)
    x, ctx_1024 = _rec_inputs()

    def _L0_xattn_setup():
        import jax, jax.numpy as jnp
        import numpy as np
        from jax import lax
        B, T, F = (32, 128, 128)
        CONV_UNITS = 256
        SHORT_UNITS = 256
        RATE = 4
        key = jax.random.key(seed)
        k1, k2, k3 = jax.random.split(key, 3)
        inputs = jax.random.normal(k1, (B, T, F), dtype=jnp.float32)
        memory = jax.random.normal(k2, (B, CONV_UNITS + SHORT_UNITS, F), dtype=jnp.float32)
        conv_w = jax.random.normal(k3, (RATE, F, F), dtype=jnp.float32) * 0.02
        conv_b = jnp.zeros((F,), dtype=jnp.float32)
        return {'inputs': inputs, 'memory': memory, 'conv_w': conv_w, 'conv_b': conv_b, 'conv_units': CONV_UNITS, 'short_units': SHORT_UNITS, 'rate': RATE}
    _L0_xattn_all = _L0_xattn_setup()
    _L0_xattn_in = {k: v for k, v in _L0_xattn_all.items() if k in ('conv_w', 'conv_b')}
    del _L0_xattn_all

    def _L0_ffn_setup():
        import jax, jax.numpy as jnp
        import numpy as np
        E = 8
        K = 2
        key = jax.random.key(seed)
        ks = jax.random.split(key, 8)
        B, T, d = (4, 256, 128)
        h = 4 * d // E
        s = 0.02
        X = jax.random.normal(ks[0], (B, T, d), jnp.float32)
        routing_W = jax.random.normal(ks[1], (E, d), jnp.float32) * s
        expert_bias = jnp.zeros((E,), jnp.float32)
        sW1 = jax.random.normal(ks[2], (d, h), jnp.float32) * s
        sb1 = jnp.zeros((h,), jnp.float32)
        sW2 = jax.random.normal(ks[3], (h, d), jnp.float32) * s
        sb2 = jnp.zeros((d,), jnp.float32)
        rW1 = jax.random.normal(ks[4], (E, d, h), jnp.float32) * s
        rb1 = jnp.zeros((E, h), jnp.float32)
        rW2 = jax.random.normal(ks[5], (E, h, d), jnp.float32) * s
        rb2 = jnp.zeros((E, d), jnp.float32)
        return dict(X=X, routing_W=routing_W, expert_bias=expert_bias, sW1=sW1, sb1=sb1, sW2=sW2, sb2=sb2, rW1=rW1, rb1=rb1, rW2=rW2, rb2=rb2)
    _L0_ffn_all = _L0_ffn_setup()
    _L0_ffn_in = {k: v for k, v in _L0_ffn_all.items() if k in ('routing_W', 'expert_bias', 'sW1', 'sb1', 'sW2', 'sb2', 'rW1', 'rb1', 'rW2', 'rb2')}
    del _L0_ffn_all

    def _L1_xattn_setup():
        import jax, jax.numpy as jnp
        import numpy as np
        EMBED = 128
        HEADS = 16
        HEAD_DIM = EMBED // HEADS
        key = jax.random.key(seed)
        ks = jax.random.split(key, 11)
        B, S = (2, 256)
        scale = 1.0 / np.sqrt(EMBED)
        inp = {'Q': jax.random.normal(ks[0], (B, S, EMBED), jnp.float32), 'K': jax.random.normal(ks[1], (B, S, EMBED), jnp.float32), 'V': jax.random.normal(ks[2], (B, S, EMBED), jnp.float32), 'Wq': jax.random.normal(ks[3], (EMBED, EMBED), jnp.float32) * scale, 'bq': jnp.zeros((EMBED,), jnp.float32), 'Wk': jax.random.normal(ks[4], (EMBED, EMBED), jnp.float32) * scale, 'bk': jnp.zeros((EMBED,), jnp.float32), 'Wv': jax.random.normal(ks[5], (EMBED, EMBED), jnp.float32) * scale, 'bv': jnp.zeros((EMBED,), jnp.float32), 'Wo': jax.random.normal(ks[6], (EMBED, EMBED), jnp.float32) * scale, 'bo': jnp.zeros((EMBED,), jnp.float32)}
        return inp
    _L1_xattn_all = _L1_xattn_setup()
    _L1_xattn_in = {k: v for k, v in _L1_xattn_all.items() if k in ('Wq', 'bq', 'Wk', 'bk', 'Wv', 'bv', 'Wo', 'bo')}
    del _L1_xattn_all

    def _L1_ffn_setup():
        import jax, jax.numpy as jnp
        import numpy as np
        D_MODEL = 128
        EXPANSION = 4
        D_HIDDEN = D_MODEL * EXPANSION
        NUM_STAGES = int(np.log2(D_HIDDEN))

        def butterfly(y, weights, dim):
            lead = y.shape[:-1]
            for stage in range(weights.shape[0]):
                s = 2 ** stage
                nb = dim // (2 * s)
                yr = y.reshape(*lead, nb, 2, s)
                a = yr[..., 0, :]
                b = yr[..., 1, :]
                w = weights[stage].reshape(nb, s, 2, 2)
                na = w[..., 0, 0] * a + w[..., 0, 1] * b
                nb2 = w[..., 1, 0] * a + w[..., 1, 1] * b
                y = jnp.stack([na, nb2], axis=-2).reshape(*lead, dim)
            return y
        key = jax.random.key(seed)
        ks = jax.random.split(key, 6)
        B, S = (4, 256)
        x = jax.random.normal(ks[0], (B, S, D_MODEL), jnp.float32)
        W_exp = jax.random.normal(ks[1], (D_MODEL, D_HIDDEN), jnp.float32) * 0.02
        b_exp = jnp.zeros((D_HIDDEN,), jnp.float32)
        up_weights = jax.random.normal(ks[2], (NUM_STAGES, D_HIDDEN // 2, 2, 2), jnp.float32) * 0.02
        up_bias = jnp.zeros((D_HIDDEN,), jnp.float32)
        down_weights = jax.random.normal(ks[3], (NUM_STAGES, D_HIDDEN // 2, 2, 2), jnp.float32) * 0.02
        W_con = jax.random.normal(ks[4], (D_HIDDEN, D_MODEL), jnp.float32) * 0.02
        b_con = jnp.zeros((D_MODEL,), jnp.float32)
        down_bias = jnp.zeros((D_MODEL,), jnp.float32)
        return dict(x=x, W_exp=W_exp, b_exp=b_exp, up_weights=up_weights, up_bias=up_bias, down_weights=down_weights, W_con=W_con, b_con=b_con, down_bias=down_bias)
    _L1_ffn_all = _L1_ffn_setup()
    _L1_ffn_in = {k: v for k, v in _L1_ffn_all.items() if k in ('W_exp', 'b_exp', 'up_weights', 'up_bias', 'down_weights', 'W_con', 'b_con', 'down_bias')}
    del _L1_ffn_all
    return {'x': x, 'ctx_1024': ctx_1024, 'L0_xattn_conv_w': _L0_xattn_in['conv_w'], 'L0_xattn_conv_b': _L0_xattn_in['conv_b'], 'L0_ffn_routing_W': _L0_ffn_in['routing_W'], 'L0_ffn_expert_bias': _L0_ffn_in['expert_bias'], 'L0_ffn_sW1': _L0_ffn_in['sW1'], 'L0_ffn_sb1': _L0_ffn_in['sb1'], 'L0_ffn_sW2': _L0_ffn_in['sW2'], 'L0_ffn_sb2': _L0_ffn_in['sb2'], 'L0_ffn_rW1': _L0_ffn_in['rW1'], 'L0_ffn_rb1': _L0_ffn_in['rb1'], 'L0_ffn_rW2': _L0_ffn_in['rW2'], 'L0_ffn_rb2': _L0_ffn_in['rb2'], 'L1_xattn_Wq': _L1_xattn_in['Wq'], 'L1_xattn_bq': _L1_xattn_in['bq'], 'L1_xattn_Wk': _L1_xattn_in['Wk'], 'L1_xattn_bk': _L1_xattn_in['bk'], 'L1_xattn_Wv': _L1_xattn_in['Wv'], 'L1_xattn_bv': _L1_xattn_in['bv'], 'L1_xattn_Wo': _L1_xattn_in['Wo'], 'L1_xattn_bo': _L1_xattn_in['bo'], 'L1_ffn_W_exp': _L1_ffn_in['W_exp'], 'L1_ffn_b_exp': _L1_ffn_in['b_exp'], 'L1_ffn_up_weights': _L1_ffn_in['up_weights'], 'L1_ffn_up_bias': _L1_ffn_in['up_bias'], 'L1_ffn_down_weights': _L1_ffn_in['down_weights'], 'L1_ffn_W_con': _L1_ffn_in['W_con'], 'L1_ffn_b_con': _L1_ffn_in['b_con'], 'L1_ffn_down_bias': _L1_ffn_in['down_bias']}

def reference(x, ctx_1024, L0_xattn_conv_w, L0_xattn_conv_b, L0_ffn_routing_W, L0_ffn_expert_bias, L0_ffn_sW1, L0_ffn_sb1, L0_ffn_sW2, L0_ffn_sb2, L0_ffn_rW1, L0_ffn_rb1, L0_ffn_rW2, L0_ffn_rb2, L1_xattn_Wq, L1_xattn_bq, L1_xattn_Wk, L1_xattn_bk, L1_xattn_Wv, L1_xattn_bv, L1_xattn_Wo, L1_xattn_bo, L1_ffn_W_exp, L1_ffn_b_exp, L1_ffn_up_weights, L1_ffn_up_bias, L1_ffn_down_weights, L1_ffn_W_con, L1_ffn_b_con, L1_ffn_down_bias):
    import jax
    import jax.numpy as jnp

    def _L0_xattn_ref(inputs, memory, conv_w, conv_b, conv_units, short_units, rate):
        import jax, jax.numpy as jnp
        import numpy as np
        from jax import lax
        B, T, F = (32, 128, 128)
        CONV_UNITS = 256
        SHORT_UNITS = 256
        RATE = 4
        b, t, f = inputs.shape
        conv_mem = memory[:, :conv_units]
        short_mem = memory[:, -short_units:]
        old_memory = short_mem[:, :t]
        compression = lax.conv_general_dilated(old_memory, conv_w, window_strides=(rate,), padding='VALID', dimension_numbers=('NWC', 'WIO', 'NWC')) + conv_b
        tc = compression.shape[1]
        new_short = jnp.concatenate([short_mem[:, t:], inputs], axis=1)
        new_conv = jnp.concatenate([conv_mem[:, tc:], compression], axis=1)
        return jnp.concatenate([new_conv, new_short], axis=1)

    def _L0_ffn_ref(X, routing_W, expert_bias, sW1, sb1, sW2, sb2, rW1, rb1, rW2, rb2):
        import jax, jax.numpy as jnp
        import numpy as np
        E = 8
        K = 2
        B, T, d = X.shape
        shared = jax.nn.silu(X @ sW1 + sb1) @ sW2 + sb2
        logits = jnp.einsum('btd,ed->bte', X, routing_W) + expert_bias
        activation = jnp.sqrt(jax.nn.softplus(logits))
        top_vals, top_idx = jax.lax.top_k(activation, K)
        combine = jnp.sum(jax.nn.one_hot(top_idx, E, dtype=X.dtype) * top_vals[..., None], axis=-2)
        Xf = X.reshape(-1, d)
        cf = combine.reshape(-1, E)
        hdn = jax.nn.silu(jnp.einsum('nd,edh->enh', Xf, rW1) + rb1[:, None, :])
        y = jnp.einsum('enh,ehd->end', hdn, rW2) + rb2[:, None, :]
        routed = jnp.einsum('ne,end->nd', cf, y).reshape(B, T, d)
        return shared + routed

    def _L1_xattn_ref(Q, K, V, Wq, bq, Wk, bk, Wv, bv, Wo, bo):
        import jax, jax.numpy as jnp
        import numpy as np
        EMBED = 128
        HEADS = 16
        HEAD_DIM = EMBED // HEADS
        B, Sq, _ = Q.shape
        Sk = K.shape[1]
        q = Q @ Wq + bq
        k = K @ Wk + bk
        v = V @ Wv + bv
        q = q.reshape(B, Sq, HEADS, HEAD_DIM).transpose(0, 2, 1, 3)
        k = k.reshape(B, Sk, HEADS, HEAD_DIM).transpose(0, 2, 1, 3)
        v = v.reshape(B, Sk, HEADS, HEAD_DIM).transpose(0, 2, 1, 3)
        scores = jnp.einsum('bhqd,bhkd->bhqk', q, k) / jnp.sqrt(jnp.float32(HEAD_DIM))
        attn = jax.nn.softmax(scores, axis=-1)
        out = jnp.einsum('bhqk,bhkd->bhqd', attn, v)
        out = out.transpose(0, 2, 1, 3).reshape(B, Sq, EMBED)
        return out @ Wo + bo

    def _L1_ffn_ref(x, W_exp, b_exp, up_weights, up_bias, down_weights, W_con, b_con, down_bias):
        import jax, jax.numpy as jnp
        import numpy as np
        D_MODEL = 128
        EXPANSION = 4
        D_HIDDEN = D_MODEL * EXPANSION
        NUM_STAGES = int(np.log2(D_HIDDEN))

        def butterfly(y, weights, dim):
            lead = y.shape[:-1]
            for stage in range(weights.shape[0]):
                s = 2 ** stage
                nb = dim // (2 * s)
                yr = y.reshape(*lead, nb, 2, s)
                a = yr[..., 0, :]
                b = yr[..., 1, :]
                w = weights[stage].reshape(nb, s, 2, 2)
                na = w[..., 0, 0] * a + w[..., 0, 1] * b
                nb2 = w[..., 1, 0] * a + w[..., 1, 1] * b
                y = jnp.stack([na, nb2], axis=-2).reshape(*lead, dim)
            return y
        h = jnp.einsum('bsd,dh->bsh', x, W_exp) + b_exp
        h = butterfly(h, up_weights, D_HIDDEN)
        h = jax.nn.gelu(h + up_bias, approximate=False)
        h = butterfly(h, down_weights, D_HIDDEN)
        y = jnp.einsum('bsh,hd->bsd', h, W_con) + b_con
        return y + down_bias
    x = x + _L0_xattn_ref(ctx_1024, _layernorm(x, axis=-1), L0_xattn_conv_w, L0_xattn_conv_b, 256, 256, 4)
    x = x + _L0_ffn_ref(_layernorm(x, axis=-1), L0_ffn_routing_W, L0_ffn_expert_bias, L0_ffn_sW1, L0_ffn_sb1, L0_ffn_sW2, L0_ffn_sb2, L0_ffn_rW1, L0_ffn_rb1, L0_ffn_rW2, L0_ffn_rb2)
    x = x + _L1_xattn_ref(_layernorm(x, axis=-1), ctx_1024, ctx_1024, L1_xattn_Wq, L1_xattn_bq, L1_xattn_Wk, L1_xattn_bk, L1_xattn_Wv, L1_xattn_bv, L1_xattn_Wo, L1_xattn_bo)
    x = x + _L1_ffn_ref(_layernorm(x, axis=-1), L1_ffn_W_exp, L1_ffn_b_exp, L1_ffn_up_weights, L1_ffn_up_bias, L1_ffn_down_weights, L1_ffn_W_con, L1_ffn_b_con, L1_ffn_down_bias)
    return x

_drawn_inputs = setup_inputs


def setup_inputs(seed=0):
    import zlib

    import numpy as np

    out = dict(_drawn_inputs(seed))
    spreads = {'L0_xattn_conv_b': (0.0, 0.515),
     'L0_ffn_expert_bias': (0.0, 0.1),
     'L0_ffn_sb1': (0.0, 0.8),
     'L0_ffn_sb2': (0.0, 0.1),
     'L0_ffn_rb1': (0.0, 0.8),
     'L0_ffn_rb2': (0.0, 0.1),
     'L1_xattn_bq': (0.0, 0.498),
     'L1_xattn_bk': (0.0, 0.8),
     'L1_xattn_bv': (0.0, 0.1),
     'L1_xattn_bo': (0.0, 0.1),
     'L1_ffn_b_exp': (0.0, 0.1),
     'L1_ffn_up_bias': (0.0, 0.1),
     'L1_ffn_b_con': (0.0, 0.1),
     'L1_ffn_down_bias': (0.0, 0.1)}
    factors = {'L0_ffn_sW1': 4.588, 'L0_ffn_sW2': 4.213, 'L0_ffn_rW1': 3.427, 'L0_ffn_rW2': 3.126}
    for name, (base, spread) in spreads.items():
        noise = np.random.default_rng([zlib.crc32(name.encode()), seed]).standard_normal(out[name].shape)
        drawn = base * np.exp(spread * noise) if base else spread * noise
        out[name] = jnp.asarray(drawn.astype(out[name].dtype))
    for name, factor in factors.items():
        out[name] = (out[name] * factor).astype(out[name].dtype)
    return out
```

```python
from contextlib import ExitStack

import concourse.bass as bass
from concourse import mybir

F32 = mybir.dt.float32
F32R = mybir.dt.float32r
BF16 = mybir.dt.bfloat16
ALU = mybir.AluOpType
ACT = mybir.ActivationFunctionType
AX = mybir.AxisListType

P = 128
EPS = 1e-5


def two_layer_block(nc, inp, out):
    x, ctx_in = inp["x"], inp["ctx_1024"]
    B, S, D = x.shape
    C = ctx_in.shape[1]
    NT = S // P
    RATE = inp["L0_xattn_conv_w"].shape[0]
    HALF = S // 2
    TC = (C - RATE) // RATE + 1
    E, HE = inp["L0_ffn_rb1"].shape
    NJ = E * HE // P
    HID = inp["L1_ffn_W_exp"].shape[1]
    NH = HID // P
    HEADS = 16
    HD = D // HEADS
    NG = D // 32
    HG = HEADS // NG
    SCALE = float(HD) ** -0.5
    NB = 3
    CUT1 = HALF - TC - P
    CUT3 = S - C - 3 * P
    CW = 96

    ctx = ExitStack()
    with ctx:
        def sb(name, shape, dt=F32):
            return ctx.enter_context(nc.sbuf_tensor(name, shape, dt))

        def sem(name):
            return ctx.enter_context(nc.semaphore(name))

        X = sb("X", [P, B, NT, D])
        XS = sb("XS", [P, B, NT, D])
        xc = sb("xc", [B * TC, RATE, D])
        xcn = sb("xcn", [B * TC, RATE, D])
        cpad = sb("cpad", [P, B, RATE, P])
        convw = sb("convw", [P, RATE, D])
        comp = sb("comp", [P, B, D])
        convb = sb("convb", [1, D])
        convm = sb("convm", [1, P])
        nrm = sb("nrm", [P, 2, NT, D])
        nT = sb("nT", [P, 2, S])
        stat = sb("stat", [P, NT, 6])
        mv = sb("mv", [P, NT, 2])
        ve = sb("ve", [P, NT])
        rstd = sb("rstd", [P, NT])
        mean0 = sb("mean0", [P, NT])
        keep = sb("keep", [P, NT])
        raw = sb("raw", [P, NT])
        mhalf = sb("mhalf", [P, NT])
        phalf = sb("phalf", [P, NT * E])
        ident = sb("ident", [P, P])
        identb = sb("identb", [P, P], BF16)
        rows = sb("rows", [32, P])
        cols = sb("cols", [P, 32])
        w1 = sb("w1", [P, E * HE + HE])
        w2 = sb("w2", [P, NJ + 1, D])
        ebias = sb("ebias", [P, E])
        tri = sb("tri", [P, E, E])
        lg = sb("lg", [P, NT, E])
        nlg = sb("nlg", [P, NT, E])
        el = sb("el", [P, NT, E])
        sp = sb("sp", [P, NT, E])
        rt = sb("rt", [P, NT, E])
        act = sb("act", [P, NT, E])
        beats = sb("beats", [P, NT, E, E])
        ties = sb("ties", [P, NT, E, E])
        rank = sb("rank", [P, NT, E])
        cnat = sb("cnat", [P, NT, CW])
        res = sb("res", [P, 2, NT, E])
        c24 = sb("c24", [P, NT, NB, E], BF16)
        cT24 = sb("cT24", [NB * E, S], BF16)
        sel8 = sb("sel8", [NB * E, E])
        sel = sb("sel", [NB * E, E, HE], BF16)
        sil = sb("sil", [P, NJ, S])
        g = sb("g", [P, 2, NJ + 1, S])
        wq = sb("wq", [P, D])
        wk = sb("wk", [P, D])
        wv = sb("wv", [P, D])
        wo = sb("wo", [P, D])
        bvb = sb("bvb", [P, D])
        bob = sb("bob", [P, D])
        bfin = sb("bfin", [P, D])
        bfin2 = sb("bfin2", [P, D])
        cx = sb("cx", [C, B, D])
        cxT = sb("cxT", [P, B * C])
        kf = sb("kf", [P, B * C])
        kh = sb("kh", [P, B * C], F32R)
        kl = sb("kl", [P, B * C], F32R)
        KR = sb("KR", [96, NG, B * C], F32R)
        hm = sb("hm", [96, HG])
        ones_p = sb("ones_p", [P, HG, C])
        KS = sb("KS", [P, NG, B, HG, C], F32R)
        VA = sb("VA", [C, B, HEADS, 32])
        qf = sb("qf", [P, S])
        qh = sb("qh", [P, 2, S], F32R)
        ql = sb("ql", [P, 2, S], F32R)
        QS = sb("QS", [P, 2, NG, S], F32R)
        nm = sb("nm", [P, NT, HEADS])
        mx = sb("mx", [P, NT, NG, 32], F32R)
        mT = sb("mT", [P, 2, S], F32R)
        pe_ = sil[0:C, :, :].rearrange("p (u i) q -> p u i q", u=2)
        US = sb("US", [P, 2, NG, S])
        rec = sb("rec", [P, 2, HEADS])
        an = sb("an", [P, NT, D])
        aT = sb("aT", [P, 2, S])
        wexp = sb("wexp", [P, HID])
        BW = sb("BW", [P, 3, 3, 4, 2, 2])
        M = sb("M", [P, 2, 3, 8, 8])
        pa = sb("pa", [P, 2, 3, 32])
        pb = sb("pb", [P, 2, 3, 32])
        Mo = sb("Mo", [P, 3, 8, 8])
        MR = sb("MR", [P, 2, 3, NH, 8])
        mk0 = sb("mk0", [P, 16])
        mk1 = sb("mk1", [P, 2, 8])
        mk2 = sb("mk2", [P, 64])
        G0 = sb("G0", [P, 2, NH, P])
        G1 = sb("G1", [P, 2, NH, P])
        G2 = US[:, :, :, :].rearrange("p u t (v k) -> p u t v k", k=P)
        U = sb("U", [P, 2, NH, D + 2])
        V = sb("V", [P, 2, NH, D])
        wup = sb("wup", [P, HID])
        bup = sb("bup", [P, NH])
        ge = g

        bank = [ctx.enter_context(nc.psum_tensor(f"bank{i}", [P, S], F32)) for i in range(8)]
        mdram = nc.dram_tensor("mdram", (2, 3, HID, 8), F32, kind="Internal").ap()

        names = """ld_xc ld_conv ld_rows ld_w1 ld_w2 ld_bc ld_cx ld_wa ld_wexp ld_wcon ld_bw z_ready ident_z ident_ready
        masks_ready rows_z cols_ps cols_ready pool_step dve_step act_step
        conv_ve conv_rstd conv_nrm conv_tp conv_T conv_ps ve_ready rstd_ready s0_ve s0_ready
        x1_done ln_nrm tp_ps nT_ready logits_ps lg_ready e_ready ln_ready sp_ready a_ready beats_ready
        comb_ready combT_ps combT_ready hid_ps silu_done gate_ps gated y_ps x2_done
        cxT_ps cxT_ready k_ps kf_ready kh_done k_split KR_ready KS_ready KS_ones v_ps VA_ready VA_z
        q_ps qf_ready q_split QS_ready a_ps max_done mx_ready mx_z mT_ps mT_ready max_in
        s_ps exp_done us_ready ut_ps an_ready anT_ps aT_ready o_ps x3_done bo_added bfin_sum bfin_added
        M_ready M_stored MR_ready G_ready wexpT_ps u_ps u_ready v2_ps v2_ready wup_ps wup_ready bup_ready
        hid1_ps gelu_done y1_ps x4_done stored
        zero_ready pv_pair x1_conv compared""".split()
        s = {n: sem(n) for n in names}
        ld_x = [sem(f"ld_x{b}") for b in range(B)]
        ld_xs = [sem(f"ld_xs{b}") for b in range(B)]
        ld_QS = [sem(f"ld_QS{u}") for u in range(2)]
        ld_MX = [sem(f"ld_MX{u}") for u in range(2)]

        block = ctx.enter_context(nc.Block())
        R_RB1, R_SB1, R_BQ, R_BK, R_BE, R_UB, R_RW = 0, 4, 5, 6, 7, 11, 15
        NR = R_RW + E

        @block.sync
        def _(sp_):
            dma = sp_.dma_start
            for b in range(B):
                dma(xc[TC * b:TC * b + TC, :, :],
                    x[b, HALF:HALF + TC * RATE, :].rearrange("(j r) d -> j r d", r=RATE)).then_inc(s["ld_xc"], 16)

            def load_rows(b):
                dma(XS[:, b, 0:2, :], x[b, TC:TC + 2 * P, :].rearrange("(t p) d -> p t d", p=P)).then_inc(ld_xs[b], 16)
                dma(XS[:, b, 2, :], x[b, HALF + C:HALF + C + P, :]).then_inc(ld_xs[b], 16)
                dma(XS[0:CUT3, b, 3, :], x[b, HALF + C + P:S, :]).then_inc(ld_xs[b], 16)
                dma(XS[CUT3:P, b, 3, :], ctx_in[b, :, :]).then_inc(ld_xs[b], 16)
                dma(X[:, b, :, :], x[b].rearrange("(t p) d -> p t d", p=P)).then_inc(ld_x[b], 16)

            load_rows(0)
            dma(convw[:, :, :], inp["L0_xattn_conv_w"].rearrange("r i o -> i r o")).then_inc(s["ld_conv"], 16)
            dma(convb[:, :], inp["L0_xattn_conv_b"].rearrange("(a d) -> a d", a=1)).then_inc(s["ld_conv"], 16)
            sp_.wait_ge(s["rows_z"], 1)
            for r, src in ((R_RB1, inp["L0_ffn_rb1"].rearrange("(j e) h -> j (e h)", j=NJ)),
                           (R_BQ, inp["L1_xattn_bq"].rearrange("(a d) -> a d", a=1)),
                           (R_BK, inp["L1_xattn_bk"].rearrange("(a d) -> a d", a=1)),
                           (R_BE, inp["L1_ffn_b_exp"].rearrange("(a d) -> a d", d=P)),
                           (R_UB, inp["L1_ffn_up_bias"].rearrange("(a d) -> a d", d=P)),
                           (R_RW, inp["L0_ffn_routing_W"])):
                dma(rows[r:r + src.shape[0], :], src).then_inc(s["ld_rows"], 16)
            dma(rows[R_SB1:R_SB1 + 1, 0:HE], inp["L0_ffn_sb1"].rearrange("(a d) -> a d", a=1)).then_inc(s["ld_rows"], 16)
            dma(ebias[:, :], inp["L0_ffn_expert_bias"].rearrange("(a d) -> a d", a=1).broadcast_to((P, E))).then_inc(s["ld_rows"], 16)
            dma(w1[:, 0:E * HE].rearrange("p (e h) -> p e h", e=E), inp["L0_ffn_rW1"].rearrange("e d h -> d e h")).then_inc(s["ld_w1"], 16)
            dma(w1[:, E * HE:], inp["L0_ffn_sW1"]).then_inc(s["ld_w1"], 16)
            load_rows(1)
            dma(w2[:, 0:NJ, :], inp["L0_ffn_rW2"].rearrange("e h d -> (e h) d").rearrange("(j p) d -> p j d", p=P)).then_inc(s["ld_w2"], 16)
            dma(w2[0:HE, NJ, :], inp["L0_ffn_sW2"]).then_inc(s["ld_w2"], 16)
            dma(w2[HE:HE + E, NJ, :], inp["L0_ffn_rb2"]).then_inc(s["ld_w2"], 16)
            dma(w2[HE + E:HE + E + 1, NJ, :], inp["L0_ffn_sb2"].rearrange("(a d) -> a d", a=1)).then_inc(s["ld_w2"], 16)
            load_rows(2)
            load_rows(3)
            dma(cx[:, :, :], ctx_in.rearrange("b c d -> c b d")).then_inc(s["ld_cx"], 16)
            for t, n in ((wq, "Wq"), (wk, "Wk"), (wv, "Wv"), (wo, "Wo")):
                dma(t[:, :], inp["L1_xattn_" + n]).then_inc(s["ld_wa"], 16)
            for t, n in ((bvb, "L1_xattn_bv"), (bob, "L1_xattn_bo"), (bfin, "L1_ffn_b_con"), (bfin2, "L1_ffn_down_bias")):
                dma(t[:, :], inp[n].rearrange("(a d) -> a d", a=1).broadcast_to((P, D))).then_inc(s["ld_bc"], 16)
            for ud, n in ((0, "L1_ffn_up_weights"), (1, "L1_ffn_down_weights")):
                W, q = inp[n], 64 * ud
                for m in range(3):
                    dma(BW[q:q + 64, 0, m, :, :, :].rearrange("g k r c -> g (k r c)"),
                        W[m].rearrange("(g k) r c -> g (k r c)", k=4)).then_inc(s["ld_bw"], 16)
                    for a in range(8):
                        dma(BW[q + 8 * a:q + 8 * a + 8, 1, m, :, :, :].rearrange("g k r c -> g k (r c)"),
                            W[3 + m, 32 * a:32 * a + 32].rearrange("(k g) r c -> g k (r c)", k=4)).then_inc(s["ld_bw"], 16)
                    dma(BW[q:q + 64, 2, m, :, :, :].rearrange("g k r c -> g k (r c)"),
                        W[6 + m].rearrange("(k g) r c -> g k (r c)", k=4)).then_inc(s["ld_bw"], 16)
            dma(wexp[:, :], inp["L1_ffn_W_exp"]).then_inc(s["ld_wexp"], 16)
            dma(V[:, 0, :, :], inp["L1_ffn_W_con"].rearrange("(t p) d -> p t d", p=P)).then_inc(s["ld_wcon"], 16)
            sp_.wait_ge(s["k_split"], 1)
            for gq in range(NG):
                r = slice(32 * gq, 32 * gq + 32)
                for at, src in ((0, kh), (32, kl), (64, kh)):
                    dma(KR[at:at + 32, gq, :].bitcast(F32), src[r, :].bitcast(F32)).then_inc(s["KR_ready"], 16)
            sp_.wait_ge(s["M_ready"], 1)
            for ud in range(2):
                q = 64 * ud
                dma(mdram[ud, 0].rearrange("(g i) j -> g (i j)", i=8),
                    Mo[q:q + 64, 0, :, :].rearrange("g i j -> g (i j)")).then_inc(s["M_stored"], 16)
                for a in range(8):
                    dma(mdram[ud, 1, 64 * a:64 * a + 64].rearrange("(i g) j -> g i j", i=8),
                        Mo[q + 8 * a:q + 8 * a + 8, 1, :, :]).then_inc(s["M_stored"], 16)
                dma(mdram[ud, 2].rearrange("(i g) j -> g i j", i=8), Mo[q:q + 64, 2, :, :]).then_inc(s["M_stored"], 16)
            sp_.wait_ge(s["M_stored"], 16 * 20)
            for ud in range(2):
                for d in range(3):
                    dma(MR[:, ud, d, :, :], mdram[ud, d].rearrange("(t p) j -> p t j", p=P)).then_inc(s["MR_ready"], 16)

            def stack_q(b):
                u = b % 2
                sp_.wait_ge(s["q_split"], b + 1)
                if b >= 2:
                    sp_.wait_ge(s["pv_pair"], 2 * NG * (b - 1))
                for gq in range(NG):
                    r = slice(32 * gq, 32 * gq + 32)
                    for at, src in ((0, qh), (32, qh), (64, ql)):
                        dma(QS[at:at + 32, u, gq, :].bitcast(F32), src[r, u, :].bitcast(F32)).then_inc(ld_QS[u], 16)

            def stack_max(b):
                u = b % 2
                sp_.wait_ge(s["mT_ready"], b + 1)
                for gq in range(NG):
                    dma(QS[96:128, u, gq, :].bitcast(F32), mT[32 * gq:32 * gq + 32, u, :].bitcast(F32)).then_inc(ld_MX[u], 16)

            for b in range(B):
                stack_q(b)
                stack_max(b)
            for b in range(B):
                sp_.wait_ge(s["x4_done"], b + 1)
                dma(out[b].rearrange("(t p) d -> p t d", p=P), X[:, b, :, :]).then_inc(s["stored"], 16)
            sp_.wait_ge(s["stored"], 16 * B)

        @block.gpsimd
        def _(pool):
            n = [0]

            def step(ins):
                n[0] += 1
                ins.then_inc(s["pool_step"], 1)
                pool.wait_ge(s["pool_step"], n[0])

            gp = nc.gpsimd
            gp.memset(rows[:, :], 0.0).then_inc(s["rows_z"], 1)
            step(gp.memset(ident[:, :], 0.0))
            gp.affine_select(out=ident[:, :], in_=ident[:, :], compare_op=ALU.not_equal, fill=1.0, base=0,
                             pattern=[[-1, P]], channel_multiplier=1).then_inc(s["ident_ready"], 1)
            gp.memset(mhalf[:, :], -0.5)
            gp.memset(phalf[:, :], 0.5)
            gp.memset(raw[:, :], 0.0)
            step(gp.memset(keep[:, :], 1.0))
            gp.memset(keep[:, 1:2], 0.0)
            gp.memset(keep[:, 3:4], 0.0)
            step(gp.memset(raw[:, 3:4], 1.0))
            gp.memset(keep[0:CUT1, 1:2], 1.0)
            gp.memset(keep[0:CUT3, 3:4], 1.0)
            gp.memset(raw[0:CUT3, 3:4], 0.0)
            step(gp.memset(convm[:, :], 0.0))
            gp.memset(convm[:, CUT1:P], 1.0)
            gp.memset(cpad[:, :, :, :], 0.0).then_inc(s["z_ready"], 1)

            pool.wait_ge(s["conv_ve"], 1)
            gp.tensor_tensor(rstd[0:B * TC, :], ve[0:B * TC, :], mhalf[0:B * TC, :], ALU.pow).then_inc(s["conv_rstd"], 1)

            def rstd_of(k):
                pool.wait_ge(s["ve_ready"], k + 1)
                gp.tensor_tensor(rstd[:, :], ve[:, :], mhalf[:, :], ALU.pow).then_inc(s["rstd_ready"], 1)

            def shift_scales(b):
                pool.wait_ge(s["s0_ve"], b + 1)
                gp.tensor_tensor(mean0[:, :], mv[:, :, 0], keep[:, :], ALU.mult)
                step(gp.tensor_tensor(rstd[:, :], ve[:, :], mhalf[:, :], ALU.pow))
                step(gp.tensor_tensor(rstd[:, :], rstd[:, :], keep[:, :], ALU.mult))
                gp.tensor_tensor(rstd[:, :], rstd[:, :], raw[:, :], ALU.add).then_inc(s["s0_ready"], 1)

            def route(b):
                pool.wait_ge(s["compared"], b + 1)
                step(gp.tensor_tensor(ties[:, :, :, :].rearrange("p t e f -> p t (e f)"),
                                      ties[:, :, :, :].rearrange("p t e f -> p t (e f)"),
                                      tri[:, :, :].rearrange("p e f -> p (e f)").unsqueeze(1).broadcast_to((P, NT, E * E)), ALU.mult))
                gp.tensor_tensor(beats[:, :, :, :].rearrange("p t e f -> p (t e f)"),
                                 beats[:, :, :, :].rearrange("p t e f -> p (t e f)"),
                                 ties[:, :, :, :].rearrange("p t e f -> p (t e f)"), ALU.add).then_inc(s["beats_ready"], 1)
                pool.wait_ge(s["sp_ready"], b + 1)
                gp.tensor_tensor(act[:, :, :].rearrange("p t e -> p (t e)"), sp[:, :, :].rearrange("p t e -> p (t e)"),
                                 phalf[:, :], ALU.pow).then_inc(s["a_ready"], 1)

            shift_scales(0)
            rstd_of(0)
            step(gp.memset(tri[:, :, :], 1.0))
            step(gp.affine_select(out=tri[:, :, :], in_=tri[:, :, :], compare_op=ALU.is_gt, fill=0.0, base=0,
                                  pattern=[[1, E], [-1, E]], channel_multiplier=0))
            step(gp.memset(cnat[:, :, :], 0.0))
            gp.memset(cnat[:, :, HE + E:HE + E + 1], 1.0).then_inc(s["zero_ready"], 1)
            gp.memset(mx[:, :, :, :].bitcast(F32), 0.0).then_inc(s["mx_z"], 1)
            step(gp.memset(VA[:, :, :, :], 0.0))
            gp.memset(VA[:, :, :, HD:HD + 1], 1.0).then_inc(s["VA_z"], 1)
            step(gp.memset(ones_p[96:128, :, :], 0.0))
            for at in (0, HG):
                step(gp.affine_select(out=ones_p[96:128, :, :], in_=ones_p[96:128, :, :], compare_op=ALU.not_equal, fill=1.0,
                                      base=-at, pattern=[[-1, HG], [0, C]], channel_multiplier=1))
            for gq in range(NG):
                last = gp.tensor_copy(KS[96:128, gq, :, :, :].rearrange("p b i c -> p b (i c)"),
                                      ones_p[96:128, :, :].rearrange("p i c -> p (i c)").unsqueeze(1).broadcast_to((32, B, HG * C)))
            last.then_inc(s["KS_ones"], 1)
            pool.wait_ge(s["KS_ones"], 1)
            step(gp.memset(M[:, 0, 0, :, :], 0.0))
            step(gp.affine_select(out=M[:, 0, 0, :, :], in_=M[:, 0, 0, :, :], compare_op=ALU.not_equal, fill=1.0, base=0,
                                  pattern=[[1, 8], [-1, 8]], channel_multiplier=0))
            gp.tensor_copy(M[:, 0, 1, :, :], M[:, 0, 0, :, :])
            step(gp.tensor_copy(M[:, 0, 2, :, :], M[:, 0, 0, :, :]))
            for b in range(B):
                if b + 1 < B:
                    shift_scales(b + 1)
                    rstd_of(b + 1)
                route(b)
                if b == 0:
                    pool.wait_ge(s["ld_bw"], 16 * 60)
                    for m in range(3):
                        lo = 2 ** m
                        hi = 4 // lo
                        src, dst = m % 2, 1 - m % 2
                        for d in range(3):
                            Mi = M[:, src, d, :, :].rearrange("p i (h c l) -> p i h c l", c=2, l=lo)
                            for r in range(2):
                                for c, t_ in ((0, pa), (1, pb)):
                                    w_ = BW[:, d, m, :, r, c].rearrange("p (h l) -> p h l", l=lo).unsqueeze(1).broadcast_to((P, 8, hi, lo))
                                    o_ = t_[:, r, d, :].rearrange("p (i h l) -> p i h l", i=8, l=lo)
                                    last = gp.tensor_tensor(o_, Mi[:, :, :, c, :], w_, ALU.mult)
                        step(last)
                        for d in range(3):
                            Mn = M[:, dst, d, :, :].rearrange("p i (h c l) -> p i h c l", c=2, l=lo)
                            for r in range(2):
                                a_ = pa[:, r, d, :].rearrange("p (i h l) -> p i h l", i=8, l=lo)
                                b_ = pb[:, r, d, :].rearrange("p (i h l) -> p i h l", i=8, l=lo)
                                last = gp.tensor_tensor(Mn[:, :, :, r, :], a_, b_, ALU.add)
                        step(last)
                    for d in range(3):
                        last = gp.tensor_copy(Mo[0:64, d, :, :], M[0:64, 1, d, :, :])
                    step(last)
                    for d in range(3):
                        last = gp.tensor_copy(Mo[64:128, d, :, :], M[64:128, 1, d, :, :].rearrange("p i j -> p j i"))
                    last.then_inc(s["M_ready"], 1)
                    pool.wait_ge(s["M_ready"], 1)
            pool.wait_ge(s["KR_ready"], 16 * 3 * NG)
            pool.wait_ge(s["masks_ready"], 1)
            for gq in range(NG):
                for b in range(B):
                    last = gp.tensor_tensor(KS[0:96, gq, b, :, :],
                                            KR[:, gq, C * b:C * b + C].bitcast(F32).unsqueeze(1).broadcast_to((96, HG, C)),
                                            hm[:, :].unsqueeze(2).broadcast_to((96, HG, C)), ALU.mult)
            last.then_inc(s["KS_ready"], 1)
            pool.wait_ge(s["ld_bc"], 64)
            gp.tensor_tensor(bfin[:, :], bfin[:, :], bfin2[:, :], ALU.add).then_inc(s["bfin_sum"], 1)
            pool.wait_ge(s["MR_ready"], 16 * 6)
            for ud in range(2):
                for t in range(NH):
                    gp.tensor_tensor(G0[:, ud, t, :].rearrange("p (k j) -> p k j", j=8),
                                     MR[:, ud, 0, t, :].unsqueeze(1).broadcast_to((P, 16, 8)),
                                     mk0[:, :].unsqueeze(2).broadcast_to((P, 16, 8)), ALU.mult)
                    for b6 in range(2):
                        gp.tensor_tensor(G1[:, ud, t, 64 * b6:64 * b6 + 64].rearrange("p (j k) -> p j k", k=8),
                                         MR[:, ud, 1, t, :].unsqueeze(2).broadcast_to((P, 8, 8)),
                                         mk1[:, b6, :].unsqueeze(1).broadcast_to((P, 8, 8)), ALU.mult)
                    last = gp.tensor_tensor(G2[:, ud, t, :, :].rearrange("p v (c k) -> p (v c) k", k=64),
                                            MR[:, ud, 2, t, :].unsqueeze(2).broadcast_to((P, 8, 64)),
                                            mk2[:, :].unsqueeze(1).broadcast_to((P, 8, 64)), ALU.mult)
            last.then_inc(s["G_ready"], 1)

            def add_row(b, k, row, done):
                pool.wait_ge(s["ln_nrm"], k)
                gp.tensor_tensor(X[:, b, :, :], X[:, b, :, :], row[:, :].unsqueeze(1).broadcast_to((P, NT, D)),
                                 ALU.add).then_inc(s[done], 1)

            for b in range(B):
                rstd_of(B + b)
                add_row(b, B + b + 1, bob, "bo_added")
            pool.wait_ge(s["bfin_sum"], 1)
            for b in range(B):
                rstd_of(2 * B + b)
                add_row(b, 2 * B + b + 1, bfin, "bfin_added")

        @block.scalar
        def _(act_):
            sc = nc.scalar
            n = [0]

            def step(ins):
                n[0] += 1
                ins.then_inc(s["act_step"], 1)
                act_.wait_ge(s["act_step"], n[0])

            act_.wait_ge(s["cols_ps"], 1)
            sc.copy(cols[:, 0:NR], bank[7][:, 0:NR]).then_inc(s["cols_ready"], 1)
            act_.wait_ge(s["conv_tp"], 1)
            act_.wait_ge(s["z_ready"], 1)
            sc.copy(cpad[:, :, :, CUT1:P].rearrange("p b r j -> p r b j"),
                    bank[0][:, 0:RATE * B * TC].rearrange("p (r b j) -> p r b j", r=RATE, b=B)).then_inc(s["conv_T"], 1)

            def copy_nT(k):
                act_.wait_ge(s["tp_ps"], k + 1)
                sc.copy(nT[:, k % 2, :], bank[0][:, :]).then_inc(s["nT_ready"], 1)

            def context(part):
                if part == 0:
                    act_.wait_ge(s["cxT_ps"], 1)
                    sc.copy(cxT[:, :], bank[7][:, 0:B * C]).then_inc(s["cxT_ready"], 1)
                    act_.wait_ge(s["k_ps"], 1)
                    sc.activation(kf[:, :], bank[7][:, 0:B * C], ACT.Identity, bias=cols[:, R_BK:R_BK + 1]).then_inc(s["kf_ready"], 1)

            for b in range(B):
                copy_nT(b)
                act_.wait_ge(s["lg_ready"], b + 1)
                step(sc.activation(el[:, :, :], nlg[:, :, :], ACT.Exp))
                sc.activation(rt[:, :, :], el[:, :, :], ACT.Ln, bias=1.0).then_inc(s["ln_ready"], 1)
                for j in range(NJ + 1):
                    act_.wait_ge(s["hid_ps"], (NJ + 1) * b + j + 1)
                    if j < NJ:
                        if b >= 1:
                            act_.wait_ge(s["gated"], NJ * (b - 1) + j + 1)
                        sc.activation(sil[:, j, :], bank[2 + ((NJ + 1) * b + j) % 2][:, :], ACT.Silu,
                                      bias=cols[:, R_RB1 + j:R_RB1 + j + 1]).then_inc(s["silu_done"], 1)
                    else:
                        if b >= 2:
                            act_.wait_ge(s["y_ps"], b - 1)
                        sc.activation(g[0:HE, b % 2, NJ, :], bank[2 + ((NJ + 1) * b + j) % 2][0:HE, :], ACT.Silu,
                                      bias=cols[0:HE, R_SB1:R_SB1 + 1]).then_inc(s["silu_done"], 1)
                act_.wait_ge(s["combT_ps"], b + 1)
                sc.copy(cT24[:, :], bank[0][0:NB * E, 0:S // 2].bitcast(BF16))
                sc.copy(g[HE:HE + E + 1, b % 2, NJ, :], bank[1][HE:HE + E + 1, :]).then_inc(s["combT_ready"], 1)
                if b == 1:
                    context(0)

            def butterfly_copies():
                act_.wait_ge(s["wexpT_ps"], 1)
                sc.copy(U[:, 0, :, 0:D], bank[7][:, :].rearrange("p (t d) -> p t d", t=NH))
                sc.copy(U[:, 0, :, D:D + 1], cols[:, R_BE:R_BE + NH].unsqueeze(2))
                sc.copy(U[:, 0, :, D + 1:D + 2], cols[:, R_BE:R_BE + NH].unsqueeze(2)).then_inc(s["u_ready"], 1)
                for k in range(3):
                    for t in range(NH):
                        act_.wait_ge(s["u_ps"], NH * k + t + 1)
                        sc.copy(U[:, (k + 1) % 2, t, :], bank[6 + t % 2][:, 0:D + 2]).then_inc(s["u_ready"], 1)
                    for t in range(NH):
                        act_.wait_ge(s["v2_ps"], NH * k + t + 1)
                        sc.copy(V[:, (k + 1) % 2, t, :], bank[6 + t % 2][:, 0:D]).then_inc(s["v2_ready"], 1)
                act_.wait_ge(s["wup_ps"], 1)
                sc.copy(wup[:, :], bank[7][:, :]).then_inc(s["wup_ready"], 1)

            butterfly_copies()

            def query(b):
                copy_nT(B + b)
                act_.wait_ge(s["q_ps"], b + 1)
                if b >= 1:
                    act_.wait_ge(s["q_split"], b)
                sc.activation(qf[:, :], bank[1][:, :], ACT.Identity, bias=cols[:, R_BQ:R_BQ + 1]).then_inc(s["qf_ready"], 1)

            def max_rows(b):
                act_.wait_ge(s["mT_ps"], b + 1)
                if b >= 2:
                    act_.wait_ge(ld_MX[b % 2], 16 * NG * (b // 2))
                sc.copy(mT[:, b % 2, :], bank[0][:, :]).then_inc(s["mT_ready"], 1)

            def probs(b):
                for gq in range(NG):
                    for i2 in range(2):
                        k = (NG * b + gq) * 2 + i2
                        act_.wait_ge(s["s_ps"], k + 1)
                        if k >= 2:
                            act_.wait_ge(s["pv_pair"], k - 1)
                        for i in range(2):
                            last = sc.activation(pe_[:, k % 2, i, :], bank[4 + 2 * (k % 2) + i][0:C, :], ACT.Exp, scale=SCALE)
                        last.then_inc(s["exp_done"], 1)
                    if gq >= 1:
                        values(b, gq - 1)
                values(b, NG - 1)

            def values(b, gq):
                act_.wait_ge(s["pv_pair"], 2 * (NG * b + gq + 1))
                if b >= 2:
                    act_.wait_ge(s["ut_ps"], NT * (b - 1))
                sc.copy(US[:, b % 2, gq, :], bank[2 + gq % 2][:, :]).then_inc(s["us_ready"], 1)

            def attn_T(b):
                act_.wait_ge(s["anT_ps"], b + 1)
                sc.copy(aT[:, b % 2, :], bank[0][:, :]).then_inc(s["aT_ready"], 1)

            for b in range(B):
                query(b)
                max_rows(b)
                probs(b)
                attn_T(b)

            for b in range(B):
                copy_nT(2 * B + b)
                act_.wait_ge(s["bup_ready"], 1)
                for j in range(NH):
                    k = NH * b + j
                    act_.wait_ge(s["hid1_ps"], k + 1)
                    if b >= 2:
                        act_.wait_ge(s["y1_ps"], b - 1)
                    sc.activation(ge[:, b % 2, j, :], bank[2 + k % 2][:, :], ACT.Gelu, bias=bup[:, j:j + 1]).then_inc(s["gelu_done"], 1)

        @block.vector
        def _(dve):
            v = nc.vector
            n = [0]

            def step(ins):
                n[0] += 1
                ins.then_inc(s["dve_step"], 1)
                dve.wait_ge(s["dve_step"], n[0])

            def moments(src, rows_, ready, tiles=NT):
                for t in range(tiles):
                    last = v.bn_stats(stat[0:rows_, t, :], src(t))
                step(last)
                for t in range(tiles):
                    last = v.bn_aggr(mv[0:rows_, t, :], stat[0:rows_, t, :])
                step(last)
                v.tensor_scalar(ve[0:rows_, 0:tiles], mv[0:rows_, 0:tiles, 1], EPS, None, ALU.add).then_inc(s[ready], 1)

            dve.wait_ge(s["ld_xc"], 16 * B)
            moments(lambda r: xc[:, r, :], B * TC, "conv_ve")
            dve.wait_ge(s["conv_rstd"], 1)
            for r in range(RATE):
                last = v.tensor_scalar(xcn[:, r, :], xc[:, r, :], mv[0:B * TC, r, 0:1], rstd[0:B * TC, r:r + 1], ALU.subtract, ALU.mult)
            last.then_inc(s["conv_nrm"], 1)

            def shift(b):
                dve.wait_ge(ld_xs[b], 64)
                moments(lambda t: XS[:, b, t, :], P, "s0_ve")
                dve.wait_ge(s["s0_ready"], b + 1)
                for t in range(NT):
                    last = v.tensor_scalar(XS[:, b, t, :], XS[:, b, t, :], mean0[:, t:t + 1], rstd[:, t:t + 1], ALU.subtract, ALU.mult)
                step(last)
                dve.wait_ge(ld_x[b], 16)
                step(v.tensor_tensor(X[:, b, :, :], X[:, b, :, :], XS[:, b, :, :], ALU.add))
                if b == 0:
                    dve.wait_ge(s["conv_ps"], B)
                    v.tensor_copy(comp[:, :, :].rearrange("p b d -> p (b d)"), bank[4][:, :]).then_inc(s["x1_conv"], 1)
                    dve.wait_ge(s["x1_conv"], 1)
                step(v.tensor_tensor(X[:, b, 1, :], X[:, b, 1, :], comp[:, b, :], ALU.add))

            def normalise(b, k):
                moments(lambda t: X[:, b, t, :], P, "ve_ready")
                dve.wait_ge(s["rstd_ready"], k + 1)
                if k >= 2:
                    dve.wait_ge(s["tp_ps"], k - 1)
                for t in range(NT):
                    last = v.tensor_scalar(nrm[:, k % 2, t, :], X[:, b, t, :], mv[:, t, 0:1], rstd[:, t:t + 1], ALU.subtract, ALU.mult)
                last.then_inc(s["ln_nrm"], 1)

            def route(b):
                dve.wait_ge(s["logits_ps"], b + 1)
                if b == 0:
                    dve.wait_ge(s["ld_rows"], 16 * 8)
                if b >= 1:
                    dve.wait_ge(s["beats_ready"], b)
                step(v.tensor_tensor(lg[:, :, :], bank[1][:, 0:NT * E].rearrange("p (t e) -> p t e", e=E),
                                     ebias[:, :].unsqueeze(1).broadcast_to((P, NT, E)), ALU.add))
                v.scalar_tensor_tensor(out=nlg[:, :, :], in0=lg[:, :, :], scalar=-1.0, in1=lg[:, :, :],
                                       op0=ALU.mult, op1=ALU.min).then_inc(s["lg_ready"], 1)
                other = lg[:, :, :].unsqueeze(2).broadcast_to((P, NT, E, E))
                own = lg[:, :, :].unsqueeze(3).broadcast_to((P, NT, E, E))
                dve.wait_ge(s["lg_ready"], b + 1)
                v.tensor_tensor(beats[:, :, :, :], other, own, ALU.is_gt)
                v.tensor_tensor(ties[:, :, :, :], other, own, ALU.is_equal).then_inc(s["compared"], 1)
                dve.wait_ge(s["ln_ready"], b + 1)
                step(v.tensor_scalar(res[:, 0, :, :], el[:, :, :], 1.0, -1.0, ALU.add, ALU.add))
                v.tensor_tensor(res[:, 1, :, :], el[:, :, :], res[:, 0, :, :], ALU.subtract)
                step(v.scalar_tensor_tensor(out=sp[:, :, :], in0=lg[:, :, :], scalar=0.0, in1=rt[:, :, :],
                                            op0=ALU.max, op1=ALU.add))
                v.tensor_tensor(sp[:, :, :], sp[:, :, :], res[:, 1, :, :], ALU.add).then_inc(s["sp_ready"], 1)
                dve.wait_ge(s["beats_ready"], b + 1)
                v.tensor_reduce(rank[:, :, :], beats[:, :, :, :], axis=AX.X, op=ALU.add)
                dve.wait_ge(s["a_ready"], b + 1)
                if b == 0:
                    dve.wait_ge(s["zero_ready"], 1)
                else:
                    dve.wait_ge(s["combT_ps"], b)
                comb = cnat[:, :, HE:HE + E]
                step(v.tensor_copy(res[:, 0, :, :], act[:, :, :]))
                step(v.scalar_tensor_tensor(out=comb, in0=rank[:, :, :], scalar=1.5, in1=act[:, :, :],
                                            op0=ALU.is_lt, op1=ALU.mult))
                step(v.tensor_copy(c24[:, :, 0, :], comb))
                step(v.tensor_tensor(res[:, 0, :, :], comb, c24[:, :, 0, :], ALU.subtract))
                step(v.tensor_copy(c24[:, :, 1, :], res[:, 0, :, :]))
                v.tensor_tensor(c24[:, :, 2, :], res[:, 0, :, :], c24[:, :, 1, :], ALU.subtract).then_inc(s["comb_ready"], 1)

            def gate(b):
                for j in range(NJ):
                    dve.wait_ge(s["gate_ps"], NJ * b + j + 1)
                    dve.wait_ge(s["silu_done"], (NJ + 1) * b + j + 1)
                    if b >= 2:
                        dve.wait_ge(s["y_ps"], b - 1)
                    v.tensor_tensor(g[:, b % 2, j, :], sil[:, j, :], bank[4 + (j % 2)][:, :], ALU.mult).then_inc(s["gated"], 1)
                dve.wait_ge(s["y_ps"], b + 1)
                v.tensor_tensor(X[:, b, :, :].rearrange("p t d -> p (t d)"), X[:, b, :, :].rearrange("p t d -> p (t d)"),
                                bank[6][:, :], ALU.add).then_inc(s["x2_done"], 1)

            shift(0)
            normalise(0, 0)
            dve.wait_ge(s["ident_ready"], 1)
            v.tensor_copy(identb[:, :], ident[:, :])
            v.tensor_reduce(mk0[:, :], ident[:, :].rearrange("p (k j) -> p k j", j=8), axis=AX.X, op=ALU.add)
            v.tensor_reduce(mk1[:, :, :], ident[:, :].rearrange("p (b j k) -> p b k j", b=2, k=8), axis=AX.X, op=ALU.add)
            v.tensor_tensor(mk2[:, :], ident[:, 0:64], ident[:, 64:128], ALU.add)
            v.tensor_reduce(hm[:, :], ident[0:96, :].rearrange("p (b i d) -> p i b d", b=NG, d=HD), axis=AX.XY, op=ALU.add)
            step(v.tensor_reduce(sel8[:, :], ident[0:NB * E, 0:NB * E].rearrange("p (s e) -> p e s", s=NB), axis=AX.X, op=ALU.add))
            v.tensor_copy(sel[:, :, :], sel8[:, :].unsqueeze(2).broadcast_to((NB * E, E, HE))).then_inc(s["masks_ready"], 1)
            for b in range(B):
                if b + 1 < B:
                    shift(b + 1)
                    normalise(b + 1, b + 1)
                route(b)
                gate(b)
                if b == 1:
                    dve.wait_ge(s["kf_ready"], 1)
                    step(v.tensor_copy(kh[:, :], kf[:, :]))
                    v.tensor_tensor(kl[:, :], kf[:, :], kh[:, :].bitcast(F32), ALU.subtract).then_inc(s["k_split"], 1)
                    dve.wait_ge(s["v_ps"], 1)
                    dve.wait_ge(s["ld_bc"], 64)
                    dve.wait_ge(s["VA_z"], 1)
                    for b_ in range(B):
                        last = v.tensor_tensor(VA[:, b_, :, 0:HD], bank[7][0:C, D * b_:D * b_ + D].rearrange("p (h d) -> p h d", d=HD),
                                               bvb[0:C, :].rearrange("p (h d) -> p h d", d=HD), ALU.add)
                    last.then_inc(s["VA_ready"], 1)

            def split_q(b):
                dve.wait_ge(s["qf_ready"], b + 1)
                if b >= 2:
                    dve.wait_ge(ld_QS[b % 2], 16 * 3 * NG * (b // 2))
                step(v.tensor_copy(qh[:, b % 2, :], qf[:, :]))
                v.tensor_tensor(ql[:, b % 2, :], qf[:, :], qh[:, b % 2, :].bitcast(F32), ALU.subtract).then_inc(s["q_split"], 1)

            def maxima(b):
                for t in range(NT):
                    for gq in range(NG):
                        k = NG * t + gq
                        dve.wait_ge(s["a_ps"], NT * NG * b + k + 1)
                        last = v.tensor_reduce(nm[:, t, HG * gq:HG * gq + HG],
                                               bank[2 + k % 2][:, 0:HG * C].rearrange("p (i c) -> p i c", i=HG),
                                               axis=AX.X, op=ALU.max, negate=True)
                        last.then_inc(s["max_done"], 1)
                dve.wait_ge(s["max_done"], NT * NG * (b + 1))
                if b == 0:
                    dve.wait_ge(s["mx_z"], 1)
                else:
                    dve.wait_ge(s["mT_ps"], b)
                nm_ = nm[:, :, :].rearrange("p t (q i) -> p t q i", i=HG)
                step(v.tensor_copy(mx[:, :, :, 0:HG], nm_))
                v.tensor_tensor(mx[:, :, :, HG:2 * HG], nm_, mx[:, :, :, 0:HG].bitcast(F32), ALU.subtract).then_inc(s["mx_ready"], 1)

            def finish_attention(b):
                for t in range(NT):
                    dve.wait_ge(s["ut_ps"], NT * b + t + 1)
                    pt = bank[t % 2][:, :].rearrange("p (h c) -> p h c", c=32)
                    step(v.reciprocal(rec[:, t % 2, :], pt[:, :, HD]))
                    v.tensor_tensor(an[:, t, :].rearrange("p (h d) -> p h d", d=HD), pt[:, :, 0:HD],
                                    rec[:, t % 2, :].unsqueeze(2).broadcast_to((P, HEADS, HD)), ALU.mult).then_inc(s["an_ready"], 1)
                dve.wait_ge(s["o_ps"], b + 1)
                dve.wait_ge(s["bo_added"], b + 1)
                v.tensor_tensor(X[:, b, :, :].rearrange("p t d -> p (t d)"), X[:, b, :, :].rearrange("p t d -> p (t d)"),
                                bank[1][:, :], ALU.add).then_inc(s["x3_done"], 1)

            for b in range(B):
                dve.wait_ge(s["x2_done"], b + 1)
                normalise(b, B + b)
                split_q(b)
                maxima(b)
                finish_attention(b)
            dve.wait_ge(s["u_ready"], 1 + 3 * NH)
            v.tensor_tensor(bup[:, :], U[:, 1, :, D], cols[:, R_UB:R_UB + NH], ALU.add).then_inc(s["bup_ready"], 1)
            for b in range(B + 1):
                if b < B:
                    dve.wait_ge(s["x3_done"], b + 1)
                    normalise(b, 2 * B + b)
                if b >= 1:
                    dve.wait_ge(s["y1_ps"], b)
                    dve.wait_ge(s["bfin_added"], b)
                    v.tensor_tensor(X[:, b - 1, :, :].rearrange("p t d -> p (t d)"), X[:, b - 1, :, :].rearrange("p t d -> p (t d)"),
                                    bank[6][:, :], ALU.add).then_inc(s["x4_done"], 1)

        @block.tensor
        def _(pe):
            mm, tp = nc.tensor.matmul, nc.tensor.transpose
            pe.wait_ge(s["ident_ready"], 1)
            pe.wait_ge(s["ld_rows"], 16 * 8)
            tp(bank[7][:, 0:NR], rows[0:NR, :], ident[0:NR, 0:NR]).then_inc(s["cols_ps"], 1)
            pe.wait_ge(s["conv_nrm"], 1)
            for r in range(RATE):
                last = tp(bank[0][:, r * B * TC:(r + 1) * B * TC], xcn[:, r, :], ident[0:B * TC, 0:B * TC])
            last.then_inc(s["conv_tp"], 1)
            pe.wait_ge(s["ld_conv"], 32)
            pe.wait_ge(s["conv_T"], 1)
            for b in range(B):
                for r in range(RATE):
                    mm(bank[4][:, P * b:P * b + P], cpad[:, b, r, :], convw[:, r, :], start=(r == 0), stop=False)
                mm(bank[4][:, P * b:P * b + P], convm[:, :], convb[:, :], start=False, stop=True).then_inc(s["conv_ps"], 1)

            def transposed_rows(k):
                pe.wait_ge(s["ln_nrm"], k + 1)
                if k >= 1:
                    pe.wait_ge(s["nT_ready"], k)
                for t in range(NT):
                    last = tp(bank[0][:, P * t:P * t + P], nrm[:, k % 2, t, :], ident[:, :])
                last.then_inc(s["tp_ps"], 1)
                pe.wait_ge(s["nT_ready"], k + 1)

            for b in range(B):
                u = b % 2
                if b >= 1:
                    pe.wait_ge(s["combT_ready"], b)
                transposed_rows(b)
                if b == 0:
                    pe.wait_ge(s["cols_ready"], 1)
                for t in range(NT):
                    last = mm(bank[1][:, E * t:E * t + E], nT[:, u, P * t:P * t + P], cols[:, R_RW:R_RW + E], start=True, stop=True)
                last.then_inc(s["logits_ps"], 1)
                if b == 0:
                    pe.wait_ge(s["ld_w1"], 32)
                for j in range(NJ + 1):
                    k = (NJ + 1) * b + j
                    m = P if j < NJ else HE
                    if k >= 2:
                        pe.wait_ge(s["silu_done"], k - 1)
                    mm(bank[2 + k % 2][0:m, :], w1[:, P * j:P * j + m], nT[:, u, :], start=True, stop=True).then_inc(s["hid_ps"], 1)
                pe.wait_ge(s["comb_ready"], b + 1)
                if b == 0:
                    pe.wait_ge(s["masks_ready"], 1)
                for t in range(NT):
                    tp(bank[1][0:CW, P * t:P * t + P], cnat[:, t, :], ident[:, :])
                    last = tp(bank[0][0:NB * E, P // 2 * t:P // 2 * t + P // 2].bitcast(BF16), c24[:, t, :, :].rearrange("p s e -> p (s e)"), identb[:, :])
                last.then_inc(s["combT_ps"], 1)
                pe.wait_ge(s["combT_ready"], b + 1)
                for j in range(NJ):
                    if j >= 2:
                        pe.wait_ge(s["gated"], NJ * b + j - 1)
                    elif b >= 1:
                        pe.wait_ge(s["gated"], NJ * b)
                    else:
                        pe.wait_ge(s["x1_conv"], 1)
                    mm(bank[4 + j % 2][:, :], sel[:, 2 * j:2 * j + 2, :].rearrange("p e h -> p (e h)"), cT24[:, :],
                       start=True, stop=True).then_inc(s["gate_ps"], 1)
                if b == 0:
                    pe.wait_ge(s["ld_w2"], 64)
                if b == 1:
                    pe.wait_ge(s["ld_cx"], 16)
                    pe.wait_ge(s["ld_wa"], 64)
                    for b_ in range(B):
                        last = tp(bank[7][:, C * b_:C * b_ + C], cx[:, b_, :], ident[0:C, 0:C])
                    last.then_inc(s["cxT_ps"], 1)
                    pe.wait_ge(s["cxT_ready"], 1)
                    mm(bank[7][:, 0:B * C], wk[:, :], cxT[:, :], start=True, stop=True).then_inc(s["k_ps"], 1)
                pe.wait_ge(s["gated"], NJ * (b + 1))
                pe.wait_ge(s["silu_done"], (NJ + 1) * (b + 1))
                if b >= 1:
                    pe.wait_ge(s["x2_done"], b)
                for t in range(NT):
                    for j in range(NJ + 1):
                        kk = P if j < NJ else HE + E + 1
                        last = mm(bank[6][:, P * t:P * t + P], g[0:kk, u, j, P * t:P * t + P], w2[0:kk, j, :],
                                  start=(j == 0), stop=(j == NJ))
                last.then_inc(s["y_ps"], 1)
                if b == 1:
                    pe.wait_ge(s["kf_ready"], 1)
                    for b_ in range(B):
                        last = mm(bank[7][0:C, D * b_:D * b_ + D], cxT[:, C * b_:C * b_ + C], wv[:, :], start=True, stop=True)
                    last.then_inc(s["v_ps"], 1)

            def butterfly():
                pe.wait_ge(s["ld_wexp"], 16)
                pe.wait_ge(s["ld_wcon"], 16)
                pe.wait_ge(s["VA_ready"], 1)
                for t in range(NH):
                    last = tp(bank[7][:, P * t:P * t + P], wexp[:, P * t:P * t + P], ident[:, :])
                last.then_inc(s["wexpT_ps"], 1)
                pe.wait_ge(s["G_ready"], 1)
                pe.wait_ge(s["x2_done"], B)

                def digit(ud, d, src, dst, width, psn, prev):
                    for t in range(NH):
                        pe.wait_ge(*prev(t))
                        o = bank[6 + t % 2][:, 0:width]
                        if d == 2:
                            for t_ in range(NH):
                                last = mm(o, G2[:, ud, t_, t, :], src[:, t_, :], start=(t_ == 0), stop=(t_ == NH - 1))
                        else:
                            last = mm(o, (G0, G1)[d][:, ud, t, :], src[:, t, :], start=True, stop=True)
                        last.then_inc(s[psn], 1)

                for k in range(3):
                    digit(0, k, U[:, k % 2, :, :], None, D + 2, "u_ps",
                          lambda t: (s["u_ready"], 1 + NH * k + max(t - 1, 0)) if t or not k else (s["u_ready"], 1 + NH * k))
                    pe.wait_ge(s["u_ready"], 1 + NH * (k + 1))
                    digit(1, 2 - k, V[:, k % 2, :, :], None, D, "v2_ps",
                          lambda t: (s["v2_ready"], NH * k + t - 1) if t >= 2 else (s["u_ready"], 1 + NH * (k + 1)))
                    pe.wait_ge(s["v2_ready"], NH * (k + 1))
                for t in range(NH):
                    last = tp(bank[7][:, P * t:P * t + P], U[:, 1, t, 0:D], ident[:, :])
                last.then_inc(s["wup_ps"], 1)
                pe.wait_ge(s["wup_ready"], 1)

            butterfly()

            for b in range(B):
                u = b % 2
                if b == 0:
                    pe.wait_ge(s["combT_ready"], B)
                else:
                    pe.wait_ge(s["aT_ready"], b)
                    pe.wait_ge(s["x3_done"], b)
                transposed_rows(B + b)
                mm(bank[1][:, :], wq[:, :], nT[:, (B + b) % 2, :], start=True, stop=True).then_inc(s["q_ps"], 1)
                if b == 0:
                    pe.wait_ge(s["KS_ready"], 1)
                    pe.wait_ge(s["KS_ones"], 1)
                    pe.wait_ge(s["silu_done"], (NJ + 1) * B)
                else:
                    pe.wait_ge(s["us_ready"], NG * b)
                pe.wait_ge(ld_QS[u], 16 * 3 * NG * (b // 2 + 1))
                for t in range(NT):
                    for gq in range(NG):
                        k = NG * t + gq
                        if k >= 2:
                            pe.wait_ge(s["max_done"], NT * NG * b + k - 1)
                        mm(bank[2 + k % 2][:, 0:HG * C], QS[0:96, u, gq, P * t:P * t + P],
                           KS[0:96, gq, b, :, :].rearrange("p i c -> p (i c)"), start=True, stop=True).then_inc(s["a_ps"], 1)
                pe.wait_ge(s["mx_ready"], b + 1)
                for t in range(NT):
                    last = tp(bank[0][:, P * t:P * t + P], mx[:, t, :, :].bitcast(F32).rearrange("p q c -> p (q c)"), ident[:, :])
                last.then_inc(s["mT_ps"], 1)
                pe.wait_ge(ld_MX[u], 16 * NG * (b // 2 + 1))

                def scores(k):
                    gq, i2 = k // 2, k % 2
                    kk = 2 * NG * b + k
                    if kk >= 2:
                        pe.wait_ge(s["exp_done"], kk - 1)
                    for i in range(2):
                        last = mm(bank[4 + 2 * (kk % 2) + i][0:C, :], KS[:, gq, b, 2 * i2 + i, :], QS[:, u, gq, :], start=True, stop=True)
                    last.then_inc(s["s_ps"], 1)

                def weighted(k):
                    gq, i2 = k // 2, k % 2
                    kk = 2 * NG * b + k
                    pe.wait_ge(s["exp_done"], kk + 1)
                    if gq >= 2:
                        pe.wait_ge(s["us_ready"], NG * b + gq - 1)
                    else:
                        pe.wait_ge(s["max_done"], NT * NG * (b + 1))
                    for i in range(2):
                        h = HG * gq + 2 * i2 + i
                        q = 32 * (2 * i2 + i)
                        last = mm(bank[2 + gq % 2][q:q + 32, :], VA[:, b, h, :], pe_[:, kk % 2, i, :], start=True, stop=True,
                                  skip_group_check=True)
                    last.then_inc(s["pv_pair"], 1)
                if b == 0:
                    pe.wait_ge(s["VA_ready"], 1)
                    pe.wait_ge(s["gated"], NJ * B)
                scores(0)
                for k in range(1, 2 * NG):
                    scores(k)
                    weighted(k - 1)
                weighted(2 * NG - 1)
                pe.wait_ge(s["us_ready"], NG * (b + 1))
                pe.wait_ge(s["mT_ready"], b + 1)
                pe.wait_ge(s["qf_ready"], b + 1)
                for t in range(NT):
                    if t >= 2:
                        pe.wait_ge(s["an_ready"], NT * b + t - 1)
                    for gq in range(NG):
                        last = tp(bank[t % 2][:, P * gq:P * gq + P], US[:, u, gq, P * t:P * t + P], ident[:, :])
                    last.then_inc(s["ut_ps"], 1)
                pe.wait_ge(s["an_ready"], NT * (b + 1))
                for t in range(NT):
                    last = tp(bank[0][:, P * t:P * t + P], an[:, t, :], ident[:, :])
                last.then_inc(s["anT_ps"], 1)
                pe.wait_ge(s["aT_ready"], b + 1)
                for t in range(NT):
                    last = mm(bank[1][:, P * t:P * t + P], aT[:, u, P * t:P * t + P], wo[:, :], start=True, stop=True)
                last.then_inc(s["o_ps"], 1)

            for b in range(B):
                u = b % 2
                if b == 0:
                    pe.wait_ge(s["aT_ready"], B)
                transposed_rows(2 * B + b)
                for j in range(NH):
                    k = NH * b + j
                    if k >= 2:
                        pe.wait_ge(s["gelu_done"], k - 1)
                    else:
                        pe.wait_ge(s["us_ready"], NG * B)
                    mm(bank[2 + k % 2][:, :], wup[:, P * j:P * j + P], nT[:, (2 * B + b) % 2, :], start=True, stop=True).then_inc(s["hid1_ps"], 1)
                pe.wait_ge(s["gelu_done"], NH * (b + 1))
                if b >= 1:
                    pe.wait_ge(s["x4_done"], b)
                else:
                    pe.wait_ge(s["exp_done"], 2 * NG * B)
                for t in range(NT):
                    for j in range(NH):
                        last = mm(bank[6][:, P * t:P * t + P], ge[:, u, j, P * t:P * t + P], V[:, 1, j, :], start=(j == 0), stop=(j == NH - 1))
                last.then_inc(s["y1_ps"], 1)


def kernel(**inputs):
    import numpy as np
    import concourse.bacc as bacc
    from concourse.bass_utils import run_bass_kernel_spmd

    nc = bacc.Bacc("TRN2", target_bir_lowering=False, num_devices=1)
    arrays, aps = {}, {}
    for name, a in inputs.items():
        a = np.ascontiguousarray(a)
        arrays[f"in_{name}"] = a
        aps[name] = nc.dram_tensor(f"in_{name}", a.shape, mybir.dt.from_np(a.dtype), kind="ExternalInput").ap()
    shape = arrays["in_x"].shape
    out = nc.dram_tensor("out_x", shape, F32, kind="ExternalOutput").ap()
    two_layer_block(nc, aps, out)
    r = run_bass_kernel_spmd(nc, [arrays], core_ids=[0])
    return r.results[0]["out_x"]
```

```python
from contextlib import ExitStack

import concourse.bass as bass
from concourse import mybir

F32 = mybir.dt.float32
F32R = mybir.dt.float32r
BF16 = mybir.dt.bfloat16
ALU = mybir.AluOpType
ACT = mybir.ActivationFunctionType
AX = mybir.AxisListType

P = 128
EPS = 1e-5


def two_layer_block(nc, inp, out):
    x, ctx_in = inp["x"], inp["ctx_1024"]
    B, S, D = x.shape
    C = ctx_in.shape[1]
    NT = S // P
    RATE = inp["L0_xattn_conv_w"].shape[0]
    HALF = S // 2
    TC = (C - RATE) // RATE + 1
    E, HE = inp["L0_ffn_rb1"].shape
    NJ = E * HE // P
    HID = inp["L1_ffn_W_exp"].shape[1]
    NH = HID // P
    HEADS = 16
    HD = D // HEADS
    NG = D // 32
    HG = HEADS // NG
    SCALE = float(HD) ** -0.5
    NB = 3
    CUT1 = HALF - TC - P
    CUT3 = S - C - 3 * P
    CW = 96

    ctx = ExitStack()
    with ctx:
        def sb(name, shape, dt=F32):
            return ctx.enter_context(nc.sbuf_tensor(name, shape, dt))

        def sem(name):
            return ctx.enter_context(nc.semaphore(name))

        X = sb("X", [P, B, NT, D])
        XS = sb("XS", [P, B, NT, D])
        xc = sb("xc", [B * TC, RATE, D])
        xcn = sb("xcn", [B * TC, RATE, D])
        cpad = sb("cpad", [P, B, RATE, P])
        convw = sb("convw", [P, RATE, D])
        comp = sb("comp", [P, B, D])
        convb = sb("convb", [1, D])
        convm = sb("convm", [1, P])
        nrm = sb("nrm", [P, 2, NT, D])
        nT = sb("nT", [P, 2, S])
        stat = sb("stat", [P, NT, 6])
        mv = sb("mv", [P, 2, NT, 2])
        ve = sb("ve", [P, 2, NT])
        rstd = sb("rstd", [P, 2, NT])
        smv = sb("smv", [P, 2, NT, 2])
        sve = sb("sve", [P, 2, NT])
        srs = sb("srs", [P, 2, NT])
        smean = sb("smean", [P, 2, NT])
        cstat = sb("cstat", [B * TC, RATE, 6])
        cmv = sb("cmv", [B * TC, RATE, 2])
        cve = sb("cve", [B * TC, RATE])
        crs = sb("crs", [B * TC, RATE])
        keep = sb("keep", [P, NT])
        raw = sb("raw", [P, NT])
        mhalf = sb("mhalf", [P, NT])
        phalf = sb("phalf", [P, NT, 2])
        ident = sb("ident", [P, P])
        identb = sb("identb", [P, P], BF16)
        rows = sb("rows", [32, P])
        cols = sb("cols", [P, 32])
        w1 = sb("w1", [P, E * HE + HE])
        w2 = sb("w2", [P, NJ + 1, D])
        ebias = sb("ebias", [P, E])
        tri = sb("tri", [P, E, E])
        lg = sb("lg", [P, NT, E])
        nlg = sb("nlg", [P, NT, E])
        el = sb("el", [P, NT, E])
        sp = sb("sp", [P, NT, E])
        rt = sb("rt", [P, NT, E])
        top = sb("top", [P, NT, 8])
        roots = sb("roots", [P, NT, 2])
        beats = sb("beats", [P, NT, E, E])
        ties = sb("ties", [P, NT, E, E])
        rank = sb("rank", [P, NT, E])
        cnat = sb("cnat", [P, NT, CW])
        res = sb("res", [P, 2, NT, E])
        c24 = sb("c24", [P, NT, NB, E], BF16)
        cT24 = sb("cT24", [NB * E, S], BF16)
        sel8 = sb("sel8", [NB * E, E])
        sel = sb("sel", [NB * E, E, HE], BF16)
        sil = sb("sil", [P, NJ, S])
        g = sb("g", [P, 2, NJ + 1, S])
        wq = sb("wq", [P, D])
        wk = sb("wk", [P, D])
        wv = sb("wv", [P, D])
        wo = sb("wo", [P, D])
        bvb = sb("bvb", [P, D])
        bob = sb("bob", [P, D])
        bfin = sb("bfin", [P, D])
        bfin2 = sb("bfin2", [P, D])
        cx = sb("cx", [C, B, D])
        cxT = sb("cxT", [P, B * C])
        kf = sb("kf", [P, B * C])
        kh = sb("kh", [P, B * C], F32R)
        kl = sb("kl", [P, B * C], F32R)
        KR = sb("KR", [96, NG, B * C], F32R)
        hm = sb("hm", [96, HG])
        ones_p = sb("ones_p", [P, HG, C])
        KS = sb("KS", [P, NG, B, HG, C], F32R)
        VA = sb("VA", [C, B, HEADS, 32])
        qf = sb("qf", [P, S])
        qh = sb("qh", [P, 2, S], F32R)
        ql = sb("ql", [P, 2, S], F32R)
        QS = sb("QS", [P, 2, NG, S], F32R)
        nm = sb("nm", [P, NT, HEADS])
        mx = sb("mx", [P, NT, NG, 32], F32R)
        mT = sb("mT", [P, 2, S], F32R)
        pe_ = sil[0:C, :, :]
        pring = 4
        US = sb("US", [P, 2, NG, S])
        rec = sb("rec", [P, 2, HEADS])
        an = sb("an", [P, NT, D])
        aT = sb("aT", [P, 2, S])
        wexp = sb("wexp", [P, HID])
        BW = sb("BW", [P, 3, 12, 2, 2])
        M = sb("M", [P, 2, 3, 8, 8])
        pa = sb("pa", [P, 2, 3, 32])
        pb = sb("pb", [P, 2, 3, 32])
        Mo = sb("Mo", [P, 3, 8, 8])
        MR = sb("MR", [P, 3, 2, NH, 8])
        mk0 = sb("mk0", [P, 16])
        mk1 = sb("mk1", [P, 2, 8])
        mk2 = sb("mk2", [P, 64])
        G0 = sb("G0", [P, 2, NH, P])
        G1 = sb("G1", [P, 2, NH, P])
        G2 = g[:, :, 0:NH, :].rearrange("p u t (v k) -> p u t v k", k=P)
        U = sb("U", [P, 2, NH, D + 2])
        V = sb("V", [P, 2, NH, D])
        wup = sb("wup", [P, HID])
        bup = sb("bup", [P, NH])
        ge = g

        bank = [ctx.enter_context(nc.psum_tensor(f"bank{i}", [P, S], F32)) for i in range(8)]
        bw_dram = nc.dram_tensor("bw_dram", (2, 4, 24, 32), F32, kind="Internal").ap()
        mid_dram = nc.dram_tensor("mid_dram", (8, P, 8), F32, kind="Internal").ap()
        mh_dram = nc.dram_tensor("mh_dram", (3, 2, HID, 8), F32, kind="Internal").ap()

        names = """ld_xc ld_conv ld_rows ld_w1 ld_w2 ld_bc ld_cx ld_wa ld_wk ld_wv ld_wexp ld_wcon bw_sorted ld_bw
        rows_z ident_ready consts_ready masks_ready cols_ps cols_ready pool_step dve_step act_step
        conv_ve conv_rstd conv_nrm conv_tp conv_T conv_ps s0_ve s0_ready x1_done
        ve_ready rstd_ready ln_nrm tp_ps nT_ready logits_ps lg_ready compared ln_ready sp_ready
        beats_ready a_ready cnat_z comb_ready combT_ps cT_ready combT_ready hid_ps silu_done gate_ps gated y_ps x2_done
        cxT_ps cxT_ready k_ps kf_ready k_split KR_ready KS_ready KS_ones v_ps VA_z VA_ready
        q_ps qf_ready q_split a_ps max_done mx_z mx_ready mT_ps mT_ready
        s_ps exp_done pv_done us_ready ut_ps an_ready anT_ps aT_ready o_ps bo_added x3_done
        ones_ready M_ready mid_stored M_sorted MR_ready G_ready wexpT_ps bf_ps bf_ready wup_ps wup_ready bup_ready
        hid1_ps gelu_done y1_ps bfin_sum bfin_added x4_done stored""".split()
        s = {n: sem(n) for n in names}
        ld_x = [sem("ld_x_first"), sem("ld_x_rest")]
        ld_xs = [sem("ld_xs_first"), sem("ld_xs_rest")]
        ld_Q = [[sem(f"ld_Q{u}{q}") for q in range(NG)] for u in range(2)]
        ld_M = [sem(f"ld_M{u}") for u in range(2)]

        block = ctx.enter_context(nc.Block())
        R_RB1, R_SB1, R_BQ, R_BK, R_BE, R_UB, R_RW = 0, 4, 5, 6, 7, 11, 15
        NR = R_RW + E
        UT_BANKS = (0, 1, 1, 0)
        UT_SLOTS = (9, 10, 12, 13)
        GATE_BANKS = (4, 5, 2, 3)
        BF_SLOTS = (9, 11, 14)

        def T_BANK(k):
            return 0 if k < 2 * B else 2 if k == 2 * B else 4 + k % 2

        @block.sync
        def _(sp_):
            dma = sp_.dma_start

            def load_shifted(b0, b1):
                bs = slice(b0, b1)
                for t in range(2):
                    dma(XS[:, bs, t, :], x[bs, TC + P * t:TC + P * t + P, :].rearrange("b p d -> p b d")).then_inc(ld_xs[b0 > 0], 16)
                dma(XS[:, bs, 2, :], x[bs, HALF + C:HALF + C + P, :].rearrange("b p d -> p b d")).then_inc(ld_xs[b0 > 0], 16)
                dma(XS[0:CUT3, bs, 3, :], x[bs, HALF + C + P:S, :].rearrange("b p d -> p b d")).then_inc(ld_xs[b0 > 0], 16)
                dma(XS[CUT3:P, bs, 3, :], ctx_in[bs, :, :].rearrange("b p d -> p b d")).then_inc(ld_xs[b0 > 0], 16)

            def load_stream(b0, b1):
                dma(X[:, b0:b1, :, :].rearrange("p b t d -> p (b t) d"),
                    x[b0:b1].rearrange("b (t p) d -> p (b t) d", p=P)).then_inc(ld_x[b0 > 0], 16)

            def row(name):
                return inp[name].rearrange("(a d) -> a d", a=1)

            for b in range(B):
                dma(xc[TC * b:TC * b + TC, :, :],
                    x[b, HALF:HALF + TC * RATE, :].rearrange("(j r) d -> j r d", r=RATE)).then_inc(s["ld_xc"], 16)
            load_shifted(0, 1)
            load_stream(0, 1)
            dma(convw[:, :, :], inp["L0_xattn_conv_w"].rearrange("r i o -> i r o")).then_inc(s["ld_conv"], 16)
            dma(convb[:, :], row("L0_xattn_conv_b")).then_inc(s["ld_conv"], 16)
            dma(cx[:, :, :], ctx_in.rearrange("b c d -> c b d")).then_inc(s["ld_cx"], 16)
            sp_.wait_ge(s["rows_z"], 1)
            for r, src in ((R_RW, inp["L0_ffn_routing_W"]), (R_RB1, inp["L0_ffn_rb1"].rearrange("(j e) h -> j (e h)", j=NJ)),
                           (R_BQ, row("L1_xattn_bq")), (R_BK, row("L1_xattn_bk")),
                           (R_BE, inp["L1_ffn_b_exp"].rearrange("(a d) -> a d", d=P)),
                           (R_UB, inp["L1_ffn_up_bias"].rearrange("(a d) -> a d", d=P))):
                dma(rows[r:r + src.shape[0], :], src).then_inc(s["ld_rows"], 16)
            dma(rows[R_SB1:R_SB1 + 1, 0:HE], row("L0_ffn_sb1")).then_inc(s["ld_rows"], 16)
            dma(ebias[:, :], row("L0_ffn_expert_bias").broadcast_to((P, E))).then_inc(s["ld_rows"], 16)
            dma(w1[:, 0:E * HE].rearrange("p (e h) -> p e h", e=E), inp["L0_ffn_rW1"].rearrange("e d h -> d e h")).then_inc(s["ld_w1"], 16)
            dma(w1[:, E * HE:], inp["L0_ffn_sW1"]).then_inc(s["ld_w1"], 16)
            dma(wk[:, :], inp["L1_xattn_Wk"]).then_inc(s["ld_wk"], 16)
            load_shifted(1, B)
            load_stream(1, B)
            dma(wv[:, :], inp["L1_xattn_Wv"]).then_inc(s["ld_wv"], 16)
            dma(bvb[:, :], row("L1_xattn_bv").broadcast_to((P, D))).then_inc(s["ld_wv"], 16)
            dma(w2[:, 0:NJ, :], inp["L0_ffn_rW2"].rearrange("e h d -> (e h) d").rearrange("(j p) d -> p j d", p=P)).then_inc(s["ld_w2"], 16)
            dma(w2[0:HE, NJ, :], inp["L0_ffn_sW2"]).then_inc(s["ld_w2"], 16)
            dma(w2[HE:HE + E, NJ, :], inp["L0_ffn_rb2"]).then_inc(s["ld_w2"], 16)
            dma(w2[HE + E:HE + E + 1, NJ, :], row("L0_ffn_sb2")).then_inc(s["ld_w2"], 16)
            W = [inp["L1_ffn_up_weights"], inp["L1_ffn_down_weights"]]
            for u in range(2):
                dma(bw_dram[u].rearrange("k n f -> n k f"),
                    W[u][3:6].rearrange("m (a k c) r s -> (m a) k (c r s)", a=8, k=4)).then_inc(s["bw_sorted"], 16)
            for t, n in ((wq, "Wq"), (wo, "Wo")):
                dma(t[:, :], inp["L1_xattn_" + n]).then_inc(s["ld_wa"], 16)
            for u in range(2):
                g64 = slice(64 * u, 64 * u + 64)
                dma(BW[g64, 0, :, :, :].rearrange("g (m k) r c -> g m (k r c)", m=3),
                    W[u][0:3].rearrange("m (g k) r c -> g m (k r c)", k=4)).then_inc(s["ld_bw"], 16)
                dma(BW[g64, 2, :, :, :].rearrange("g n r c -> g n (r c)"),
                    W[u][6:9].rearrange("m (k g) r c -> g (m k) (r c)", k=4)).then_inc(s["ld_bw"], 16)
            sp_.wait_ge(s["bw_sorted"], 32)
            for u in range(2):
                dma(BW[64 * u:64 * u + 64, 1, :, :, :].rearrange("g n r c -> g n (r c)"),
                    bw_dram[u].rearrange("k n f -> (k n f)").rearrange("(n g f) -> g n f", g=64, f=4)).then_inc(s["ld_bw"], 16)
            dma(wexp[:, :], inp["L1_ffn_W_exp"]).then_inc(s["ld_wexp"], 16)
            dma(V[:, 0, :, :], inp["L1_ffn_W_con"].rearrange("(t p) d -> p t d", p=P)).then_inc(s["ld_wcon"], 16)
            for t, n in ((bob, "L1_xattn_bo"), (bfin, "L1_ffn_b_con"), (bfin2, "L1_ffn_down_bias")):
                dma(t[:, :], row(n).broadcast_to((P, D))).then_inc(s["ld_bc"], 16)
            sp_.wait_ge(s["k_split"], 1)
            for gq in range(NG):
                r = slice(32 * gq, 32 * gq + 32)
                for at, src in ((0, kh), (32, kl), (64, kh)):
                    dma(KR[at:at + 32, gq, :].bitcast(F32), src[r, :].bitcast(F32)).then_inc(s["KR_ready"], 16)
            sp_.wait_ge(s["M_ready"], 1)
            dma(mid_dram.rearrange("i p j -> p i j"), Mo[:, 1, :, :]).then_inc(s["mid_stored"], 16)
            dma(mh_dram[0].rearrange("u (g i) j -> (u g) (i j)", i=8),
                Mo[:, 0, :, :].rearrange("p i j -> p (i j)")).then_inc(s["M_sorted"], 16)
            for u in range(2):
                dma(mh_dram[2, u].rearrange("(i g) j -> g i j", i=8), Mo[64 * u:64 * u + 64, 2, :, :]).then_inc(s["M_sorted"], 16)
            sp_.wait_ge(s["mid_stored"], 16)
            dma(mh_dram[1].rearrange("u (a i c) j -> (u a) i (c j)", a=8, i=8),
                mid_dram.rearrange("i (n c) j -> n i (c j)", c=8)).then_inc(s["M_sorted"], 16)
            sp_.wait_ge(s["M_sorted"], 16 * 4)
            for d in range(3):
                dma(MR[:, d, :, :, :].rearrange("p u t j -> p (u t) j"),
                    mh_dram[d].rearrange("u (t p) j -> p (u t) j", p=P)).then_inc(s["MR_ready"], 16)

            def stack_q(b, gq):
                u = b % 2
                sp_.wait_ge(s["q_split"], b + 1)
                if b >= 2:
                    sp_.wait_ge(s["exp_done"], HEADS * (b - 2) + HG * (gq + 1))
                r = slice(32 * gq, 32 * gq + 32)
                for at, src in ((0, qh), (32, qh), (64, ql)):
                    dma(QS[at:at + 32, u, gq, :].bitcast(F32), src[r, u, :].bitcast(F32)).then_inc(ld_Q[u][gq], 16)

            def stack_max(b):
                u = b % 2
                sp_.wait_ge(s["mT_ready"], b + 1)
                if b >= 2:
                    sp_.wait_ge(s["exp_done"], HEADS * (b - 1))
                for gq in range(NG):
                    dma(QS[96:128, u, gq, :].bitcast(F32), mT[32 * gq:32 * gq + 32, u, :].bitcast(F32)).then_inc(ld_M[u], 16)

            for gq in range(NG):
                stack_q(0, gq)
            for b in range(-1, B):
                if b + 2 < B:
                    stack_q(b + 2, 0)
                    stack_q(b + 2, 1)
                if b + 1 < B:
                    stack_max(b + 1)
                if b + 2 < B:
                    stack_q(b + 2, 2)
                    stack_q(b + 2, 3)
            for b in range(B):
                sp_.wait_ge(s["x4_done"], b + 1)
                dma(out[b].rearrange("(t p) d -> p t d", p=P), X[:, b, :, :]).then_inc(s["stored"], 16)
            sp_.wait_ge(s["stored"], 16 * B)

        @block.gpsimd
        def _(pool):
            gp = nc.gpsimd
            n = [0]

            def step(ins):
                n[0] += 1
                ins.then_inc(s["pool_step"], 1)
                pool.wait_ge(s["pool_step"], n[0])

            gp.memset(rows[:, :], 0.0).then_inc(s["rows_z"], 1)
            step(gp.memset(ident[:, :], 0.0))
            gp.affine_select(out=ident[:, :], in_=ident[:, :], compare_op=ALU.not_equal, fill=1.0, base=0,
                             pattern=[[-1, P]], channel_multiplier=1).then_inc(s["ident_ready"], 1)
            gp.memset(cpad[:, :, :, :], 0.0).then_inc(s["consts_ready"], 1)
            gp.memset(mhalf[:, :], -0.5)
            gp.memset(phalf[:, :], 0.5)
            gp.memset(raw[:, :], 0.0)
            step(gp.memset(keep[:, :], 1.0))
            gp.memset(keep[:, 1:2], 0.0)
            gp.memset(keep[:, 3:4], 0.0)
            step(gp.memset(raw[:, 3:4], 1.0))
            gp.memset(keep[0:CUT1, 1:2], 1.0)
            gp.memset(keep[0:CUT3, 3:4], 1.0)
            gp.memset(raw[0:CUT3, 3:4], 0.0)
            step(gp.memset(convm[:, :], 0.0))
            step(gp.memset(convm[:, CUT1:P], 1.0))

            def shift_scales(b):
                u = b % 2
                pool.wait_ge(s["s0_ve"], b + 1)
                if b >= 2:
                    pool.wait_ge(s["x1_done"], b - 1)
                gp.tensor_tensor(smean[:, u, :], smv[:, u, :, 0], keep[:, :], ALU.mult)
                step(gp.tensor_tensor(srs[:, u, :], sve[:, u, :], mhalf[:, :], ALU.pow))
                step(gp.tensor_tensor(srs[:, u, :], srs[:, u, :], keep[:, :], ALU.mult))
                gp.tensor_tensor(srs[:, u, :], srs[:, u, :], raw[:, :], ALU.add).then_inc(s["s0_ready"], 1)

            def rstd_of(k):
                pool.wait_ge(s["ve_ready"], k + 1)
                gp.tensor_tensor(rstd[:, k % 2, :], ve[:, k % 2, :], mhalf[:, :], ALU.pow).then_inc(s["rstd_ready"], 1)

            def count_beaten(b):
                pool.wait_ge(s["compared"], b + 1)
                step(gp.tensor_tensor(ties[:, :, :, :].rearrange("p t e f -> p t (e f)"),
                                      ties[:, :, :, :].rearrange("p t e f -> p t (e f)"),
                                      tri[:, :, :].rearrange("p e f -> p (e f)").unsqueeze(1).broadcast_to((P, NT, E * E)), ALU.mult))
                gp.tensor_tensor(beats[:, :, :, :].rearrange("p t e f -> p (t e f)"),
                                 beats[:, :, :, :].rearrange("p t e f -> p (t e f)"),
                                 ties[:, :, :, :].rearrange("p t e f -> p (t e f)"), ALU.add).then_inc(s["beats_ready"], 1)

            def roots_of(b):
                pool.wait_ge(s["sp_ready"], b + 1)
                gp.tensor_tensor(roots[:, :, :], top[:, :, 0:2], phalf[:, :, :], ALU.pow).then_inc(s["a_ready"], 1)

            pool.wait_ge(s["conv_ve"], 1)
            gp.tensor_tensor(crs[:, :], cve[:, :], mhalf[0:B * TC, :], ALU.pow).then_inc(s["conv_rstd"], 1)
            shift_scales(0)
            step(gp.memset(tri[:, :, :], 1.0))
            gp.affine_select(out=tri[:, :, :], in_=tri[:, :, :], compare_op=ALU.is_gt, fill=0.0, base=0,
                             pattern=[[1, E], [-1, E]], channel_multiplier=0)
            step(gp.memset(cnat[:, :, :], 0.0))
            gp.memset(cnat[:, :, HE + E:HE + E + 1], 1.0).then_inc(s["cnat_z"], 1)
            step(gp.memset(VA[:, :, :, :], 0.0))
            gp.memset(VA[:, :, :, HD:HD + 1], 1.0).then_inc(s["VA_z"], 1)
            rstd_of(0)
            shift_scales(1)

            def block_stage(m):
                if m == 0:
                    pool.wait_ge(s["ld_bw"], 16 * 6)
                lo = 2 ** m
                hi = 4 // lo
                src, dst = m % 2, 1 - m % 2
                for d in range(3):
                    Mi = M[:, src, d, :, :].rearrange("p i (h c l) -> p i h c l", c=2, l=lo)
                    Wm = BW[:, d, m::3, :, :] if d == 1 else BW[:, d, 4 * m:4 * m + 4, :, :]
                    for r in range(2):
                        for c, t_ in ((0, pa), (1, pb)):
                            w_ = Wm[:, :, r, c].rearrange("p (h l) -> p h l", l=lo).unsqueeze(1).broadcast_to((P, 8, hi, lo))
                            o_ = t_[:, r, d, :].rearrange("p (i h l) -> p i h l", i=8, l=lo)
                            last = gp.tensor_tensor(o_, Mi[:, :, :, c, :], w_, ALU.mult)
                step(last)
                for d in range(3):
                    Mn = M[:, dst, d, :, :].rearrange("p i (h c l) -> p i h c l", c=2, l=lo)
                    for r in range(2):
                        a_ = pa[:, r, d, :].rearrange("p (i h l) -> p i h l", i=8, l=lo)
                        b_ = pb[:, r, d, :].rearrange("p (i h l) -> p i h l", i=8, l=lo)
                        last = gp.tensor_tensor(Mn[:, :, :, r, :], a_, b_, ALU.add)
                step(last)

            def blocks_out():
                step(gp.tensor_copy(Mo[0:64, :, :, :].rearrange("p d i j -> p (d i j)"), M[0:64, 1, :, :, :].rearrange("p d i j -> p (d i j)")))
                for d in range(3):
                    last = gp.tensor_copy(Mo[64:128, d, :, :], M[64:128, 1, d, :, :].rearrange("p i j -> p j i"))
                last.then_inc(s["M_ready"], 1)
                pool.wait_ge(s["M_ready"], 1)

            def head_keys(gqs):
                pool.wait_ge(s["KR_ready"], 16 * 3 * NG)
                pool.wait_ge(s["masks_ready"], 1)
                for gq in gqs:
                    for b in range(B):
                        gp.tensor_tensor(KS[0:96, gq, b, :, :],
                                         KR[:, gq, C * b:C * b + C].bitcast(F32).unsqueeze(1).broadcast_to((96, HG, C)),
                                         hm[:, :].unsqueeze(2).broadcast_to((96, HG, C)), ALU.mult).then_inc(s["KS_ready"], 1)

            def digit_matrix(u, d):
                for t in range(NH):
                    if d == 0:
                        last = gp.tensor_tensor(G0[:, u, t, :].rearrange("p (k j) -> p k j", j=8),
                                                MR[:, 0, u, t, :].unsqueeze(1).broadcast_to((P, 16, 8)),
                                                mk0[:, :].unsqueeze(2).broadcast_to((P, 16, 8)), ALU.mult)
                    elif d == 1:
                        for b6 in range(2):
                            last = gp.tensor_tensor(G1[:, u, t, 64 * b6:64 * b6 + 64].rearrange("p (j k) -> p j k", k=8),
                                                    MR[:, 1, u, t, :].unsqueeze(2).broadcast_to((P, 8, 8)),
                                                    mk1[:, b6, :].unsqueeze(1).broadcast_to((P, 8, 8)), ALU.mult)
                    else:
                        last = gp.tensor_tensor(G2[:, u, t, :, :].rearrange("p v (c k) -> p (v c) k", k=64),
                                                MR[:, 2, u, t, :].unsqueeze(2).broadcast_to((P, 8, 64)),
                                                mk2[:, :].unsqueeze(1).broadcast_to((P, 8, 64)), ALU.mult)
                last.then_inc(s["G_ready"], 1)

            def add_row(b, k, row_, done):
                pool.wait_ge(s["ln_nrm"], k)
                gp.tensor_tensor(X[:, b, :, :], X[:, b, :, :], row_[:, :].unsqueeze(1).broadcast_to((P, NT, D)),
                                 ALU.add).then_inc(s[done], 1)

            for b in range(B):
                count_beaten(b)
                roots_of(b)
                rstd_of(b + 1)
                if b == 0:
                    step(gp.memset(M[:, 0, 0, :, :], 0.0))
                    step(gp.affine_select(out=M[:, 0, 0, :, :], in_=M[:, 0, 0, :, :], compare_op=ALU.not_equal, fill=1.0,
                                          base=0, pattern=[[1, 8], [-1, 8]], channel_multiplier=0))
                    gp.tensor_copy(M[:, 0, 1, :, :], M[:, 0, 0, :, :])
                    step(gp.tensor_copy(M[:, 0, 2, :, :], M[:, 0, 0, :, :]))
                    block_stage(0)
                if b == 1:
                    block_stage(1)
                    step(gp.memset(ones_p[96:128, :, :], 0.0))
                    for at in (0, HG):
                        last = gp.affine_select(out=ones_p[96:128, :, :], in_=ones_p[96:128, :, :], compare_op=ALU.not_equal,
                                                fill=1.0, base=-at, pattern=[[-1, HG], [0, C]], channel_multiplier=1)
                        if at == 0:
                            step(last)
                    last.then_inc(s["ones_ready"], 1)
                    pool.wait_ge(s["ones_ready"], 1)
                if b + 2 < B:
                    shift_scales(b + 2)
                if b == 2:
                    block_stage(2)
                    blocks_out()
                    head_keys((0,))
                    gp.memset(mx[:, :, :, :].bitcast(F32), 0.0).then_inc(s["mx_z"], 1)
            head_keys((1, 2, 3))
            pool.wait_ge(s["MR_ready"], 16 * 3)
            digit_matrix(0, 0)
            rstd_of(B + 1)
            pool.wait_ge(s["y_ps"], B)
            digit_matrix(1, 2)
            digit_matrix(0, 1)
            digit_matrix(1, 1)
            pool.wait_ge(s["ld_bc"], 48)
            add_row(0, B + 1, bob, "bo_added")
            digit_matrix(0, 2)
            digit_matrix(1, 0)
            add_row(1, B + 2, bob, "bo_added")
            gp.tensor_tensor(bfin[:, :], bfin[:, :], bfin2[:, :], ALU.add).then_inc(s["bfin_sum"], 1)
            for b in range(2, B):
                rstd_of(B + b)
                add_row(b, B + b + 1, bob, "bo_added")
            pool.wait_ge(s["bfin_sum"], 1)
            for b in range(B):
                rstd_of(2 * B + b)
                add_row(b, 2 * B + b + 1, bfin, "bfin_added")

        @block.scalar
        def _(act_):
            sc = nc.scalar
            n = [0]

            def step(ins):
                n[0] += 1
                ins.then_inc(s["act_step"], 1)
                act_.wait_ge(s["act_step"], n[0])

            def copy_nT(k):
                act_.wait_ge(s["tp_ps"], k + 1)
                sc.copy(nT[:, k % 2, :], bank[T_BANK(k)][:, :]).then_inc(s["nT_ready"], 1)

            def copy_q(b):
                act_.wait_ge(s["q_ps"], b + 1)
                if b >= 1:
                    act_.wait_ge(s["q_split"], b)
                sc.activation(qf[:, :], bank[min(b, 1)][:, :], ACT.Identity, bias=cols[:, R_BQ:R_BQ + 1]).then_inc(s["qf_ready"], 1)

            sc.preload_act_table_set("natural_log_exp_and_others")
            act_.wait_ge(s["conv_tp"], 1)
            act_.wait_ge(s["consts_ready"], 1)
            sc.copy(cpad[:, :, :, CUT1:P].rearrange("p b r j -> p r b j"),
                    bank[5][:, 0:RATE * B * TC].rearrange("p (r b j) -> p r b j", r=RATE, b=B)).then_inc(s["conv_T"], 1)
            act_.wait_ge(s["cols_ps"], 1)
            sc.copy(cols[:, 0:NR], bank[7][:, 0:NR]).then_inc(s["cols_ready"], 1)
            act_.wait_ge(s["cxT_ps"], 1)
            sc.copy(cxT[:, :], bank[5][:, 0:B * C]).then_inc(s["cxT_ready"], 1)
            copy_nT(0)
            for b in range(B):
                if b:
                    sc.preload_act_table_set("natural_log_exp_and_others")
                act_.wait_ge(s["lg_ready"], b + 1)
                step(sc.activation(el[:, :, :], nlg[:, :, :], ACT.Exp))
                sc.activation(rt[:, :, :], el[:, :, :], ACT.Ln, bias=1.0).then_inc(s["ln_ready"], 1)
                for j in range(NJ + 1):
                    if b == 0 and j == 2:
                        act_.wait_ge(s["k_ps"], 1)
                        sc.activation(kf[:, :], bank[7][:, 0:B * C], ACT.Identity, bias=cols[:, R_BK:R_BK + 1]).then_inc(s["kf_ready"], 1)
                    if b and j == NJ:
                        copy_nT(b + 1)
                    act_.wait_ge(s["hid_ps"], (NJ + 1) * b + j + 1)
                    hb = bank[2 + ((NJ + 1) * b + j) % 2]
                    if j < NJ:
                        if b >= 1:
                            act_.wait_ge(s["gated"], NJ * (2 * b - 1) + j + 1)
                        sc.activation(sil[:, j, :], hb[:, :], ACT.Silu,
                                      bias=cols[:, R_RB1 + j:R_RB1 + j + 1]).then_inc(s["silu_done"], 1)
                    else:
                        if b >= 2:
                            act_.wait_ge(s["y_ps"], b - 1)
                        sc.activation(g[0:HE, b % 2, NJ, :], hb[0:HE, :], ACT.Silu,
                                      bias=cols[0:HE, R_SB1:R_SB1 + 1]).then_inc(s["silu_done"], 1)
                act_.wait_ge(s["combT_ps"], b + 1)
                sc.copy(cT24[:, :], bank[6][0:NB * E, 0:S // 2].bitcast(BF16)).then_inc(s["cT_ready"], 1)
                sc.copy(g[HE:HE + E + 1, b % 2, NJ, :], bank[1][HE:HE + E + 1, :]).then_inc(s["combT_ready"], 1)
                if b == 0:
                    copy_nT(b + 1)
                if b >= 2:
                    if b == B - 1:
                        copy_q(0)
                    act_.wait_ge(s["ones_ready"], 1)
                    for gq in (2 * b - 4, 2 * b - 3):
                        last = sc.copy(KS[96:128, gq, :, :, :].rearrange("p b i c -> p b (i c)"),
                                       ones_p[96:128, :, :].rearrange("p i c -> p (i c)").unsqueeze(1).broadcast_to((32, B, HG * C)))
                    last.then_inc(s["KS_ones"], 1)
            act_.wait_ge(s["wexpT_ps"], 1)
            sc.copy(U[:, 0, :, 0:D], bank[7][:, :].rearrange("p (t d) -> p t d", t=NH))
            sc.copy(U[:, 0, :, D:D + 2], cols[:, R_BE:R_BE + NH].unsqueeze(2).broadcast_to((P, NH, 2))).then_inc(s["bf_ready"], 1)

            def copy_butterfly(c):
                k, part = divmod(c, 3)
                act_.wait_ge(s["bf_ps"], c + 1)
                if part < 2:
                    sc.copy(U[:, (k + 1) % 2, 2 * part:2 * part + 2, :],
                            bank[2 + part][:, 0:2 * (D + 2)].rearrange("p (t d) -> p t d", t=2)).then_inc(s["bf_ready"], 1)
                else:
                    sc.copy(V[:, (k + 1) % 2, :, :], bank[2][:, :].rearrange("p (t d) -> p t d", t=NH)).then_inc(s["bf_ready"], 1)

            def weights_of(h):
                act_.wait_ge(s["s_ps"], h + 1)
                if h >= 4:
                    act_.wait_ge(s["pv_done"], h - 3)
                sc.activation(pe_[:, h % 4, :], bank[4 + h % 2][0:C, :], ACT.Exp, scale=SCALE).then_inc(s["exp_done"], 1)

            def copy_values(q):
                act_.wait_ge(s["pv_done"], HG * (q + 1))
                if q >= 2 * NG:
                    act_.wait_ge(s["ut_ps"], NT * (q // NG - 1))
                sc.copy(US[:, q // NG % 2, q % NG, :], bank[6 + q % 2][:, :]).then_inc(s["us_ready"], 1)

            for b in range(-1, B):
                for i in range(HEADS):
                    if b >= 0:
                        h = HEADS * b + i
                        weights_of(h)
                        if h >= HG and h % HG == 1:
                            copy_values(h // HG - 1)
                    if i == 1 and b + 2 < B:
                        copy_nT(B + b + 2)
                    if i == 3 and b + 2 < B:
                        copy_q(b + 2)
                    if i == 8 and b + 1 < B:
                        act_.wait_ge(s["mT_ps"], b + 2)
                        if b >= 1:
                            act_.wait_ge(ld_M[(b + 1) % 2], 16 * NG * ((b + 1) // 2))
                        sc.copy(mT[:, (b + 1) % 2, :], bank[0][:, :]).then_inc(s["mT_ready"], 1)
                    if b <= 1 and i in BF_SLOTS:
                        copy_butterfly(3 * (b + 1) + BF_SLOTS.index(i))
                    if b == 2 and i == 9:
                        act_.wait_ge(s["wup_ps"], 1)
                        sc.copy(wup[:, :], bank[2][:, :]).then_inc(s["wup_ready"], 1)
                    if i == 8 and b == B - 1:
                        copy_nT(2 * B)
                    if i == 15 and b >= 1:
                        act_.wait_ge(s["anT_ps"], b)
                        sc.copy(aT[:, (b - 1) % 2, :], bank[0][:, :]).then_inc(s["aT_ready"], 1)
            copy_values(NG * B - 1)

            def gelu(k):
                act_.wait_ge(s["hid1_ps"], k + 1)
                if k == 0:
                    act_.wait_ge(s["bup_ready"], 1)
                b, j = divmod(k, NH)
                if b >= 2:
                    act_.wait_ge(s["y1_ps"], b - 1)
                sc.activation(ge[:, b % 2, j, :], bank[2 + k % 2][:, :], ACT.Gelu, bias=bup[:, j:j + 1]).then_inc(s["gelu_done"], 1)

            for j in range(NH):
                gelu(j)
            act_.wait_ge(s["anT_ps"], B)
            sc.copy(aT[:, (B - 1) % 2, :], bank[0][:, :]).then_inc(s["aT_ready"], 1)
            for b in range(1, B):
                copy_nT(2 * B + b)
                for j in range(NH):
                    gelu(NH * b + j)

        @block.vector
        def _(dve):
            v = nc.vector
            n = [0]

            def step(ins):
                n[0] += 1
                ins.then_inc(s["dve_step"], 1)
                dve.wait_ge(s["dve_step"], n[0])

            def moments(src, st, mv_, ve_, ready):
                for t in range(NT):
                    last = v.bn_stats(st[:, t, :], src(t))
                step(last)
                for t in range(NT):
                    last = v.bn_aggr(mv_[:, t, :], st[:, t, :])
                step(last)
                v.tensor_scalar(ve_, mv_[:, :, 1], EPS, None, ALU.add).then_inc(s[ready], 1)

            def shift_moments(b):
                dve.wait_ge(ld_xs[b > 0], 80)
                if b >= 2:
                    dve.wait_ge(s["x1_done"], b - 1)
                moments(lambda t: XS[:, b, t, :], stat[:, :, :], smv[:, b % 2, :, :], sve[:, b % 2, :], "s0_ve")

            def shift_add(b):
                u = b % 2
                dve.wait_ge(s["s0_ready"], b + 1)
                for t in range(NT):
                    last = v.tensor_scalar(XS[:, b, t, :], XS[:, b, t, :], smean[:, u, t:t + 1], srs[:, u, t:t + 1], ALU.subtract, ALU.mult)
                step(last)
                dve.wait_ge(ld_x[b > 0], 16)
                step(v.tensor_tensor(X[:, b, :, :], X[:, b, :, :], XS[:, b, :, :], ALU.add))
                if b == 0:
                    dve.wait_ge(s["conv_ps"], 1)
                    v.tensor_tensor(X[:, 0, 1, :], X[:, 0, 1, :], bank[4][:, 0:D], ALU.add).then_inc(s["x1_done"], 1)
                else:
                    v.tensor_tensor(X[:, b, 1, :], X[:, b, 1, :], comp[:, b, :], ALU.add).then_inc(s["x1_done"], 1)
                dve.wait_ge(s["x1_done"], b + 1)

            def stream_moments(b, k):
                moments(lambda t: X[:, b, t, :], stat[:, :, :], mv[:, k % 2, :, :], ve[:, k % 2, :], "ve_ready")

            def scale_rows(b, k):
                u = k % 2
                dve.wait_ge(s["rstd_ready"], k + 1)
                if k >= 2:
                    dve.wait_ge(s["tp_ps"], k - 1)
                for t in range(NT):
                    last = v.tensor_scalar(nrm[:, u, t, :], X[:, b, t, :], mv[:, u, t, 0:1], rstd[:, u, t:t + 1], ALU.subtract, ALU.mult)
                last.then_inc(s["ln_nrm"], 1)

            def normalise(b, k):
                stream_moments(b, k)
                scale_rows(b, k)

            def logits(b):
                dve.wait_ge(s["logits_ps"], b + 1)
                if b == 0:
                    dve.wait_ge(s["ld_rows"], 16 * 8)
                else:
                    dve.wait_ge(s["beats_ready"], b)
                step(v.tensor_tensor(lg[:, :, :], bank[0][:, 0:NT * E].rearrange("p (t e) -> p t e", e=E),
                                     ebias[:, :].unsqueeze(1).broadcast_to((P, NT, E)), ALU.add))
                v.scalar_tensor_tensor(out=nlg[:, :, :], in0=lg[:, :, :], scalar=-1.0, in1=lg[:, :, :],
                                       op0=ALU.mult, op1=ALU.min).then_inc(s["lg_ready"], 1)
                other = lg[:, :, :].unsqueeze(2).broadcast_to((P, NT, E, E))
                own = lg[:, :, :].unsqueeze(3).broadcast_to((P, NT, E, E))
                v.tensor_tensor(beats[:, :, :, :], other, own, ALU.is_gt)
                v.tensor_tensor(ties[:, :, :, :], other, own, ALU.is_equal).then_inc(s["compared"], 1)

            def softplus(b):
                dve.wait_ge(s["ln_ready"], b + 1)
                v.scalar_tensor_tensor(out=sp[:, :, :], in0=lg[:, :, :], scalar=0.0, in1=rt[:, :, :],
                                       op0=ALU.max, op1=ALU.add)
                step(v.tensor_scalar(res[:, 0, :, :], el[:, :, :], 1.0, -1.0, ALU.add, ALU.add))
                step(v.tensor_tensor(res[:, 1, :, :], el[:, :, :], res[:, 0, :, :], ALU.subtract))
                step(v.tensor_tensor(sp[:, :, :], sp[:, :, :], res[:, 1, :, :], ALU.add))
                if b >= 1:
                    dve.wait_ge(s["a_ready"], b)
                for t in range(NT):
                    last = v.max(top[:, t, :], sp[:, t, :])
                last.then_inc(s["sp_ready"], 1)

            def combine(b):
                dve.wait_ge(s["beats_ready"], b + 1)
                step(v.tensor_reduce(rank[:, :, :], beats[:, :, :, :], axis=AX.X, op=ALU.add))
                dve.wait_ge(s["a_ready"], b + 1)
                if b == 0:
                    dve.wait_ge(s["cnat_z"], 1)
                else:
                    dve.wait_ge(s["combT_ps"], b)
                comb = cnat[:, :, HE:HE + E]
                for r in range(2):
                    last = v.scalar_tensor_tensor(out=res[:, r, :, :], in0=rank[:, :, :], scalar=float(r),
                                                  in1=roots[:, :, r:r + 1].broadcast_to((P, NT, E)), op0=ALU.is_equal, op1=ALU.mult)
                step(last)
                step(v.tensor_tensor(comb, res[:, 0, :, :], res[:, 1, :, :], ALU.add))
                step(v.tensor_copy(c24[:, :, 0, :], comb))
                step(v.tensor_tensor(res[:, 0, :, :], comb, c24[:, :, 0, :], ALU.subtract))
                step(v.tensor_copy(c24[:, :, 1, :], res[:, 0, :, :]))
                v.tensor_tensor(c24[:, :, 2, :], res[:, 0, :, :], c24[:, :, 1, :], ALU.subtract).then_inc(s["comb_ready"], 1)

            def split_q(b):
                u = b % 2
                dve.wait_ge(s["qf_ready"], b + 1)
                if b >= 2:
                    for gq in range(NG):
                        dve.wait_ge(ld_Q[u][gq], 48 * (b // 2))
                step(v.tensor_copy(qh[:, u, :], qf[:, :]))
                v.tensor_tensor(ql[:, u, :], qf[:, :], qh[:, u, :].bitcast(F32), ALU.subtract).then_inc(s["q_split"], 1)

            def gate(b, half):
                for j in range(NJ):
                    if half == 0:
                        dve.wait_ge(s["gate_ps"], NJ * b + j + 1)
                        dve.wait_ge(s["silu_done"], (NJ + 1) * b + j + 1)
                        if b >= 2:
                            dve.wait_ge(s["y_ps"], b - 1)
                    c = slice(HALF * half, HALF * half + HALF)
                    v.tensor_tensor(g[:, b % 2, j, c], sil[:, j, c], bank[GATE_BANKS[j]][:, c], ALU.mult).then_inc(s["gated"], 1)

            def add_to_stream(b, src, done):
                v.tensor_tensor(X[:, b, :, :].rearrange("p t d -> p (t d)"), X[:, b, :, :].rearrange("p t d -> p (t d)"),
                                src[:, :], ALU.add).then_inc(s[done], 1)

            def add_y(b):
                dve.wait_ge(s["y_ps"], b + 1)
                add_to_stream(b, bank[6], "x2_done")

            dve.wait_ge(s["ident_ready"], 1)
            v.tensor_copy(identb[:, :], ident[:, :])
            v.tensor_reduce(mk0[:, :], ident[:, :].rearrange("p (k j) -> p k j", j=8), axis=AX.X, op=ALU.add)
            v.tensor_reduce(mk1[:, :, :], ident[:, :].rearrange("p (b j k) -> p b k j", b=2, k=8), axis=AX.X, op=ALU.add)
            v.tensor_tensor(mk2[:, :], ident[:, 0:64], ident[:, 64:128], ALU.add)
            v.tensor_reduce(hm[:, :], ident[0:96, :].rearrange("p (b i d) -> p i b d", b=NG, d=HD), axis=AX.XY, op=ALU.add)
            step(v.tensor_reduce(sel8[:, :], ident[0:NB * E, 0:NB * E].rearrange("p (s e) -> p e s", s=NB), axis=AX.X, op=ALU.add))
            v.tensor_copy(sel[:, :, :], sel8[:, :].unsqueeze(2).broadcast_to((NB * E, E, HE))).then_inc(s["masks_ready"], 1)
            dve.wait_ge(s["ld_xc"], 16 * B)
            moments(lambda r: xc[:, r, :], cstat[:, :, :], cmv[:, :, :], cve[:, :], "conv_ve")
            shift_moments(0)
            dve.wait_ge(s["conv_rstd"], 1)
            for r in range(RATE):
                last = v.tensor_scalar(xcn[:, r, :], xc[:, r, :], cmv[:, r, 0:1], crs[:, r:r + 1], ALU.subtract, ALU.mult)
            last.then_inc(s["conv_nrm"], 1)
            shift_add(0)
            normalise(0, 0)
            shift_moments(1)
            dve.wait_ge(s["conv_ps"], B)
            step(v.tensor_copy(comp[:, 1:B, :].rearrange("p b d -> p (b d)"), bank[6][:, D:B * D]))
            for b in range(B):
                logits(b)
                softplus(b)
                if b + 1 < B:
                    shift_add(b + 1)
                else:
                    dve.wait_ge(s["x2_done"], 1)
                stream_moments((b + 1) % B, b + 1)
                if b >= 1:
                    scale_rows((b + 1) % B, b + 1)
                    add_y(b - 1)
                combine(b)
                if b == 0:
                    scale_rows(b + 1, b + 1)
                if b == 0:
                    dve.wait_ge(s["v_ps"], 1)
                    dve.wait_ge(s["ld_wv"], 32)
                    dve.wait_ge(s["VA_z"], 1)
                    for b_ in range(B):
                        last = v.tensor_tensor(VA[:, b_, :, 0:HD], bank[5][0:C, D * b_:D * b_ + D].rearrange("p (h d) -> p h d", d=HD),
                                               bvb[0:C, :].rearrange("p (h d) -> p h d", d=HD), ALU.add)
                    last.then_inc(s["VA_ready"], 1)
                if 1 <= b < B - 2:
                    shift_moments(b + 2)
                gate(b, 0)
                if b == B - 1:
                    split_q(0)
                gate(b, 1)
                if b == 0:
                    shift_moments(b + 2)
                if b == 0:
                    dve.wait_ge(s["kf_ready"], 1)
                    step(v.tensor_copy(kh[:, :], kf[:, :]))
                    v.tensor_tensor(kl[:, :], kf[:, :], kh[:, :].bitcast(F32), ALU.subtract).then_inc(s["k_split"], 1)

            def maximum(b, k):
                gq, t = divmod(k, NT)
                k = NT * NG * b + k
                dve.wait_ge(s["a_ps"], k + 1)
                v.tensor_reduce(nm[:, t, HG * gq:HG * gq + HG], bank[2 + k % 2][:, 0:HG * C].rearrange("p (i c) -> p i c", i=HG),
                                axis=AX.X, op=ALU.max, negate=True).then_inc(s["max_done"], 1)

            def split_max(b):
                dve.wait_ge(s["max_done"], NT * NG * (b + 1))
                if b == 0:
                    dve.wait_ge(s["mx_z"], 1)
                else:
                    dve.wait_ge(s["mT_ps"], b)
                nm_ = nm[:, :, :].rearrange("p t (q i) -> p t q i", i=HG)
                step(v.tensor_copy(mx[:, :, :, 0:HG], nm_))
                v.tensor_tensor(mx[:, :, :, HG:2 * HG], nm_, mx[:, :, :, 0:HG].bitcast(F32), ALU.subtract).then_inc(s["mx_ready"], 1)

            def divide(b, t):
                dve.wait_ge(s["ut_ps"], NT * b + t + 1)
                if b >= 1:
                    dve.wait_ge(s["anT_ps"], b)
                pt = bank[UT_BANKS[t]][:, :].rearrange("p (h c) -> p h c", c=32)
                step(v.reciprocal(rec[:, t % 2, :], pt[:, :, HD]))
                v.tensor_tensor(an[:, t, :].rearrange("p (h d) -> p h d", d=HD), pt[:, :, 0:HD],
                                rec[:, t % 2, :].unsqueeze(2).broadcast_to((P, HEADS, HD)), ALU.mult).then_inc(s["an_ready"], 1)

            def add_o(b):
                dve.wait_ge(s["o_ps"], b + 1)
                dve.wait_ge(s["bo_added"], b + 1)
                add_to_stream(b, bank[1], "x3_done")

            dve.wait_ge(s["x2_done"], 2)
            normalise(1, B + 1)
            add_y(B - 1)
            for b in range(-1, B):
                for i in range(8):
                    if b + 1 < B:
                        maximum(b + 1, 2 * i)
                        maximum(b + 1, 2 * i + 1)
                    if i == 2 and b >= 2:
                        add_o(b - 2)
                    if i == 5 and b + 2 < B:
                        split_q(b + 2)
                if b + 1 < B:
                    split_max(b + 1)
                if b == B - 1:
                    for b_ in range(2):
                        dve.wait_ge(s["x3_done"], b_ + 1)
                        normalise(b_, 2 * B + b_)
                if b >= 1:
                    divide(b - 1, 0)
                    divide(b - 1, 1)
                if b == 2:
                    dve.wait_ge(s["bf_ready"], 1 + 8)
                    v.tensor_tensor(bup[:, :], U[:, 1, :, D], cols[:, R_UB:R_UB + NH], ALU.add).then_inc(s["bup_ready"], 1)
                if b + 3 < B:
                    dve.wait_ge(s["x2_done"], b + 4)
                    normalise(b + 3, B + b + 3)
                if b >= 1:
                    divide(b - 1, 2)
                    divide(b - 1, 3)
            add_o(B - 2)
            for t in range(NT):
                divide(B - 1, t)
            add_o(B - 1)
            for b in range(B):
                if b + 2 < B:
                    dve.wait_ge(s["x3_done"], b + 3)
                    normalise(b + 2, 2 * B + b + 2)
                dve.wait_ge(s["y1_ps"], b + 1)
                dve.wait_ge(s["bfin_added"], b + 1)
                add_to_stream(b, bank[6 + b % 2], "x4_done")

        @block.tensor
        def _(pe):
            mm, tp = nc.tensor.matmul, nc.tensor.transpose
            def compress(b):
                cb = bank[6 if b else 4]
                for r in range(RATE):
                    mm(cb[:, P * b:P * b + P], cpad[:, b, r, :], convw[:, r, :], start=(r == 0), stop=False)
                mm(cb[:, P * b:P * b + P], convm[:, :], convb[:, :], start=False, stop=True).then_inc(s["conv_ps"], 1)

            pe.wait_ge(s["ident_ready"], 1)
            pe.wait_ge(s["conv_nrm"], 1)
            for r in range(RATE):
                last = tp(bank[5][:, r * B * TC:(r + 1) * B * TC], xcn[:, r, :], ident[0:B * TC, 0:B * TC])
            last.then_inc(s["conv_tp"], 1)
            pe.wait_ge(s["ld_conv"], 32)
            pe.wait_ge(s["conv_T"], 1)
            compress(0)
            pe.wait_ge(s["ld_rows"], 16 * 8)
            tp(bank[7][:, 0:NR], rows[0:NR, :], ident[0:NR, 0:NR]).then_inc(s["cols_ps"], 1)
            pe.wait_ge(s["ld_cx"], 16)
            for b_ in range(B):
                last = tp(bank[5][:, C * b_:C * b_ + C], cx[:, b_, :], ident[0:C, 0:C])
            last.then_inc(s["cxT_ps"], 1)
            compress(1)
            compress(2)

            def transposed_rows(k):
                pe.wait_ge(s["ln_nrm"], k + 1)
                for t in range(NT):
                    last = tp(bank[T_BANK(k)][:, P * t:P * t + P], nrm[:, k % 2, t, :], ident[:, :])
                last.then_inc(s["tp_ps"], 1)

            def route(b):
                pe.wait_ge(s["nT_ready"], b + 1)
                if b == 0:
                    pe.wait_ge(s["cols_ready"], 1)
                for t in range(NT):
                    last = mm(bank[0][:, E * t:E * t + E], nT[:, b % 2, P * t:P * t + P], cols[:, R_RW:R_RW + E], start=True, stop=True)
                last.then_inc(s["logits_ps"], 1)

            def query(b):
                pe.wait_ge(s["nT_ready"], B + b + 1)
                if b == 0:
                    pe.wait_ge(s["ld_wa"], 32)
                mm(bank[min(b, 1)][:, :], wq[:, :], nT[:, (B + b) % 2, :], start=True, stop=True).then_inc(s["q_ps"], 1)

            transposed_rows(0)
            compress(3)
            route(0)
            for b in range(B):
                u = b % 2
                if b == 0:
                    pe.wait_ge(s["ld_w1"], 32)
                for j in range(NJ + 1):
                    if b == 0 and j == 2:
                        pe.wait_ge(s["ld_wk"], 16)
                        pe.wait_ge(s["cxT_ready"], 1)
                        mm(bank[7][:, 0:B * C], wk[:, :], cxT[:, :], start=True, stop=True).then_inc(s["k_ps"], 1)
                    if b == 0 and j == NJ:
                        pe.wait_ge(s["ld_wv"], 32)
                        for b_ in range(B):
                            last = mm(bank[5][0:C, D * b_:D * b_ + D], cxT[:, C * b_:C * b_ + C], wv[:, :], start=True, stop=True)
                        last.then_inc(s["v_ps"], 1)
                    if b and j == NJ:
                        pe.wait_ge(s["compared"], b + 1)
                        transposed_rows(b + 1)
                    k = (NJ + 1) * b + j
                    m = P if j < NJ else HE
                    if j >= 2:
                        pe.wait_ge(s["silu_done"], k - 1)
                    mm(bank[2 + k % 2][0:m, :], w1[:, P * j:P * j + m], nT[:, u, :], start=True, stop=True).then_inc(s["hid_ps"], 1)
                pe.wait_ge(s["comb_ready"], b + 1)
                if b == 0:
                    pe.wait_ge(s["masks_ready"], 1)
                    pe.wait_ge(s["x1_done"], 2)
                else:
                    pe.wait_ge(s["x2_done"], b)
                for t in range(NT):
                    tp(bank[1][0:CW, P * t:P * t + P], cnat[:, t, :], ident[:, :])
                    last = tp(bank[6][0:NB * E, P // 2 * t:P // 2 * t + P // 2].bitcast(BF16), c24[:, t, :, :].rearrange("p s e -> p (s e)"), identb[:, :])
                last.then_inc(s["combT_ps"], 1)
                if 1 <= b < B - 1:
                    route(b + 1)
                elif b:
                    query(0)
                pe.wait_ge(s["cT_ready"], b + 1)
                if b == 0:
                    pe.wait_ge(s["VA_ready"], 1)
                for j in range(NJ):
                    if j >= 2:
                        pe.wait_ge(s["silu_done"], (NJ + 1) * (b + 1))
                    mm(bank[GATE_BANKS[j]][:, :], sel[:, 2 * j:2 * j + 2, :].rearrange("p e h -> p (e h)"), cT24[:, :],
                       start=True, stop=True).then_inc(s["gate_ps"], 1)
                if b == 1:
                    pe.wait_ge(s["ld_wexp"], 16)
                    pe.wait_ge(s["kf_ready"], 1)
                    for t in range(NH):
                        last = tp(bank[7][:, P * t:P * t + P], wexp[:, P * t:P * t + P], ident[:, :])
                    last.then_inc(s["wexpT_ps"], 1)
                if b == 0:
                    pe.wait_ge(s["ld_w2"], 64)
                if b == 0:
                    pe.wait_ge(s["compared"], b + 1)
                    transposed_rows(b + 1)
                    route(b + 1)
                pe.wait_ge(s["combT_ready"], b + 1)
                for t in range(NT):
                    for j in [NJ] + list(range(NJ)):
                        kk = P if j < NJ else HE + E + 1
                        if t % 2 == 0 and j < NJ:
                            pe.wait_ge(s["gated"], NJ * (2 * b + t // 2) + j + 1)
                        last = mm(bank[6][:, P * t:P * t + P], g[0:kk, u, j, P * t:P * t + P], w2[0:kk, j, :],
                                  start=(j == NJ), stop=(j == NJ - 1))
                last.then_inc(s["y_ps"], 1)

            def butterfly(c):
                k, part = divmod(c, 3)
                if part == 0:
                    pe.wait_ge(s["max_done"], NT * NG * (k + 1))
                    pe.wait_ge(s["bf_ready"], 1 + max(3 * k - 1, 0))
                    pe.wait_ge(s["G_ready"], 2 * k + 1)
                if part == 2:
                    pe.wait_ge(s["G_ready"], 2 * k + 2)
                    pe.wait_ge(s["bf_ready"], 1 + 3 * k + 1)
                    if k == 0:
                        pe.wait_ge(s["ld_wcon"], 16)
                up = part < 2
                src, d = (U[:, k % 2, :, :], k) if up else (V[:, k % 2, :, :], 2 - k)
                w, o = (D + 2, bank[2 + part]) if up else (D, bank[2])
                for i, t in enumerate((2 * part, 2 * part + 1) if up else range(NH)):
                    for t_ in (range(NH) if d == 2 else (t,)):
                        m = G2[:, 1 - up, t_, t, :] if d == 2 else (G0, G1)[d][:, 1 - up, t, :]
                        last = mm(o[:, w * i:w * i + w], m, src[:, t_, :], start=(t_ == 0 or d < 2), stop=(t_ == NH - 1 or d < 2))
                last.then_inc(s["bf_ps"], 1)

            def score(b, k):
                gq, t = divmod(k, NT)
                u = b % 2
                if k == 0 and b == 0:
                    pe.wait_ge(s["gated"], 2 * NJ * B)
                if k == 0 and b:
                    pe.wait_ge(s["bf_ready"], 1 + 3 * b)
                if t == 0:
                    pe.wait_ge(ld_Q[u][gq], 48 * (b // 2 + 1))
                    pe.wait_ge(s["KS_ready"], B * gq + b + 1)
                k += NT * NG * b
                if k >= 2:
                    pe.wait_ge(s["max_done"], k - 1)
                mm(bank[2 + k % 2][:, 0:HG * C], QS[0:96, u, gq, P * t:P * t + P],
                   KS[0:96, gq, b, :, :].rearrange("p i c -> p (i c)"), start=True, stop=True).then_inc(s["a_ps"], 1)

            def shifted_score(h):
                b, i = divmod(h, HEADS)
                gq = i // HG
                if i == 0:
                    pe.wait_ge(ld_M[b % 2], 16 * NG * (b // 2 + 1))
                if h == 0:
                    pe.wait_ge(s["KS_ones"], 2)
                    pe.wait_ge(s["x2_done"], B)
                if h >= 2:
                    pe.wait_ge(s["exp_done"], h - 1)
                mm(bank[4 + h % 2][0:C, :], KS[:, gq, b, i % HG, :], QS[:, b % 2, gq, :], start=True, stop=True).then_inc(s["s_ps"], 1)

            def weighted(h):
                b, i = divmod(h, HEADS)
                q, at = h // HG, 32 * (h % HG)
                pe.wait_ge(s["exp_done"], h + 1)
                if q >= 2:
                    pe.wait_ge(s["us_ready"], q - 1)
                mm(bank[6 + q % 2][at:at + 32, :], VA[:, b, i, :], pe_[:, h % 4, :], start=True, stop=True).then_inc(s["pv_done"], 1)

            def rows_of_values(b, t):
                pe.wait_ge(s["us_ready"], NG * (b + 1))
                if t >= 2:
                    pe.wait_ge(s["an_ready"], NT * b + 4 - t)
                if t == 1 and b:
                    pe.wait_ge(s["x3_done"], b)
                if t == 1 and b + 3 < B:
                    pe.wait_ge(s["qf_ready"], b + 4)
                if t == 0 and b + 2 < B:
                    pe.wait_ge(s["mT_ready"], b + 3)
                for gq in range(NG):
                    last = tp(bank[UT_BANKS[t]][:, P * gq:P * gq + P], US[:, b % 2, gq, P * t:P * t + P], ident[:, :])
                last.then_inc(s["ut_ps"], 1)

            def attended(b):
                pe.wait_ge(s["an_ready"], NT * (b + 1))
                for t in range(NT):
                    last = tp(bank[0][:, P * t:P * t + P], an[:, t, :], ident[:, :])
                last.then_inc(s["anT_ps"], 1)

            def project(b):
                pe.wait_ge(s["aT_ready"], b + 1)
                for t in range(NT):
                    last = mm(bank[1][:, P * t:P * t + P], aT[:, b % 2, P * t:P * t + P], wo[:, :], start=True, stop=True)
                last.then_inc(s["o_ps"], 1)

            def maxima_by_rows(b):
                pe.wait_ge(s["mx_ready"], b + 1)
                for t in range(NT):
                    last = tp(bank[0][:, P * t:P * t + P], mx[:, t, :, :].bitcast(F32).rearrange("p q c -> p (q c)"), ident[:, :])
                last.then_inc(s["mT_ps"], 1)

            def expand(k):
                b, j = divmod(k, NH)
                pe.wait_ge(s["nT_ready"], 2 * B + b + 1)
                if k >= 2:
                    pe.wait_ge(s["gelu_done"], k - 1)
                mm(bank[2 + k % 2][:, :], wup[:, P * j:P * j + P], nT[:, b % 2, :], start=True, stop=True).then_inc(s["hid1_ps"], 1)

            for b in range(-1, B):
                for i in range(HEADS):
                    if b >= 0:
                        h = HEADS * b + i
                        shifted_score(h)
                    if i < 8 and b + 1 < B:
                        score(b + 1, 2 * i)
                    if b >= 0 and h >= 2:
                        weighted(h - 2)
                    if i < 8 and b + 1 < B:
                        score(b + 1, 2 * i + 1)
                    if b + 2 < B and i == 1:
                        if b == -1:
                            pe.wait_ge(s["qf_ready"], 1)
                        transposed_rows(B + b + 2)
                    if b + 2 < B and i == 3:
                        query(b + 2)
                    if i == 8 and b + 1 < B:
                        maxima_by_rows(b + 1)
                    if b <= 1 and i in BF_SLOTS:
                        butterfly(3 * (b + 1) + BF_SLOTS.index(i))
                    if b == 2 and i == 9:
                        pe.wait_ge(s["bf_ready"], 1 + 9)
                        for t in range(NH):
                            last = tp(bank[2][:, P * t:P * t + P], U[:, 1, t, 0:D], ident[:, :])
                        last.then_inc(s["wup_ps"], 1)
                    if i == 1 and b >= 2:
                        project(b - 2)
                    if b >= 1:
                        if i in UT_SLOTS:
                            rows_of_values(b - 1, UT_SLOTS.index(i))
                        if i == 15:
                            attended(b - 1)
                    if b == B - 1:
                        if i == 8:
                            transposed_rows(2 * B)
                        if i == 10:
                            expand(0)
                            expand(1)
            weighted(HEADS * B - 2)
            weighted(HEADS * B - 1)

            project(B - 2)
            rows_of_values(B - 1, 0)
            rows_of_values(B - 1, 1)
            expand(2)
            rows_of_values(B - 1, 2)
            rows_of_values(B - 1, 3)
            expand(3)
            attended(B - 1)
            transposed_rows(2 * B + 1)
            project(B - 1)
            for b in range(B):
                if b:
                    for j in range(NH):
                        expand(NH * b + j)
                    if b + 1 < B:
                        transposed_rows(2 * B + b + 1)
                if b >= 2:
                    pe.wait_ge(s["x4_done"], b - 1)
                for t in range(NT):
                    for j in range(NH):
                        if t == 0:
                            pe.wait_ge(s["gelu_done"], NH * b + j + 1)
                        last = mm(bank[6 + b % 2][:, P * t:P * t + P], ge[:, b % 2, j, P * t:P * t + P], V[:, 1, j, :], start=(j == 0), stop=(j == NH - 1))
                last.then_inc(s["y1_ps"], 1)


def kernel(**inputs):
    import numpy as np
    import concourse.bacc as bacc
    from concourse.bass_utils import run_bass_kernel_spmd

    nc = bacc.Bacc("TRN2", target_bir_lowering=False, num_devices=1)
    arrays, aps = {}, {}
    for name, a in inputs.items():
        a = np.ascontiguousarray(a)
        arrays[f"in_{name}"] = a
        aps[name] = nc.dram_tensor(f"in_{name}", a.shape, mybir.dt.from_np(a.dtype), kind="ExternalInput").ap()
    shape = arrays["in_x"].shape
    out = nc.dram_tensor("out_x", shape, F32, kind="ExternalOutput").ap()
    two_layer_block(nc, aps, out)
    r = run_bass_kernel_spmd(nc, [arrays], core_ids=[0])
    return r.results[0]["out_x"]
```

```python
from contextlib import ExitStack

import concourse.bass as bass
from concourse import mybir

F32 = mybir.dt.float32
F32R = mybir.dt.float32r
BF16 = mybir.dt.bfloat16
ALU = mybir.AluOpType
ACT = mybir.ActivationFunctionType
AX = mybir.AxisListType

P = 128
EPS = 1e-5


def two_layer_block(nc, inp, out):
    x, ctx_in = inp["x"], inp["ctx_1024"]
    B, S, D = x.shape
    C = ctx_in.shape[1]
    NT = S // P
    RATE = inp["L0_xattn_conv_w"].shape[0]
    HALF = S // 2
    TC = (C - RATE) // RATE + 1
    E, HE = inp["L0_ffn_rb1"].shape
    NJ = E * HE // P
    HID = inp["L1_ffn_W_exp"].shape[1]
    NH = HID // P
    HEADS = 16
    HD = D // HEADS
    NG = D // 32
    HG = HEADS // NG
    SCALE = float(HD) ** -0.5
    NB = 3
    CUT1 = HALF - TC - P
    CUT3 = S - C - 3 * P
    CW = 96

    ctx = ExitStack()
    with ctx:
        def sb(name, shape, dt=F32):
            return ctx.enter_context(nc.sbuf_tensor(name, shape, dt))

        def sem(name):
            return ctx.enter_context(nc.semaphore(name))

        X = sb("X", [P, B, NT, D])
        XS = sb("XS", [P, B, NT, D])
        xc = sb("xc", [B * TC, RATE, D])
        xcn = sb("xcn", [B * TC, RATE, D])
        cpad = sb("cpad", [P, B, RATE, P])
        convw = sb("convw", [P, RATE, D])
        comp = sb("comp", [P, B, D])
        convb = sb("convb", [1, D])
        convm = sb("convm", [1, P])
        nrm = sb("nrm", [P, 2, NT, D])
        nT = sb("nT", [P, 2, S])
        stat = sb("stat", [P, NT, 6])
        mv = sb("mv", [P, 2, NT, 2])
        ve = sb("ve", [P, 2, NT])
        rstd = sb("rstd", [P, 2, NT])
        smv = sb("smv", [P, B, NT, 2])
        sve = sb("sve", [P, B, NT])
        srs = sb("srs", [P, B, NT])
        smean = sb("smean", [P, B, NT])
        sscale = sb("sscale", [P, B, NT])
        sbias = sb("sbias", [P, B, NT])
        cstat = sb("cstat", [B * TC, RATE, 6])
        cmv = sb("cmv", [B * TC, RATE, 2])
        cve = sb("cve", [B * TC, RATE])
        crs = sb("crs", [B * TC, RATE])
        keep = sb("keep", [P, NT])
        nkeep = sb("nkeep", [P, NT])
        raw = sb("raw", [P, NT])
        mhalf = sb("mhalf", [P, NT])
        phalf = sb("phalf", [P, NT, 2])
        ident = sb("ident", [P, P])
        identb = sb("identb", [P, P], BF16)
        rows = sb("rows", [32, P])
        cols = sb("cols", [P, 32])
        w1 = sb("w1", [P, E * HE + HE])
        w2 = sb("w2", [P, NJ + 1, D])
        ebias = sb("ebias", [P, E])
        tri = sb("tri", [P, E, E])
        lg = sb("lg", [P, NT, E])
        nlg = sb("nlg", [P, NT, E])
        el = sb("el", [P, NT, E])
        sp = sb("sp", [P, NT, E])
        rt = sb("rt", [P, NT, E])
        top = sb("top", [P, NT, 8])
        roots = sb("roots", [P, NT, 2])
        beats = sb("beats", [P, NT, E, E])
        ties = sb("ties", [P, NT, E, E])
        rank = sb("rank", [P, NT, E])
        cnat = sb("cnat", [P, NT, CW])
        res = sb("res", [P, 2, NT, E])
        c24 = sb("c24", [P, NT, NB, E], BF16)
        cT24 = sb("cT24", [NB * E, S], BF16)
        sel8 = sb("sel8", [NB * E, E])
        sel = sb("sel", [NB * E, E, HE], BF16)
        sil = sb("sil", [P, NJ, S])
        g = sb("g", [P, 2, NJ + 1, S])
        wq = sb("wq", [P, D])
        wk = sb("wk", [P, D])
        wv = sb("wv", [P, D])
        wo = sb("wo", [P, D])
        bvb = sb("bvb", [P, D])
        bob = sb("bob", [P, D])
        bfin = sb("bfin", [P, D])
        bfin2 = sb("bfin2", [P, D])
        cx = sb("cx", [C, B, D])
        cxT = sb("cxT", [P, B * C])
        kf = sb("kf", [P, B * C])
        kh = sb("kh", [P, B * C], F32R)
        kl = sb("kl", [P, B * C], F32R)
        KR = sb("KR", [96, NG, B * C], F32R)
        hm = sb("hm", [96, HG])
        ones_p = sb("ones_p", [P, HG, C])
        KS = sb("KS", [P, NG, B, HG, C], F32R)
        VA = sb("VA", [C, B, HEADS, 32])
        qf = sb("qf", [P, S])
        qh = sb("qh", [P, 2, S], F32R)
        ql = sb("ql", [P, 2, S], F32R)
        QS = sb("QS", [P, 2, NG, S], F32R)
        nm = sb("nm", [P, NT, HEADS])
        mx = sb("mx", [P, NT, NG, 32], F32R)
        mT = sb("mT", [P, 2, S], F32R)
        RING = NJ
        expw = sil[0:C, 0:RING, :]
        US = sb("US", [P, 2, NG, S])
        rec = sb("rec", [P, 2, HEADS])
        an = sb("an", [P, NT, D])
        aT = sb("aT", [P, 2, S])
        wexp = sb("wexp", [P, HID])
        BW = sb("BW", [P, 3, 12, 2, 2])
        M = sb("M", [P, 2, 3, 8, 8])
        pa = sb("pa", [P, 2, 3, 32])
        pb = sb("pb", [P, 2, 3, 32])
        Mo = sb("Mo", [P, 3, 8, 8])
        MR = sb("MR", [P, 3, 2, NH, 8])
        mk0 = sb("mk0", [P, 16])
        mk1 = sb("mk1", [P, 2, 8])
        mk2 = sb("mk2", [P, 64])
        G0 = sb("G0", [P, 2, NH, P])
        G1 = sb("G1", [P, 2, NH, P])
        G2 = g[:, :, 0:NH, :].rearrange("p u t (v k) -> p u t v k", k=P)
        U = sb("U", [P, 2, NH, D + 2])
        V = sb("V", [P, 2, NH, D])
        wuh = sb("wuh", [P, HID], F32R)
        wul = mT[:, 0, :]
        nh, nl = qh, ql
        bup = sb("bup", [P, NH])

        bank = [ctx.enter_context(nc.psum_tensor(f"bank{i}", [P, S], F32)) for i in range(8)]
        bw_dram = nc.dram_tensor("bw_dram", (2, 4, 24, 32), F32, kind="Internal").ap()
        mid_dram = nc.dram_tensor("mid_dram", (8, P, 8), F32, kind="Internal").ap()
        mh_dram = nc.dram_tensor("mh_dram", (3, 2, HID, 8), F32, kind="Internal").ap()

        names = """ld_xc ld_conv ld_rows ld_w1 ld_w2 ld_bc ld_cx ld_wa ld_wk ld_wv ld_wexp ld_wcon bw_sorted ld_bw
        rows_z ident_ready consts_ready masks_ready cols_ps cols_ready pool_step dve_step act_step
        conv_ve conv_rstd conv_nrm conv_tp conv_T conv_ps s0_ve s0_ready xs_ready x1_done
        ve_ready rstd_ready ln_nrm tp_ps nT_ready logits_ps lg_ready compared ln_ready sp_ready
        beats_ready rank_ready a_ready cnat_z comb_ready combT_ps cT_ready combT_ready hid_ps silu_done gate_ps gated y_ps x2_done
        cxT_ps cxT_ready k_ps kf_ready k_split KR_ready KS_ready KS_ones v_ps VA_z VA_ready
        q_ps qf_ready q_split a_ps max_done mx_z mx_ready mT_ps mT_ready
        s_ps exp_done pv_done us_ready ut_ps an_ready anT_ps aT_ready o_ps bo_added x3_done
        ones_ready M_ready mid_stored M_sorted MR_ready G_ready wexpT_ps bf_ps bf_ready wup_ps wuh_ready wul_ready nl_ready bup_ready
        hid1_ps hid1_kept gelu_done y1_ps bfin_sum bfin_added x4_done stored""".split()
        s = {n: sem(n) for n in names}
        ld_x = [sem("ld_x_first"), sem("ld_x_rest")]
        ld_xs = [sem("ld_xs_first"), sem("ld_xs_rest")]
        ld_Q = [[sem(f"ld_Q{u}{q}") for q in range(NG)] for u in range(2)]
        ld_M = [sem(f"ld_M{u}") for u in range(2)]

        block = ctx.enter_context(nc.Block())
        R_RB1, R_SB1, R_BQ, R_BK, R_BE, R_UB, R_RW = 0, 4, 5, 6, 7, 11, 15
        NR = R_RW + E
        A_SLOTS = (1, 1, 2, 2, 3, 3, 4, 4, 5, 6, 6, 7, 7, 8, 9, 9)
        MT_SLOT = 10
        UT_SLOTS = (4, 6, 7, 9)
        EXP_SLOTS = (11, 12, 13, 14)
        GATE_BANKS = (4, 5, 2, 3)

        def T_SLOT(b):
            return 4 if b < 0 else 1

        def Q_SLOT(b):
            return 6 if b < 0 else 3

        def BF_SLOTS(b):
            return (1, 3, 12) if b < 0 else (11, 13, 15)

        def T_BANK(k):
            return 0 if k < 2 * B else 2 if k < 2 * B + 2 else 4 + k % 2

        def A_BANK(k):
            return 2 + k % (4 if k < NT * NG else 2)

        def BF_BANK(k, part):
            return ((6, 7, 6) if k == 0 else (2, 3, 2))[part]

        @block.sync
        def _(sp_):
            dma = sp_.dma_start

            def load_shifted(b0, b1):
                bs = slice(b0, b1)
                for t in range(2):
                    dma(XS[:, bs, t, :], x[bs, TC + P * t:TC + P * t + P, :].rearrange("b p d -> p b d")).then_inc(ld_xs[b0 > 0], 16)
                dma(XS[:, bs, 2, :], x[bs, HALF + C:HALF + C + P, :].rearrange("b p d -> p b d")).then_inc(ld_xs[b0 > 0], 16)
                dma(XS[0:CUT3, bs, 3, :], x[bs, HALF + C + P:S, :].rearrange("b p d -> p b d")).then_inc(ld_xs[b0 > 0], 16)
                dma(XS[CUT3:P, bs, 3, :], ctx_in[bs, :, :].rearrange("b p d -> p b d")).then_inc(ld_xs[b0 > 0], 16)

            def load_stream(b0, b1):
                dma(X[:, b0:b1, :, :].rearrange("p b t d -> p (b t) d"),
                    x[b0:b1].rearrange("b (t p) d -> p (b t) d", p=P)).then_inc(ld_x[b0 > 0], 16)

            def row(name):
                return inp[name].rearrange("(a d) -> a d", a=1)

            for b in range(B):
                dma(xc[TC * b:TC * b + TC, :, :],
                    x[b, HALF:HALF + TC * RATE, :].rearrange("(j r) d -> j r d", r=RATE)).then_inc(s["ld_xc"], 16)
            load_shifted(0, 1)
            load_stream(0, 1)
            dma(convw[:, :, :], inp["L0_xattn_conv_w"].rearrange("r i o -> i r o")).then_inc(s["ld_conv"], 16)
            dma(convb[:, :], row("L0_xattn_conv_b")).then_inc(s["ld_conv"], 16)
            load_shifted(1, B)
            dma(cx[:, :, :], ctx_in.rearrange("b c d -> c b d")).then_inc(s["ld_cx"], 16)
            sp_.wait_ge(s["rows_z"], 1)
            for r, src in ((R_RW, inp["L0_ffn_routing_W"]), (R_RB1, inp["L0_ffn_rb1"].rearrange("(j e) h -> j (e h)", j=NJ)),
                           (R_BQ, row("L1_xattn_bq")), (R_BK, row("L1_xattn_bk")),
                           (R_BE, inp["L1_ffn_b_exp"].rearrange("(a d) -> a d", d=P)),
                           (R_UB, inp["L1_ffn_up_bias"].rearrange("(a d) -> a d", d=P))):
                dma(rows[r:r + src.shape[0], :], src).then_inc(s["ld_rows"], 16)
            dma(rows[R_SB1:R_SB1 + 1, 0:HE], row("L0_ffn_sb1")).then_inc(s["ld_rows"], 16)
            dma(ebias[:, :], row("L0_ffn_expert_bias").broadcast_to((P, E))).then_inc(s["ld_rows"], 16)
            dma(w1[:, 0:E * HE].rearrange("p (e h) -> p e h", e=E), inp["L0_ffn_rW1"].rearrange("e d h -> d e h")).then_inc(s["ld_w1"], 16)
            dma(w1[:, E * HE:], inp["L0_ffn_sW1"]).then_inc(s["ld_w1"], 16)
            dma(wk[:, :], inp["L1_xattn_Wk"]).then_inc(s["ld_wk"], 16)
            load_stream(1, B)
            dma(wv[:, :], inp["L1_xattn_Wv"]).then_inc(s["ld_wv"], 16)
            dma(bvb[:, :], row("L1_xattn_bv").broadcast_to((P, D))).then_inc(s["ld_wv"], 16)
            dma(w2[:, 0:NJ, :], inp["L0_ffn_rW2"].rearrange("e h d -> (e h) d").rearrange("(j p) d -> p j d", p=P)).then_inc(s["ld_w2"], 16)
            dma(w2[0:HE, NJ, :], inp["L0_ffn_sW2"]).then_inc(s["ld_w2"], 16)
            dma(w2[HE:HE + E, NJ, :], inp["L0_ffn_rb2"]).then_inc(s["ld_w2"], 16)
            dma(w2[HE + E:HE + E + 1, NJ, :], row("L0_ffn_sb2")).then_inc(s["ld_w2"], 16)
            W = [inp["L1_ffn_up_weights"], inp["L1_ffn_down_weights"]]
            for u in range(2):
                dma(bw_dram[u].rearrange("k n f -> n k f"),
                    W[u][3:6].rearrange("m (a k c) r s -> (m a) k (c r s)", a=8, k=4)).then_inc(s["bw_sorted"], 16)
            for t, n in ((wq, "Wq"), (wo, "Wo")):
                dma(t[:, :], inp["L1_xattn_" + n]).then_inc(s["ld_wa"], 16)
            for u in range(2):
                g64 = slice(64 * u, 64 * u + 64)
                dma(BW[g64, 0, :, :, :].rearrange("g (m k) r c -> g m (k r c)", m=3),
                    W[u][0:3].rearrange("m (g k) r c -> g m (k r c)", k=4)).then_inc(s["ld_bw"], 16)
                dma(BW[g64, 2, :, :, :].rearrange("g n r c -> g n (r c)"),
                    W[u][6:9].rearrange("m (k g) r c -> g (m k) (r c)", k=4)).then_inc(s["ld_bw"], 16)
            sp_.wait_ge(s["bw_sorted"], 32)
            for u in range(2):
                dma(BW[64 * u:64 * u + 64, 1, :, :, :].rearrange("g n r c -> g n (r c)"),
                    bw_dram[u].rearrange("k n f -> (k n f)").rearrange("(n g f) -> g n f", g=64, f=4)).then_inc(s["ld_bw"], 16)
            dma(wexp[:, :], inp["L1_ffn_W_exp"]).then_inc(s["ld_wexp"], 16)
            dma(V[:, 0, :, :], inp["L1_ffn_W_con"].rearrange("(t p) d -> p t d", p=P)).then_inc(s["ld_wcon"], 16)
            for t, n in ((bob, "L1_xattn_bo"), (bfin, "L1_ffn_b_con"), (bfin2, "L1_ffn_down_bias")):
                dma(t[:, :], row(n).broadcast_to((P, D))).then_inc(s["ld_bc"], 16)
            sp_.wait_ge(s["k_split"], 1)
            for gq in range(NG):
                r = slice(32 * gq, 32 * gq + 32)
                for at, src in ((0, kh), (32, kl), (64, kh)):
                    dma(KR[at:at + 32, gq, :].bitcast(F32), src[r, :].bitcast(F32)).then_inc(s["KR_ready"], 16)
            sp_.wait_ge(s["M_ready"], 1)
            dma(mid_dram.rearrange("i p j -> p i j"), Mo[:, 1, :, :]).then_inc(s["mid_stored"], 16)
            dma(mh_dram[0].rearrange("u (g i) j -> (u g) (i j)", i=8),
                Mo[:, 0, :, :].rearrange("p i j -> p (i j)")).then_inc(s["M_sorted"], 16)
            for u in range(2):
                dma(mh_dram[2, u].rearrange("(i g) j -> g i j", i=8), Mo[64 * u:64 * u + 64, 2, :, :]).then_inc(s["M_sorted"], 16)
            sp_.wait_ge(s["mid_stored"], 16)
            dma(mh_dram[1].rearrange("u (a i c) j -> (u a) i (c j)", a=8, i=8),
                mid_dram.rearrange("i (n c) j -> n i (c j)", c=8)).then_inc(s["M_sorted"], 16)
            sp_.wait_ge(s["M_sorted"], 16 * 4)
            for d in range(3):
                dma(MR[:, d, :, :, :].rearrange("p u t j -> p (u t) j"),
                    mh_dram[d].rearrange("u (t p) j -> p (u t) j", p=P)).then_inc(s["MR_ready"], 16)

            def stack_q(b, gq):
                u = b % 2
                sp_.wait_ge(s["q_split"], b + 1)
                if b >= 2:
                    sp_.wait_ge(s["exp_done"], HEADS * (b - 2) + HG * (gq + 1))
                r = slice(32 * gq, 32 * gq + 32)
                for at, src in ((0, qh), (32, qh), (64, ql)):
                    dma(QS[at:at + 32, u, gq, :].bitcast(F32), src[r, u, :].bitcast(F32)).then_inc(ld_Q[u][gq], 16)

            def stack_max(b):
                u = b % 2
                sp_.wait_ge(s["mT_ready"], b + 1)
                if b >= 2:
                    sp_.wait_ge(s["exp_done"], HEADS * (b - 1))
                for gq in range(NG):
                    dma(QS[96:128, u, gq, :].bitcast(F32), mT[32 * gq:32 * gq + 32, u, :].bitcast(F32)).then_inc(ld_M[u], 16)

            for gq in range(NG):
                stack_q(0, gq)
            for b in range(-1, B):
                if 0 <= b < B - 2:
                    stack_q(b + 2, 0)
                    stack_q(b + 2, 1)
                if b + 1 < B:
                    stack_max(b + 1)
                if b + 2 < B:
                    for gq in range(2 if b >= 0 else 0, NG):
                        stack_q(b + 2, gq)
            for b in range(B):
                for h, ts in enumerate((slice(0, NT // 2), slice(NT // 2, NT))):
                    sp_.wait_ge(s["x4_done"], 2 * b + h + 1)
                    dma(out[b].rearrange("(t p) d -> p t d", p=P)[:, ts, :], X[:, b, ts, :]).then_inc(s["stored"], 16)
            sp_.wait_ge(s["stored"], 16 * 2 * B)

        @block.gpsimd
        def _(pool):
            gp = nc.gpsimd
            n = [0]

            def step(ins):
                n[0] += 1
                ins.then_inc(s["pool_step"], 1)
                pool.wait_ge(s["pool_step"], n[0])

            gp.memset(rows[:, :], 0.0).then_inc(s["rows_z"], 1)
            step(gp.memset(ident[:, :], 0.0))
            gp.affine_select(out=ident[:, :], in_=ident[:, :], compare_op=ALU.not_equal, fill=1.0, base=0,
                             pattern=[[-1, P]], channel_multiplier=1).then_inc(s["ident_ready"], 1)
            gp.memset(cpad[:, :, :, :], 0.0).then_inc(s["consts_ready"], 1)
            gp.memset(mhalf[:, :], -0.5)
            gp.memset(phalf[:, :], 0.5)
            gp.memset(raw[:, :], 0.0)
            step(gp.memset(keep[:, :], 1.0))
            gp.memset(keep[:, 1:2], 0.0)
            gp.memset(keep[:, 3:4], 0.0)
            step(gp.memset(raw[:, 3:4], 1.0))
            gp.memset(keep[0:CUT1, 1:2], 1.0)
            step(gp.memset(keep[0:CUT3, 3:4], 1.0))
            gp.tensor_scalar(nkeep[:, :], keep[:, :], -1.0, None, ALU.mult)
            gp.memset(raw[0:CUT3, 3:4], 0.0)
            step(gp.memset(convm[:, :], 0.0))
            step(gp.memset(convm[:, CUT1:P], 1.0))

            def shift_scales(b):
                pool.wait_ge(s["s0_ve"], b + 1)
                gp.tensor_tensor(smean[:, b, :], smv[:, b, :, 0], nkeep[:, :], ALU.mult)
                step(gp.tensor_tensor(srs[:, b, :], sve[:, b, :], mhalf[:, :], ALU.pow))
                gp.tensor_tensor(sbias[:, b, :], smean[:, b, :], srs[:, b, :], ALU.mult)
                step(gp.tensor_tensor(sscale[:, b, :], srs[:, b, :], keep[:, :], ALU.mult))
                gp.tensor_tensor(sscale[:, b, :], sscale[:, b, :], raw[:, :], ALU.add).then_inc(s["s0_ready"], 1)

            def rstd_of(k):
                pool.wait_ge(s["ve_ready"], k + 1)
                gp.tensor_tensor(rstd[:, k % 2, :], ve[:, k % 2, :], mhalf[:, :], ALU.pow).then_inc(s["rstd_ready"], 1)

            def count_beaten(b):
                pool.wait_ge(s["compared"], b + 1)
                step(gp.tensor_tensor(ties[:, :, :, :].rearrange("p t e f -> p t (e f)"),
                                      ties[:, :, :, :].rearrange("p t e f -> p t (e f)"),
                                      tri[:, :, :].rearrange("p e f -> p (e f)").unsqueeze(1).broadcast_to((P, NT, E * E)), ALU.mult))
                gp.tensor_tensor(beats[:, :, :, :].rearrange("p t e f -> p (t e f)"),
                                 beats[:, :, :, :].rearrange("p t e f -> p (t e f)"),
                                 ties[:, :, :, :].rearrange("p t e f -> p (t e f)"), ALU.add).then_inc(s["beats_ready"], 1)

            def roots_of(b):
                pool.wait_ge(s["sp_ready"], b + 1)
                gp.tensor_tensor(roots[:, :, :], top[:, :, 0:2], phalf[:, :, :], ALU.pow).then_inc(s["a_ready"], 1)

            pool.wait_ge(s["conv_ve"], 1)
            gp.tensor_tensor(crs[:, :], cve[:, :], mhalf[0:B * TC, :], ALU.pow).then_inc(s["conv_rstd"], 1)
            shift_scales(0)
            step(gp.memset(tri[:, :, :], 1.0))
            gp.affine_select(out=tri[:, :, :], in_=tri[:, :, :], compare_op=ALU.is_gt, fill=0.0, base=0,
                             pattern=[[1, E], [-1, E]], channel_multiplier=0)
            step(gp.memset(cnat[:, :, :], 0.0))
            gp.memset(cnat[:, :, HE + E:HE + E + 1], 1.0).then_inc(s["cnat_z"], 1)
            step(gp.memset(VA[:, :, :, :], 0.0))
            gp.memset(VA[:, :, :, HD:HD + 1], 1.0).then_inc(s["VA_z"], 1)
            shift_scales(1)
            rstd_of(0)
            step(gp.memset(M[:, 0, 0, :, :], 0.0))
            step(gp.affine_select(out=M[:, 0, 0, :, :], in_=M[:, 0, 0, :, :], compare_op=ALU.not_equal, fill=1.0,
                                  base=0, pattern=[[1, 8], [-1, 8]], channel_multiplier=0))
            gp.tensor_copy(M[:, 0, 1, :, :], M[:, 0, 0, :, :])
            step(gp.tensor_copy(M[:, 0, 2, :, :], M[:, 0, 0, :, :]))
            pool.wait_ge(s["rstd_ready"], 1)
            step(gp.memset(ones_p[96:128, :, :], 0.0))
            for at in (0, HG):
                last = gp.affine_select(out=ones_p[96:128, :, :], in_=ones_p[96:128, :, :], compare_op=ALU.not_equal,
                                        fill=1.0, base=-at, pattern=[[-1, HG], [0, C]], channel_multiplier=1)
                if at == 0:
                    step(last)
            last.then_inc(s["ones_ready"], 1)
            pool.wait_ge(s["ones_ready"], 1)
            shift_scales(2)

            def block_stage(m):
                if m == 0:
                    pool.wait_ge(s["ld_bw"], 16 * 6)
                lo = 2 ** m
                hi = 4 // lo
                src, dst = m % 2, 1 - m % 2
                for d in range(3):
                    Mi = M[:, src, d, :, :].rearrange("p i (h c l) -> p i h c l", c=2, l=lo)
                    Wm = BW[:, d, m::3, :, :] if d == 1 else BW[:, d, 4 * m:4 * m + 4, :, :]
                    for r in range(2):
                        for c, t_ in ((0, pa), (1, pb)):
                            w_ = Wm[:, :, r, c].rearrange("p (h l) -> p h l", l=lo).unsqueeze(1).broadcast_to((P, 8, hi, lo))
                            o_ = t_[:, r, d, :].rearrange("p (i h l) -> p i h l", i=8, l=lo)
                            last = gp.tensor_tensor(o_, Mi[:, :, :, c, :], w_, ALU.mult)
                step(last)
                for d in range(3):
                    Mn = M[:, dst, d, :, :].rearrange("p i (h c l) -> p i h c l", c=2, l=lo)
                    for r in range(2):
                        a_ = pa[:, r, d, :].rearrange("p (i h l) -> p i h l", i=8, l=lo)
                        b_ = pb[:, r, d, :].rearrange("p (i h l) -> p i h l", i=8, l=lo)
                        last = gp.tensor_tensor(Mn[:, :, :, r, :], a_, b_, ALU.add)
                step(last)

            def blocks_out():
                step(gp.tensor_copy(Mo[0:64, :, :, :].rearrange("p d i j -> p (d i j)"), M[0:64, 1, :, :, :].rearrange("p d i j -> p (d i j)")))
                for d in range(3):
                    last = gp.tensor_copy(Mo[64:128, d, :, :], M[64:128, 1, d, :, :].rearrange("p i j -> p j i"))
                last.then_inc(s["M_ready"], 1)
                pool.wait_ge(s["M_ready"], 1)

            def head_keys(gqs):
                pool.wait_ge(s["KR_ready"], 16 * 3 * NG)
                pool.wait_ge(s["masks_ready"], 1)
                for gq in gqs:
                    for b in range(B):
                        gp.tensor_tensor(KS[0:96, gq, b, :, :],
                                         KR[:, gq, C * b:C * b + C].bitcast(F32).unsqueeze(1).broadcast_to((96, HG, C)),
                                         hm[:, :].unsqueeze(2).broadcast_to((96, HG, C)), ALU.mult).then_inc(s["KS_ready"], 1)

            def digit_matrix(u, d):
                for t in range(NH):
                    if d == 0:
                        last = gp.tensor_tensor(G0[:, u, t, :].rearrange("p (k j) -> p k j", j=8),
                                                MR[:, 0, u, t, :].unsqueeze(1).broadcast_to((P, 16, 8)),
                                                mk0[:, :].unsqueeze(2).broadcast_to((P, 16, 8)), ALU.mult)
                    elif d == 1:
                        for b6 in range(2):
                            last = gp.tensor_tensor(G1[:, u, t, 64 * b6:64 * b6 + 64].rearrange("p (j k) -> p j k", k=8),
                                                    MR[:, 1, u, t, :].unsqueeze(2).broadcast_to((P, 8, 8)),
                                                    mk1[:, b6, :].unsqueeze(1).broadcast_to((P, 8, 8)), ALU.mult)
                    else:
                        last = gp.tensor_tensor(G2[:, u, t, :, :].rearrange("p v (c k) -> p (v c) k", k=64),
                                                MR[:, 2, u, t, :].unsqueeze(2).broadcast_to((P, 8, 64)),
                                                mk2[:, :].unsqueeze(1).broadcast_to((P, 8, 64)), ALU.mult)
                last.then_inc(s["G_ready"], 1)

            def add_row(b, k, row_, done):
                pool.wait_ge(s["ln_nrm"], k)
                gp.tensor_tensor(X[:, b, :, :], X[:, b, :, :], row_[:, :].unsqueeze(1).broadcast_to((P, NT, D)),
                                 ALU.add).then_inc(s[done], 1)

            for b in range(B):
                count_beaten(b)
                roots_of(b)
                rstd_of(b + 1)
                if b == 0:
                    shift_scales(3)
                if b == 1:
                    block_stage(0)
                    block_stage(1)
                if b == 2:
                    block_stage(2)
                    blocks_out()
                    head_keys((0,))
                    gp.memset(mx[:, :, :, :].bitcast(F32), 0.0).then_inc(s["mx_z"], 1)
            head_keys((1, 2, 3))
            pool.wait_ge(s["MR_ready"], 16 * 3)
            digit_matrix(0, 0)
            rstd_of(B + 1)
            pool.wait_ge(s["y_ps"], B)
            digit_matrix(1, 2)
            digit_matrix(0, 1)
            digit_matrix(1, 1)
            pool.wait_ge(s["ld_bc"], 48)
            add_row(0, B + 1, bob, "bo_added")
            digit_matrix(0, 2)
            digit_matrix(1, 0)
            add_row(1, B + 2, bob, "bo_added")
            gp.tensor_tensor(bfin[:, :], bfin[:, :], bfin2[:, :], ALU.add).then_inc(s["bfin_sum"], 1)
            for b in range(2, B):
                rstd_of(B + b)
                add_row(b, B + b + 1, bob, "bo_added")
            pool.wait_ge(s["bfin_sum"], 1)
            for b in range(B):
                rstd_of(2 * B + b)
                add_row(b, 2 * B + b + 1, bfin, "bfin_added")

        @block.scalar
        def _(act_):
            sc = nc.scalar
            n = [0]

            def step(ins):
                n[0] += 1
                ins.then_inc(s["act_step"], 1)
                act_.wait_ge(s["act_step"], n[0])

            def copy_nT(k):
                act_.wait_ge(s["tp_ps"], k + 1)
                to = nT if k < 2 * B else nh
                sc.copy(to[:, k % 2, :], bank[T_BANK(k)][:, :]).then_inc(s["nT_ready"], 1)

            def copy_q(b):
                act_.wait_ge(s["q_ps"], b + 1)
                if b >= 1:
                    act_.wait_ge(s["q_split"], b)
                sc.activation(qf[:, :], bank[min(b, 1)][:, :], ACT.Identity, bias=cols[:, R_BQ:R_BQ + 1]).then_inc(s["qf_ready"], 1)

            def shift_rows(b):
                act_.wait_ge(s["s0_ready"], b + 1)
                for t in range(NT):
                    last = sc.activation(XS[:, b, t, :], XS[:, b, t, :], ACT.Identity, scale=sscale[:, b, t:t + 1], bias=sbias[:, b, t:t + 1])
                last.then_inc(s["xs_ready"], 1)

            sc.preload_act_table_set("natural_log_exp_and_others")
            act_.wait_ge(s["conv_tp"], 1)
            act_.wait_ge(s["consts_ready"], 1)
            sc.copy(cpad[:, :, :, CUT1:P].rearrange("p b r j -> p r b j"),
                    bank[5][:, 0:RATE * B * TC].rearrange("p (r b j) -> p r b j", r=RATE, b=B)).then_inc(s["conv_T"], 1)
            shift_rows(0)
            act_.wait_ge(s["cxT_ps"], 1)
            sc.copy(cxT[:, :], bank[5][:, 0:B * C]).then_inc(s["cxT_ready"], 1)
            shift_rows(1)
            act_.wait_ge(s["cols_ps"], 1)
            sc.copy(cols[:, 0:NR], bank[7][:, 0:NR]).then_inc(s["cols_ready"], 1)
            copy_nT(0)
            for b in range(B):
                if b:
                    sc.preload_act_table_set("natural_log_exp_and_others")
                act_.wait_ge(s["lg_ready"], b + 1)
                step(sc.activation(el[:, :, :], nlg[:, :, :], ACT.Exp))
                sc.activation(rt[:, :, :], el[:, :, :], ACT.Ln, bias=1.0).then_inc(s["ln_ready"], 1)
                for j in range(NJ + 1):
                    if b == 0 and j == NJ:
                        act_.wait_ge(s["k_ps"], 1)
                        sc.activation(kf[:, :], bank[7][:, 0:B * C], ACT.Identity, bias=cols[:, R_BK:R_BK + 1]).then_inc(s["kf_ready"], 1)
                    if b and j == NJ:
                        copy_nT(b + 1)
                    act_.wait_ge(s["hid_ps"], (NJ + 1) * b + j + 1)
                    hb = bank[2 + ((NJ + 1) * b + j) % 2]
                    if j < NJ:
                        if b >= 1:
                            act_.wait_ge(s["gated"], NJ * (2 * b - 1) + j + 1)
                        sc.activation(sil[:, j, :], hb[:, :], ACT.Silu,
                                      bias=cols[:, R_RB1 + j:R_RB1 + j + 1]).then_inc(s["silu_done"], 1)
                    else:
                        if b >= 2:
                            act_.wait_ge(s["y_ps"], b - 1)
                        sc.activation(g[0:HE, b % 2, NJ, :], hb[0:HE, :], ACT.Silu,
                                      bias=cols[0:HE, R_SB1:R_SB1 + 1]).then_inc(s["silu_done"], 1)
                act_.wait_ge(s["combT_ps"], b + 1)
                sc.copy(cT24[:, :], bank[6][0:NB * E, 0:S // 2].bitcast(BF16)).then_inc(s["cT_ready"], 1)
                sc.copy(g[HE:HE + E + 1, b % 2, NJ, :], bank[1][HE:HE + E + 1, :]).then_inc(s["combT_ready"], 1)
                if b == 0:
                    copy_nT(b + 1)
                if b + 2 < B:
                    shift_rows(b + 2)
                if b >= 2:
                    if b == B - 1:
                        copy_q(0)
                    act_.wait_ge(s["ones_ready"], 1)
                    for gq in (2 * b - 4, 2 * b - 3):
                        last = sc.copy(KS[96:128, gq, :, :, :].rearrange("p b i c -> p b (i c)"),
                                       ones_p[96:128, :, :].rearrange("p i c -> p (i c)").unsqueeze(1).broadcast_to((32, B, HG * C)))
                    last.then_inc(s["KS_ones"], 1)
            act_.wait_ge(s["wexpT_ps"], 1)
            sc.copy(U[:, 0, :, 0:D], bank[7][:, :].rearrange("p (t d) -> p t d", t=NH))
            sc.copy(U[:, 0, :, D:D + 2], cols[:, R_BE:R_BE + NH].unsqueeze(2).broadcast_to((P, NH, 2))).then_inc(s["bf_ready"], 1)

            def copy_butterfly(c):
                k, part = divmod(c, 3)
                act_.wait_ge(s["bf_ps"], c + 1)
                if part < 2:
                    sc.copy(U[:, (k + 1) % 2, 2 * part:2 * part + 2, :],
                            bank[BF_BANK(k, part)][:, 0:2 * (D + 2)].rearrange("p (t d) -> p t d", t=2)).then_inc(s["bf_ready"], 1)
                else:
                    sc.copy(V[:, (k + 1) % 2, :, :], bank[BF_BANK(k, part)][:, :].rearrange("p (t d) -> p t d", t=NH)).then_inc(s["bf_ready"], 1)

            def weights_of(h):
                act_.wait_ge(s["s_ps"], h + 1)
                if h >= RING:
                    act_.wait_ge(s["pv_done"], h - RING + 1)
                sc.activation(expw[:, h % RING, :], bank[4 + h % 2][0:C, :], ACT.Exp, scale=SCALE).then_inc(s["exp_done"], 1)

            def copy_values(q):
                act_.wait_ge(s["pv_done"], HG * (q + 1))
                if q >= 2 * NG:
                    act_.wait_ge(s["ut_ps"], NT * (q // NG - 1))
                sc.copy(US[:, q // NG % 2, q % NG, :], bank[6 + q % 2][:, :]).then_inc(s["us_ready"], 1)

            for b in range(-1, B):
                for i in range(HEADS):
                    if b >= 0:
                        h = HEADS * b + i
                        weights_of(h)
                        if h >= HG and h % HG == 1:
                            copy_values(h // HG - 1)
                    if i == T_SLOT(b) and b + 2 < B:
                        copy_nT(B + b + 2)
                    if i == Q_SLOT(b) and b + 2 < B:
                        copy_q(b + 2)
                    if i == MT_SLOT and b + 1 < B:
                        act_.wait_ge(s["mT_ps"], b + 2)
                        if b >= 1:
                            act_.wait_ge(ld_M[(b + 1) % 2], 16 * NG * ((b + 1) // 2))
                        sc.copy(mT[:, (b + 1) % 2, :], bank[0][:, :]).then_inc(s["mT_ready"], 1)
                    if b <= 1 and i in BF_SLOTS(b):
                        copy_butterfly(3 * (b + 1) + BF_SLOTS(b).index(i))
                    if b == 2 and i == MT_SLOT + 1:
                        act_.wait_ge(s["wup_ps"], 1)
                        sc.copy(wuh[:, :], bank[2][:, :]).then_inc(s["wuh_ready"], 1)
                    if i == 8 and b == B - 1:
                        copy_nT(2 * B)
                    if i == 15 and b >= 1:
                        act_.wait_ge(s["anT_ps"], b)
                        sc.copy(aT[:, (b - 1) % 2, :], bank[0][:, :]).then_inc(s["aT_ready"], 1)
            copy_values(NG * B - 1)

            def gelu(k):
                b, j = divmod(k, NH)
                if b:
                    act_.wait_ge(s["hid1_ps"], k + 1)
                else:
                    act_.wait_ge(s["hid1_kept"], k + 1)
                if k == 0:
                    act_.wait_ge(s["bup_ready"], 1)
                if b >= 2:
                    act_.wait_ge(s["y1_ps"], 2 * (b - 1))
                src = bank[2 + k % 2] if b else g[:, 0, j, :]
                sc.activation(g[:, b % 2, j, :], src[:, :], ACT.Gelu, bias=bup[:, j:j + 1]).then_inc(s["gelu_done"], 1)

            copy_nT(2 * B + 1)
            for j in range(NH):
                gelu(j)
            act_.wait_ge(s["anT_ps"], B)
            sc.copy(aT[:, (B - 1) % 2, :], bank[0][:, :]).then_inc(s["aT_ready"], 1)
            for b in range(1, B):
                for j in range(NH):
                    if j == 2 and b + 1 < B:
                        copy_nT(2 * B + b + 1)
                    gelu(NH * b + j)

        @block.vector
        def _(dve):
            v = nc.vector
            n = [0]

            def step(ins):
                n[0] += 1
                ins.then_inc(s["dve_step"], 1)
                dve.wait_ge(s["dve_step"], n[0])

            def moments(src, st, mv_, ve_, ready):
                for t in range(NT):
                    last = v.bn_stats(st[:, t, :], src(t))
                step(last)
                for t in range(NT):
                    last = v.bn_aggr(mv_[:, t, :], st[:, t, :])
                step(last)
                v.tensor_scalar(ve_, mv_[:, :, 1], EPS, None, ALU.add).then_inc(s[ready], 1)

            def shift_moments(b):
                dve.wait_ge(ld_xs[b > 0], 80)
                moments(lambda t: XS[:, b, t, :], stat[:, :, :], smv[:, b, :, :], sve[:, b, :], "s0_ve")

            def shift_add(b):
                dve.wait_ge(s["xs_ready"], b + 1)
                dve.wait_ge(ld_x[b > 0], 16)
                step(v.tensor_tensor(X[:, b, :, :], X[:, b, :, :], XS[:, b, :, :], ALU.add))
                if b == 0:
                    dve.wait_ge(s["conv_ps"], 1)
                    v.tensor_tensor(X[:, 0, 1, :], X[:, 0, 1, :], bank[4][:, 0:D], ALU.add).then_inc(s["x1_done"], 1)
                else:
                    v.tensor_tensor(X[:, b, 1, :], X[:, b, 1, :], comp[:, b, :], ALU.add).then_inc(s["x1_done"], 1)
                dve.wait_ge(s["x1_done"], b + 1)

            def stream_moments(b, k):
                moments(lambda t: X[:, b, t, :], stat[:, :, :], mv[:, k % 2, :, :], ve[:, k % 2, :], "ve_ready")

            def scale_rows(b, k):
                u = k % 2
                dve.wait_ge(s["rstd_ready"], k + 1)
                if k >= 2:
                    dve.wait_ge(s["tp_ps"], k - 1)
                for t in range(NT):
                    last = v.tensor_scalar(nrm[:, u, t, :], X[:, b, t, :], mv[:, u, t, 0:1], rstd[:, u, t:t + 1], ALU.subtract, ALU.mult)
                last.then_inc(s["ln_nrm"], 1)

            def normalise(b, k):
                stream_moments(b, k)
                scale_rows(b, k)

            def logits(b):
                dve.wait_ge(s["logits_ps"], b + 1)
                if b == 0:
                    dve.wait_ge(s["ld_rows"], 16 * 8)
                else:
                    dve.wait_ge(s["beats_ready"], b)
                step(v.tensor_tensor(lg[:, :, :], bank[0][:, 0:NT * E].rearrange("p (t e) -> p t e", e=E),
                                     ebias[:, :].unsqueeze(1).broadcast_to((P, NT, E)), ALU.add))
                v.scalar_tensor_tensor(out=nlg[:, :, :], in0=lg[:, :, :], scalar=-1.0, in1=lg[:, :, :],
                                       op0=ALU.mult, op1=ALU.min).then_inc(s["lg_ready"], 1)
                other = lg[:, :, :].unsqueeze(2).broadcast_to((P, NT, E, E))
                own = lg[:, :, :].unsqueeze(3).broadcast_to((P, NT, E, E))
                v.tensor_tensor(beats[:, :, :, :], other, own, ALU.is_gt)
                v.tensor_tensor(ties[:, :, :, :], other, own, ALU.is_equal).then_inc(s["compared"], 1)

            def softplus(b):
                dve.wait_ge(s["ln_ready"], b + 1)
                v.scalar_tensor_tensor(out=sp[:, :, :], in0=lg[:, :, :], scalar=0.0, in1=rt[:, :, :],
                                       op0=ALU.max, op1=ALU.add)
                step(v.tensor_scalar(res[:, 0, :, :], el[:, :, :], 1.0, -1.0, ALU.add, ALU.add))
                step(v.tensor_tensor(res[:, 1, :, :], el[:, :, :], res[:, 0, :, :], ALU.subtract))
                step(v.tensor_tensor(sp[:, :, :], sp[:, :, :], res[:, 1, :, :], ALU.add))
                if b >= 1:
                    dve.wait_ge(s["a_ready"], b)
                for t in range(NT):
                    last = v.max(top[:, t, :], sp[:, t, :])
                last.then_inc(s["sp_ready"], 1)

            def ranks(b):
                dve.wait_ge(s["beats_ready"], b + 1)
                v.tensor_reduce(rank[:, :, :], beats[:, :, :, :], axis=AX.X, op=ALU.add).then_inc(s["rank_ready"], 1)

            def combine(b):
                dve.wait_ge(s["a_ready"], b + 1)
                dve.wait_ge(s["rank_ready"], b + 1)
                if b == 0:
                    dve.wait_ge(s["cnat_z"], 1)
                else:
                    dve.wait_ge(s["combT_ps"], b)
                comb = cnat[:, :, HE:HE + E]
                for r in range(2):
                    last = v.scalar_tensor_tensor(out=res[:, r, :, :], in0=rank[:, :, :], scalar=float(r),
                                                  in1=roots[:, :, r:r + 1].broadcast_to((P, NT, E)), op0=ALU.is_equal, op1=ALU.mult)
                step(last)
                step(v.tensor_tensor(comb, res[:, 0, :, :], res[:, 1, :, :], ALU.add))
                step(v.tensor_copy(c24[:, :, 0, :], comb))
                step(v.tensor_tensor(res[:, 0, :, :], comb, c24[:, :, 0, :], ALU.subtract))
                step(v.tensor_copy(c24[:, :, 1, :], res[:, 0, :, :]))
                v.tensor_tensor(c24[:, :, 2, :], res[:, 0, :, :], c24[:, :, 1, :], ALU.subtract).then_inc(s["comb_ready"], 1)

            def split_q(b):
                u = b % 2
                dve.wait_ge(s["qf_ready"], b + 1)
                if b >= 2:
                    for gq in range(NG):
                        dve.wait_ge(ld_Q[u][gq], 48 * (b // 2))
                step(v.tensor_copy(qh[:, u, :], qf[:, :]))
                v.tensor_tensor(ql[:, u, :], qf[:, :], qh[:, u, :].bitcast(F32), ALU.subtract).then_inc(s["q_split"], 1)

            def gate(b, half):
                for j in range(NJ):
                    if half == 0:
                        dve.wait_ge(s["gate_ps"], NJ * b + j + 1)
                        dve.wait_ge(s["silu_done"], (NJ + 1) * b + j + 1)
                        if b >= 2:
                            dve.wait_ge(s["y_ps"], b - 1)
                    c = slice(HALF * half, HALF * half + HALF)
                    v.tensor_tensor(g[:, b % 2, j, c], sil[:, j, c], bank[GATE_BANKS[j]][:, c], ALU.mult).then_inc(s["gated"], 1)

            def add_to_stream(b, src, done):
                v.tensor_tensor(X[:, b, :, :].rearrange("p t d -> p (t d)"), X[:, b, :, :].rearrange("p t d -> p (t d)"),
                                src[:, :], ALU.add).then_inc(s[done], 1)

            def add_y(b):
                dve.wait_ge(s["y_ps"], b + 1)
                add_to_stream(b, bank[6], "x2_done")

            dve.wait_ge(s["ident_ready"], 1)
            v.tensor_copy(identb[:, :], ident[:, :])
            v.tensor_reduce(mk0[:, :], ident[:, :].rearrange("p (k j) -> p k j", j=8), axis=AX.X, op=ALU.add)
            v.tensor_reduce(mk1[:, :, :], ident[:, :].rearrange("p (b j k) -> p b k j", b=2, k=8), axis=AX.X, op=ALU.add)
            v.tensor_tensor(mk2[:, :], ident[:, 0:64], ident[:, 64:128], ALU.add)
            v.tensor_reduce(hm[:, :], ident[0:96, :].rearrange("p (b i d) -> p i b d", b=NG, d=HD), axis=AX.XY, op=ALU.add)
            step(v.tensor_reduce(sel8[:, :], ident[0:NB * E, 0:NB * E].rearrange("p (s e) -> p e s", s=NB), axis=AX.X, op=ALU.add))
            v.tensor_copy(sel[:, :, :], sel8[:, :].unsqueeze(2).broadcast_to((NB * E, E, HE))).then_inc(s["masks_ready"], 1)
            dve.wait_ge(s["ld_xc"], 16 * B)
            moments(lambda r: xc[:, r, :], cstat[:, :, :], cmv[:, :, :], cve[:, :], "conv_ve")
            shift_moments(0)
            dve.wait_ge(s["conv_rstd"], 1)
            for r in range(RATE):
                last = v.tensor_scalar(xcn[:, r, :], xc[:, r, :], cmv[:, r, 0:1], crs[:, r:r + 1], ALU.subtract, ALU.mult)
            last.then_inc(s["conv_nrm"], 1)
            shift_moments(1)
            shift_add(0)
            normalise(0, 0)
            shift_moments(2)
            dve.wait_ge(s["conv_ps"], B)
            step(v.tensor_copy(comp[:, 1:B, :].rearrange("p b d -> p (b d)"), bank[6][:, D:B * D]))
            shift_add(1)
            for b in range(B):
                logits(b)
                softplus(b)
                if 1 <= b < B - 1:
                    shift_add(b + 1)
                if b == B - 1:
                    dve.wait_ge(s["x2_done"], 1)
                stream_moments((b + 1) % B, b + 1)
                ranks(b)
                if b >= 1:
                    add_y(b - 1)
                if b >= 1:
                    scale_rows((b + 1) % B, b + 1)
                combine(b)
                if b == 0:
                    scale_rows(b + 1, b + 1)
                    dve.wait_ge(s["v_ps"], 1)
                    dve.wait_ge(s["ld_wv"], 32)
                    dve.wait_ge(s["VA_z"], 1)
                    for b_ in range(B):
                        last = v.tensor_tensor(VA[:, b_, :, 0:HD], bank[5][0:C, D * b_:D * b_ + D].rearrange("p (h d) -> p h d", d=HD),
                                               bvb[0:C, :].rearrange("p (h d) -> p h d", d=HD), ALU.add)
                    last.then_inc(s["VA_ready"], 1)
                    shift_moments(3)
                gate(b, 0)
                if b == B - 1:
                    split_q(0)
                gate(b, 1)
                if b == 0:
                    dve.wait_ge(s["kf_ready"], 1)
                    step(v.tensor_copy(kh[:, :], kf[:, :]))
                    v.tensor_tensor(kl[:, :], kf[:, :], kh[:, :].bitcast(F32), ALU.subtract).then_inc(s["k_split"], 1)

            def maximum(b, k):
                gq, t = divmod(k, NT)
                k = NT * NG * b + k
                dve.wait_ge(s["a_ps"], k + 1)
                v.tensor_reduce(nm[:, t, HG * gq:HG * gq + HG], bank[A_BANK(k)][:, 0:HG * C].rearrange("p (i c) -> p i c", i=HG),
                                axis=AX.X, op=ALU.max, negate=True).then_inc(s["max_done"], 1)

            def split_max(b):
                dve.wait_ge(s["max_done"], NT * NG * (b + 1))
                if b == 0:
                    dve.wait_ge(s["mx_z"], 1)
                else:
                    dve.wait_ge(s["mT_ps"], b)
                nm_ = nm[:, :, :].rearrange("p t (q i) -> p t q i", i=HG)
                step(v.tensor_copy(mx[:, :, :, 0:HG], nm_))
                v.tensor_tensor(mx[:, :, :, HG:2 * HG], nm_, mx[:, :, :, 0:HG].bitcast(F32), ALU.subtract).then_inc(s["mx_ready"], 1)

            def divide(b, t):
                dve.wait_ge(s["ut_ps"], NT * b + t + 1)
                if b >= 1:
                    dve.wait_ge(s["anT_ps"], b)
                pt = bank[t % 2][:, :].rearrange("p (h c) -> p h c", c=32)
                step(v.reciprocal(rec[:, t % 2, :], pt[:, :, HD]))
                v.tensor_tensor(an[:, t, :].rearrange("p (h d) -> p h d", d=HD), pt[:, :, 0:HD],
                                rec[:, t % 2, :].unsqueeze(2).broadcast_to((P, HEADS, HD)), ALU.mult).then_inc(s["an_ready"], 1)

            def add_o(b):
                dve.wait_ge(s["o_ps"], b + 1)
                dve.wait_ge(s["bo_added"], b + 1)
                add_to_stream(b, bank[1], "x3_done")

            def low_terms(k):
                dve.wait_ge(s["nT_ready"], k + 1)
                v.tensor_tensor(nl[:, k % 2, :], bank[T_BANK(k)][:, :], nh[:, k % 2, :].bitcast(F32), ALU.subtract).then_inc(s["nl_ready"], 1)

            def keep_hidden(j):
                dve.wait_ge(s["hid1_ps"], j + 1)
                v.tensor_copy(g[:, 0, j, :], bank[2 + j % 2][:, :]).then_inc(s["hid1_kept"], 1)

            dve.wait_ge(s["x2_done"], 2)
            stream_moments(1, B + 1)
            add_y(B - 1)
            for b in range(-1, B):
                for i in range(MT_SLOT):
                    for k in range(NT * NG):
                        if A_SLOTS[k] == i and b + 1 < B:
                            maximum(b + 1, k)
                    if i == 2 and b == -1:
                        scale_rows(1, B + 1)
                    if i == 2 and b >= 2:
                        add_o(b - 2)
                    if i == 3 and b == B - 1:
                        dve.wait_ge(s["x3_done"], 1)
                        normalise(0, 2 * B)
                    if i == 5 and 0 <= b < B - 2:
                        split_q(b + 2)
                    if i in UT_SLOTS and b >= 1:
                        divide(b - 1, UT_SLOTS.index(i))
                if b + 1 < B:
                    split_max(b + 1)
                if b == B - 1:
                    low_terms(2 * B)
                    dve.wait_ge(s["x3_done"], 2)
                    stream_moments(1, 2 * B + 1)
                    keep_hidden(0)
                    keep_hidden(1)
                    scale_rows(1, 2 * B + 1)
                    keep_hidden(2)
                    keep_hidden(3)
                    low_terms(2 * B + 1)
                if b == -1:
                    split_q(b + 2)
                if b == 2:
                    dve.wait_ge(s["wuh_ready"], 1)
                    v.tensor_tensor(wul, bank[2][:, :], wuh[:, :].bitcast(F32), ALU.subtract).then_inc(s["wul_ready"], 1)
                    dve.wait_ge(s["bf_ready"], 1 + 8)
                    v.tensor_tensor(bup[:, :], U[:, 1, :, D], cols[:, R_UB:R_UB + NH], ALU.add).then_inc(s["bup_ready"], 1)
                if b + 3 < B:
                    dve.wait_ge(s["x2_done"], b + 4)
                    normalise(b + 3, B + b + 3)
            add_o(B - 2)
            for t in range(NT):
                divide(B - 1, t)
            dve.wait_ge(s["x3_done"], B - 1)
            normalise(B - 2, 3 * B - 2)
            add_o(B - 1)
            dve.wait_ge(s["x3_done"], B)
            stream_moments(B - 1, 3 * B - 1)
            low_terms(2 * B + 2)
            scale_rows(B - 1, 3 * B - 1)
            for b in range(B):
                if b == 1:
                    low_terms(3 * B - 1)
                dve.wait_ge(s["bfin_added"], b + 1)
                for h, ts in enumerate((slice(0, NT // 2), slice(NT // 2, NT))):
                    dve.wait_ge(s["y1_ps"], 2 * b + h + 1)
                    v.tensor_tensor(X[:, b, ts, :], X[:, b, ts, :],
                                    bank[6 + h][:, 0:HALF // P * D].rearrange("p (t d) -> p t d", d=D), ALU.add).then_inc(s["x4_done"], 1)

        @block.tensor
        def _(pe):
            mm, tp = nc.tensor.matmul, nc.tensor.transpose
            def compress(b):
                cb = bank[6 if b else 4]
                for r in range(RATE):
                    mm(cb[:, P * b:P * b + P], cpad[:, b, r, :], convw[:, r, :], start=(r == 0), stop=False)
                mm(cb[:, P * b:P * b + P], convm[:, :], convb[:, :], start=False, stop=True).then_inc(s["conv_ps"], 1)

            pe.wait_ge(s["ident_ready"], 1)
            pe.wait_ge(s["conv_nrm"], 1)
            for r in range(RATE):
                last = tp(bank[5][:, r * B * TC:(r + 1) * B * TC], xcn[:, r, :], ident[0:B * TC, 0:B * TC])
            last.then_inc(s["conv_tp"], 1)
            pe.wait_ge(s["ld_conv"], 32)
            pe.wait_ge(s["conv_T"], 1)
            compress(0)
            pe.wait_ge(s["ld_cx"], 16)
            for b_ in range(B):
                last = tp(bank[5][:, C * b_:C * b_ + C], cx[:, b_, :], ident[0:C, 0:C])
            last.then_inc(s["cxT_ps"], 1)
            compress(1)
            compress(2)
            pe.wait_ge(s["ld_rows"], 16 * 8)
            tp(bank[7][:, 0:NR], rows[0:NR, :], ident[0:NR, 0:NR]).then_inc(s["cols_ps"], 1)

            def transposed_rows(k):
                pe.wait_ge(s["ln_nrm"], k + 1)
                for t in range(NT):
                    last = tp(bank[T_BANK(k)][:, P * t:P * t + P], nrm[:, k % 2, t, :], ident[:, :])
                last.then_inc(s["tp_ps"], 1)

            def route(b):
                pe.wait_ge(s["nT_ready"], b + 1)
                if b == 0:
                    pe.wait_ge(s["cols_ready"], 1)
                for t in range(NT):
                    last = mm(bank[0][:, E * t:E * t + E], nT[:, b % 2, P * t:P * t + P], cols[:, R_RW:R_RW + E], start=True, stop=True)
                last.then_inc(s["logits_ps"], 1)

            def query(b):
                pe.wait_ge(s["nT_ready"], B + b + 1)
                if b == 0:
                    pe.wait_ge(s["ld_wa"], 32)
                mm(bank[min(b, 1)][:, :], wq[:, :], nT[:, (B + b) % 2, :], start=True, stop=True).then_inc(s["q_ps"], 1)

            transposed_rows(0)
            compress(3)
            route(0)
            for b in range(B):
                u = b % 2
                if b == 0:
                    pe.wait_ge(s["ld_w1"], 32)
                for j in range(NJ + 1):
                    if b == 0 and j == 2:
                        pe.wait_ge(s["ld_wk"], 16)
                        pe.wait_ge(s["cxT_ready"], 1)
                        mm(bank[7][:, 0:B * C], wk[:, :], cxT[:, :], start=True, stop=True).then_inc(s["k_ps"], 1)
                    if b == 0 and j == NJ:
                        pe.wait_ge(s["ld_wv"], 32)
                        for b_ in range(B):
                            last = mm(bank[5][0:C, D * b_:D * b_ + D], cxT[:, C * b_:C * b_ + C], wv[:, :], start=True, stop=True)
                        last.then_inc(s["v_ps"], 1)
                    if b and j == NJ:
                        pe.wait_ge(s["compared"], b + 1)
                        transposed_rows(b + 1)
                    k = (NJ + 1) * b + j
                    m = P if j < NJ else HE
                    if j >= 2:
                        pe.wait_ge(s["silu_done"], k - 1)
                    mm(bank[2 + k % 2][0:m, :], w1[:, P * j:P * j + m], nT[:, u, :], start=True, stop=True).then_inc(s["hid_ps"], 1)
                pe.wait_ge(s["comb_ready"], b + 1)
                if b == 0:
                    pe.wait_ge(s["masks_ready"], 1)
                    pe.wait_ge(s["x1_done"], 2)
                else:
                    pe.wait_ge(s["x2_done"], b)
                for t in range(NT):
                    tp(bank[1][0:CW, P * t:P * t + P], cnat[:, t, :], ident[:, :])
                    last = tp(bank[6][0:NB * E, P // 2 * t:P // 2 * t + P // 2].bitcast(BF16), c24[:, t, :, :].rearrange("p s e -> p (s e)"), identb[:, :])
                last.then_inc(s["combT_ps"], 1)
                if 1 <= b < B - 1:
                    route(b + 1)
                elif b:
                    query(0)
                pe.wait_ge(s["cT_ready"], b + 1)
                if b == 0:
                    pe.wait_ge(s["VA_ready"], 1)
                for j in range(NJ):
                    if j >= 2:
                        pe.wait_ge(s["silu_done"], (NJ + 1) * (b + 1))
                    mm(bank[GATE_BANKS[j]][:, :], sel[:, 2 * j:2 * j + 2, :].rearrange("p e h -> p (e h)"), cT24[:, :],
                       start=True, stop=True).then_inc(s["gate_ps"], 1)
                if b == 1:
                    pe.wait_ge(s["ld_wexp"], 16)
                    pe.wait_ge(s["kf_ready"], 1)
                    for t in range(NH):
                        last = tp(bank[7][:, P * t:P * t + P], wexp[:, P * t:P * t + P], ident[:, :])
                    last.then_inc(s["wexpT_ps"], 1)
                if b == 0:
                    pe.wait_ge(s["ld_w2"], 64)
                    pe.wait_ge(s["compared"], b + 1)
                    transposed_rows(b + 1)
                pe.wait_ge(s["combT_ready"], b + 1)
                for t in range(NT):
                    if b == 0 and t == 1:
                        route(b + 1)
                    for j in [NJ] + list(range(NJ)):
                        kk = P if j < NJ else HE + E + 1
                        if t % 2 == 0 and j < NJ:
                            pe.wait_ge(s["gated"], NJ * (2 * b + t // 2) + j + 1)
                        last = mm(bank[6][:, P * t:P * t + P], g[0:kk, u, j, P * t:P * t + P], w2[0:kk, j, :],
                                  start=(j == NJ), stop=(j == NJ - 1))
                last.then_inc(s["y_ps"], 1)

            def butterfly(c):
                k, part = divmod(c, 3)
                if part == 0:
                    if k == 0:
                        pe.wait_ge(s["x2_done"], B)
                    else:
                        pe.wait_ge(s["max_done"], NT * NG * (k + 1))
                    pe.wait_ge(s["bf_ready"], 1 + max(3 * k - 1, 0))
                    pe.wait_ge(s["G_ready"], 2 * k + 1)
                if part == 2:
                    pe.wait_ge(s["G_ready"], 2 * k + 2)
                    pe.wait_ge(s["bf_ready"], 1 + 3 * k + 1)
                    if k == 0:
                        pe.wait_ge(s["ld_wcon"], 16)
                up = part < 2
                src, d = (U[:, k % 2, :, :], k) if up else (V[:, k % 2, :, :], 2 - k)
                w, o = D + 2 if up else D, bank[BF_BANK(k, part)]
                for i, t in enumerate((2 * part, 2 * part + 1) if up else range(NH)):
                    for t_ in (range(NH) if d == 2 else (t,)):
                        m = G2[:, 1 - up, t_, t, :] if d == 2 else (G0, G1)[d][:, 1 - up, t, :]
                        last = mm(o[:, w * i:w * i + w], m, src[:, t_, :], start=(t_ == 0 or d < 2), stop=(t_ == NH - 1 or d < 2))
                last.then_inc(s["bf_ps"], 1)

            def score(b, k):
                gq, t = divmod(k, NT)
                u = b % 2
                if k == 0 and b == 0:
                    pe.wait_ge(s["gated"], 2 * NJ * B)
                if k == 0 and b:
                    pe.wait_ge(s["bf_ready"], 1 + 3 * b)
                if t == 0:
                    pe.wait_ge(ld_Q[u][gq], 48 * (b // 2 + 1))
                    pe.wait_ge(s["KS_ready"], B * gq + b + 1)
                k += NT * NG * b
                n_ = 2 if b else 4
                if k >= n_:
                    pe.wait_ge(s["max_done"], k - n_ + 1)
                mm(bank[A_BANK(k)][:, 0:HG * C], QS[0:96, u, gq, P * t:P * t + P],
                   KS[0:96, gq, b, :, :].rearrange("p i c -> p (i c)"), start=True, stop=True).then_inc(s["a_ps"], 1)

            def shifted_score(h):
                b, i = divmod(h, HEADS)
                gq = i // HG
                if i == 0:
                    pe.wait_ge(ld_M[b % 2], 16 * NG * (b // 2 + 1))
                if h == 0:
                    pe.wait_ge(s["KS_ones"], 2)
                    pe.wait_ge(s["x2_done"], B)
                if h >= 2:
                    pe.wait_ge(s["exp_done"], h - 1)
                mm(bank[4 + h % 2][0:C, :], KS[:, gq, b, i % HG, :], QS[:, b % 2, gq, :], start=True, stop=True).then_inc(s["s_ps"], 1)

            def weighted(h):
                b, i = divmod(h, HEADS)
                q, at = h // HG, 32 * (h % HG)
                pe.wait_ge(s["exp_done"], h + 1)
                if q >= 2:
                    pe.wait_ge(s["us_ready"], q - 1)
                mm(bank[6 + q % 2][at:at + 32, :], VA[:, b, i, :], expw[:, h % RING, :], start=True, stop=True).then_inc(s["pv_done"], 1)

            def rows_of_values(b, t):
                pe.wait_ge(s["us_ready"], NG * (b + 1))
                if t >= 2:
                    pe.wait_ge(s["an_ready"], NT * b + t - 1)
                if t == 1 and b:
                    pe.wait_ge(s["x3_done"], b)
                if t == 1 and b + 3 < B:
                    pe.wait_ge(s["qf_ready"], b + 4)
                for gq in range(NG):
                    last = tp(bank[t % 2][:, P * gq:P * gq + P], US[:, b % 2, gq, P * t:P * t + P], ident[:, :])
                last.then_inc(s["ut_ps"], 1)

            def attended(b):
                pe.wait_ge(s["an_ready"], NT * (b + 1))
                if b + 2 < B:
                    pe.wait_ge(s["mT_ready"], b + 3)
                for t in range(NT):
                    last = tp(bank[0][:, P * t:P * t + P], an[:, t, :], ident[:, :])
                last.then_inc(s["anT_ps"], 1)

            def project(b):
                pe.wait_ge(s["aT_ready"], b + 1)
                for t in range(NT):
                    last = mm(bank[1][:, P * t:P * t + P], aT[:, b % 2, P * t:P * t + P], wo[:, :], start=True, stop=True)
                last.then_inc(s["o_ps"], 1)

            def maxima_by_rows(b):
                pe.wait_ge(s["mx_ready"], b + 1)
                if b >= 2:
                    pe.wait_ge(s["an_ready"], NT * (b - 2) + 3)
                for t in range(NT):
                    last = tp(bank[0][:, P * t:P * t + P], mx[:, t, :, :].bitcast(F32).rearrange("p q c -> p (q c)"), ident[:, :])
                last.then_inc(s["mT_ps"], 1)

            def expand(k):
                b, j = divmod(k, NH)
                pe.wait_ge(s["nT_ready"], 2 * B + b + 1)
                pe.wait_ge(s["nl_ready"], b + 1)
                if 2 <= k < NH + 2:
                    pe.wait_ge(s["hid1_kept"], k - 1)
                elif k >= 2:
                    pe.wait_ge(s["gelu_done"], k - 1)
                o, w = bank[2 + k % 2][:, :], slice(P * j, P * j + P)
                mm(o, wuh[:, w], nh[:, b % 2, :], start=True, stop=False)
                mm(o, wul[:, w], nh[:, b % 2, :], start=False, stop=False)
                mm(o, wuh[:, w], nl[:, b % 2, :], start=False, stop=True).then_inc(s["hid1_ps"], 1)

            for b in range(-1, B):
                for i in range(HEADS):
                    if b >= 0:
                        h = HEADS * b + i
                        shifted_score(h)
                    ks = [k for k in range(NT * NG) if A_SLOTS[k] == i and b + 1 < B]
                    for k in ks[:1]:
                        score(b + 1, k)
                    if b >= 0 and h >= 2:
                        weighted(h - 2)
                    for k in ks[1:]:
                        score(b + 1, k)
                    if b + 2 < B and i == T_SLOT(b):
                        if b == -1:
                            pe.wait_ge(s["qf_ready"], 1)
                        transposed_rows(B + b + 2)
                    if b + 2 < B and i == Q_SLOT(b):
                        query(b + 2)
                    if b <= 1 and i in BF_SLOTS(b):
                        butterfly(3 * (b + 1) + BF_SLOTS(b).index(i))
                    if b == 2 and i == MT_SLOT + 1:
                        pe.wait_ge(s["bf_ready"], 1 + 9)
                        for t in range(NH):
                            last = tp(bank[2][:, P * t:P * t + P], U[:, 1, t, 0:D], ident[:, :])
                        last.then_inc(s["wup_ps"], 1)
                    if i == 1 and b >= 2:
                        project(b - 2)
                    if b >= 1:
                        if i in UT_SLOTS:
                            rows_of_values(b - 1, UT_SLOTS.index(i))
                    if i == MT_SLOT and b + 1 < B:
                        maxima_by_rows(b + 1)
                    if b >= 1 and i == 15:
                        attended(b - 1)
                    if b == B - 1:
                        if i == 8:
                            pe.wait_ge(s["wul_ready"], 1)
                            transposed_rows(2 * B)
                        if i in EXP_SLOTS:
                            expand(EXP_SLOTS.index(i))
            weighted(HEADS * B - 2)
            weighted(HEADS * B - 1)

            pe.wait_ge(s["hid1_kept"], NH)
            transposed_rows(2 * B + 1)
            project(B - 2)
            rows_of_values(B - 1, 0)
            expand(NH)
            rows_of_values(B - 1, 1)
            rows_of_values(B - 1, 2)
            rows_of_values(B - 1, 3)
            expand(NH + 1)
            attended(B - 1)
            for b in range(B):
                if 1 <= b < B - 1:
                    for j in range(NH):
                        expand(NH * (b + 1) + j)
                    if b + 2 < B:
                        transposed_rows(2 * B + b + 2)
                for t in range(NT):
                    h, i = divmod(t, NT // 2)
                    if b and i == 0:
                        pe.wait_ge(s["x4_done"], 2 * (b - 1) + h + 1)
                    for j in range(NH):
                        if t == 0:
                            pe.wait_ge(s["gelu_done"], NH * b + j + 1)
                        last = mm(bank[6 + h][:, P * i:P * i + P], g[:, b % 2, j, P * t:P * t + P], V[:, 1, j, :], start=(j == 0), stop=(j == NH - 1))
                    if i == NT // 2 - 1:
                        last.then_inc(s["y1_ps"], 1)
                    if b == 0 and t == 1:
                        project(B - 1)
                        expand(NH + 2)
                        transposed_rows(2 * B + 2)
                        expand(NH + 3)


def kernel(**inputs):
    import numpy as np
    import concourse.bacc as bacc
    from concourse.bass_utils import run_bass_kernel_spmd

    nc = bacc.Bacc("TRN2", target_bir_lowering=False, num_devices=1)
    arrays, aps = {}, {}
    for name, a in inputs.items():
        a = np.ascontiguousarray(a)
        arrays[f"in_{name}"] = a
        aps[name] = nc.dram_tensor(f"in_{name}", a.shape, mybir.dt.from_np(a.dtype), kind="ExternalInput").ap()
    shape = arrays["in_x"].shape
    out = nc.dram_tensor("out_x", shape, F32, kind="ExternalOutput").ap()
    two_layer_block(nc, aps, out)
    r = run_bass_kernel_spmd(nc, [arrays], core_ids=[0])
    return r.results[0]["out_x"]
```
